# Optimizing a Trainium2 kernel written in Bass

```python
import numpy as np
import jax
import jax.numpy as jnp

def _softmax(x, axis=-1):
    return jax.nn.softmax(x, axis=axis)

def _gelu(x):
    return jax.nn.gelu(x, approximate=True)

def _silu(x):
    return jax.nn.silu(x)

def _sigmoid(x):
    return jax.nn.sigmoid(x)

def _layernorm(x, axis=-1, eps=1e-05):
    m = jnp.mean(x, axis=axis, keepdims=True)
    v = jnp.var(x, axis=axis, keepdims=True)
    return (x - m) / jnp.sqrt(v + eps)

def _scatter_add(tgt, idx, src, axis=0):
    return tgt.at[idx].add(src)

def _segment_sum(src, seg, n):
    return jax.ops.segment_sum(src, seg, n)
kernel_name = 'mk_gnn_preln_d4_gnn_r32_fa12d4'

def setup_inputs(seed: int=0):
    np.random.seed(seed)
    _w = jnp.asarray

    def _rec_inputs():
        import jax
        import jax.numpy as jnp
        _gk = jax.random.key(seed)
        x = -0.0003713 + 1 * jax.random.normal(jax.random.fold_in(_gk, 1), (3125, 128), jnp.float32)
        src = jax.random.randint(jax.random.fold_in(_gk, 2), (100000,), 0, 3125, jnp.int32)
        dst = jnp.minimum((3125 * jax.random.uniform(jax.random.fold_in(_gk, 3), (100000,)) ** 2.0).astype(jnp.int32), 99999)
        _o = jnp.argsort(dst, stable=True)
        src = src[_o]
        dst = dst[_o]
        edge_attr_64 = -9.77346e-05 + 0.999888 * jax.random.normal(jax.random.fold_in(_gk, 12), (100000, 64), jnp.float32)
        edge_type_4 = jax.random.randint(jax.random.fold_in(_gk, 14), (100000,), 0, 4, jnp.int32)
        edge_weight = jax.random.uniform(jax.random.fold_in(_gk, 15), (100000,), jnp.float32, 0.0, 0.999999)
        edge_weight1 = jax.random.uniform(jax.random.fold_in(_gk, 16), (100000, 1), jnp.float32, 0.0, 0.999998)
        node_vec1 = jax.random.uniform(jax.random.fold_in(_gk, 17), (3125, 1), jnp.float32, 0.0, 0.999884)
        return (x, src, dst, edge_attr_64, edge_type_4, edge_weight, edge_weight1, node_vec1)
    x, src, dst, edge_attr_64, edge_type_4, edge_weight, edge_weight1, node_vec1 = _rec_inputs()

    def _L0_gnn_setup():
        import jax, jax.numpy as jnp
        import numpy as np
        N_NODES = 3125
        N_EDGES = 100000
        D_FEAT = 128
        THETA = (0.5, 0.3, 0.2, 0.1)
        key = jax.random.key(seed)
        k1, k2, k3 = jax.random.split(key, 3)
        feat = jax.random.normal(k1, (N_NODES, D_FEAT), dtype=jnp.float32)
        src = jax.random.randint(k2, (N_EDGES,), 0, N_NODES, dtype=jnp.int32)
        dst = jax.random.randint(k3, (N_EDGES,), 0, N_NODES, dtype=jnp.int32)
        return {'feat': feat, 'src': src, 'dst': dst}
    _L0_gnn_all = _L0_gnn_setup()
    _L0_gnn_in = {k: v for k, v in _L0_gnn_all.items() if k in ()}
    del _L0_gnn_all

    def _L1_gnn_setup():
        import jax, jax.numpy as jnp
        import numpy as np
        N, E, DIN, H, C = (3125, 50000, 128, 8, 16)
        NEG_SLOPE = 0.2
        key = jax.random.key(seed)
        k1, k2, k3, k4, k5, k6 = jax.random.split(key, 6)
        x = jax.random.normal(k1, (N, DIN), dtype=jnp.float32)
        src = jax.random.randint(k2, (E,), 0, N, dtype=jnp.int64)
        dst = jax.random.randint(k3, (E,), 0, N, dtype=jnp.int64)
        dst = jnp.where(src == dst, (dst + 1) % N, dst)
        edge_index = jnp.stack([src, dst], axis=0)
        W = jax.random.normal(k4, (DIN, H * C), dtype=jnp.float32) * (1.0 / np.sqrt(DIN))
        att_src = jax.random.normal(k5, (H, C), dtype=jnp.float32) * (1.0 / np.sqrt(C))
        att_dst = jax.random.normal(k6, (H, C), dtype=jnp.float32) * (1.0 / np.sqrt(C))
        bias = jnp.zeros((H * C,), dtype=jnp.float32)
        return {'x': x, 'edge_index': edge_index, 'W': W, 'att_src': att_src, 'att_dst': att_dst, 'bias': bias}
    _L1_gnn_all = _L1_gnn_setup()
    _L1_gnn_in = {k: v for k, v in _L1_gnn_all.items() if k in ('W', 'att_src', 'att_dst', 'bias')}
    del _L1_gnn_all

    def _L2_gnn_setup():
        import jax, jax.numpy as jnp
        import numpy as np
        N_TYPES = 4
        NEG_SLOPE = 0.01

        def _conv(x, row, col, edge_type, edge_weight, W, b):
            N = x.shape[0]
            deg = jax.ops.segment_sum(jnp.ones(col.shape[0], dtype=x.dtype), col, num_segments=N)
            deg_inv_sqrt = jnp.where(deg > 0, deg ** (-0.5), jnp.zeros((), x.dtype))
            norm = deg_inv_sqrt[row] * deg_inv_sqrt[col] * edge_weight
            xw = jnp.einsum('ni,tio->tno', x, W)
            x_j = xw[edge_type, col] * norm[:, None]
            out = jax.ops.segment_sum(x_j, row, num_segments=N) + b
            return jax.nn.leaky_relu(out, negative_slope=NEG_SLOPE)
        key = jax.random.key(seed)
        ks = jax.random.split(key, 10)
        N, d, E = (50000, 128, 625000)
        x = jax.random.normal(ks[0], (N, d), dtype=jnp.float32)
        edge_index = jax.random.randint(ks[1], (2, E), 0, N, dtype=jnp.int64 if jax.config.jax_enable_x64 else jnp.int32)
        edge_type = jax.random.randint(ks[2], (E,), 0, N_TYPES)
        edge_attr = jax.random.uniform(ks[3], (E,), dtype=jnp.float32)
        bound = float(np.sqrt(6.0 / (d + d)))
        W1 = jax.random.uniform(ks[4], (N_TYPES, d, d), minval=-bound, maxval=bound, dtype=jnp.float32)
        W2 = jax.random.uniform(ks[5], (N_TYPES, d, d), minval=-bound, maxval=bound, dtype=jnp.float32)
        W3 = jax.random.uniform(ks[6], (N_TYPES, d, d), minval=-bound, maxval=bound, dtype=jnp.float32)
        b1 = jnp.zeros((d,), jnp.float32)
        b2 = jnp.zeros((d,), jnp.float32)
        b3 = jnp.zeros((d,), jnp.float32)
        return {'x': x, 'edge_index': edge_index, 'edge_type': edge_type, 'edge_attr': edge_attr, 'W1': W1, 'b1': b1, 'W2': W2, 'b2': b2, 'W3': W3, 'b3': b3}
    _L2_gnn_all = _L2_gnn_setup()
    _L2_gnn_in = {k: v for k, v in _L2_gnn_all.items() if k in ('W1', 'b1', 'W2', 'b2', 'W3', 'b3')}
    del _L2_gnn_all

    def _L3_gnn_setup():
        import jax, jax.numpy as jnp
        import numpy as np
        N_NODES, N_EDGES = (50000, 25000)
        NODE_DIM, EDGE_DIM, HIDDEN, HEADS = (128, 64, 128, 8)
        HEAD_DIM = HIDDEN // HEADS
        key = jax.random.key(seed)
        ks = jax.random.split(key, 24)

        def lin(k, fan_in, fan_out):
            lim = 1.0 / np.sqrt(fan_in)
            kw, kb = jax.random.split(k)
            W = jax.random.uniform(kw, (fan_in, fan_out), jnp.float32, -lim, lim)
            b = jax.random.uniform(kb, (fan_out,), jnp.float32, -lim, lim)
            return (W, b)
        inp = {}
        inp['nodes'] = jax.random.normal(ks[0], (N_NODES, NODE_DIM), jnp.float32)
        inp['edges'] = jax.random.normal(ks[1], (N_EDGES, EDGE_DIM), jnp.float32)
        inp['edge_index'] = jax.random.randint(ks[2], (2, N_EDGES), 0, N_NODES, jnp.int32)
        inp['conservation_scores'] = jax.random.uniform(ks[3], (N_NODES, 1), jnp.float32)
        inp['distances'] = jax.random.uniform(ks[4], (N_EDGES, 1), jnp.float32)
        inp['Wq'], inp['bq'] = lin(ks[5], NODE_DIM, HIDDEN)
        inp['Wk'], inp['bk'] = lin(ks[6], NODE_DIM, HIDDEN)
        inp['Wv'], inp['bv'] = lin(ks[7], NODE_DIM, HIDDEN)
        inp['We'], inp['be'] = lin(ks[8], EDGE_DIM, HEADS)
        inp['Wc1'], inp['bc1'] = lin(ks[9], 1, 32)
        inp['Wc2'], inp['bc2'] = lin(ks[10], 32, HEADS)
        inp['Wd1'], inp['bd1'] = lin(ks[11], 1, 16)
        inp['Wd2'], inp['bd2'] = lin(ks[12], 16, HEADS)
        inp['Wo'], inp['bo'] = lin(ks[13], HIDDEN, NODE_DIM)
        inp['gamma'] = jnp.ones((NODE_DIM,), jnp.float32)
        inp['beta'] = jnp.zeros((NODE_DIM,), jnp.float32)
        return inp
    _L3_gnn_all = _L3_gnn_setup()
    _L3_gnn_in = {k: v for k, v in _L3_gnn_all.items() if k in ('Wq', 'bq', 'Wk', 'bk', 'Wv', 'bv', 'We', 'be', 'Wc1', 'bc1', 'Wc2', 'bc2', 'Wd1', 'bd1', 'Wd2', 'bd2', 'Wo', 'bo', 'gamma', 'beta')}
    del _L3_gnn_all
    return {'x': x, 'src': src, 'dst': dst, 'edge_attr_64': edge_attr_64, 'edge_type_4': edge_type_4, 'edge_weight': edge_weight, 'edge_weight1': edge_weight1, 'node_vec1': node_vec1, 'L1_gnn_W': _L1_gnn_in['W'], 'L1_gnn_att_src': _L1_gnn_in['att_src'], 'L1_gnn_att_dst': _L1_gnn_in['att_dst'], 'L1_gnn_bias': _L1_gnn_in['bias'], 'L2_gnn_W1': _L2_gnn_in['W1'], 'L2_gnn_b1': _L2_gnn_in['b1'], 'L2_gnn_W2': _L2_gnn_in['W2'], 'L2_gnn_b2': _L2_gnn_in['b2'], 'L2_gnn_W3': _L2_gnn_in['W3'], 'L2_gnn_b3': _L2_gnn_in['b3'], 'L3_gnn_Wq': _L3_gnn_in['Wq'], 'L3_gnn_bq': _L3_gnn_in['bq'], 'L3_gnn_Wk': _L3_gnn_in['Wk'], 'L3_gnn_bk': _L3_gnn_in['bk'], 'L3_gnn_Wv': _L3_gnn_in['Wv'], 'L3_gnn_bv': _L3_gnn_in['bv'], 'L3_gnn_We': _L3_gnn_in['We'], 'L3_gnn_be': _L3_gnn_in['be'], 'L3_gnn_Wc1': _L3_gnn_in['Wc1'], 'L3_gnn_bc1': _L3_gnn_in['bc1'], 'L3_gnn_Wc2': _L3_gnn_in['Wc2'], 'L3_gnn_bc2': _L3_gnn_in['bc2'], 'L3_gnn_Wd1': _L3_gnn_in['Wd1'], 'L3_gnn_bd1': _L3_gnn_in['bd1'], 'L3_gnn_Wd2': _L3_gnn_in['Wd2'], 'L3_gnn_bd2': _L3_gnn_in['bd2'], 'L3_gnn_Wo': _L3_gnn_in['Wo'], 'L3_gnn_bo': _L3_gnn_in['bo'], 'L3_gnn_gamma': _L3_gnn_in['gamma'], 'L3_gnn_beta': _L3_gnn_in['beta']}

def reference(x, src, dst, edge_attr_64, edge_type_4, edge_weight, edge_weight1, node_vec1, L1_gnn_W, L1_gnn_att_src, L1_gnn_att_dst, L1_gnn_bias, L2_gnn_W1, L2_gnn_b1, L2_gnn_W2, L2_gnn_b2, L2_gnn_W3, L2_gnn_b3, L3_gnn_Wq, L3_gnn_bq, L3_gnn_Wk, L3_gnn_bk, L3_gnn_Wv, L3_gnn_bv, L3_gnn_We, L3_gnn_be, L3_gnn_Wc1, L3_gnn_bc1, L3_gnn_Wc2, L3_gnn_bc2, L3_gnn_Wd1, L3_gnn_bd1, L3_gnn_Wd2, L3_gnn_bd2, L3_gnn_Wo, L3_gnn_bo, L3_gnn_gamma, L3_gnn_beta):
    import jax
    import jax.numpy as jnp

    def _L0_gnn_ref(feat, src, dst):
        import jax, jax.numpy as jnp
        import numpy as np
        N_NODES = 3125
        N_EDGES = 100000
        D_FEAT = 128
        THETA = (0.5, 0.3, 0.2, 0.1)
        deg = jax.ops.segment_sum(jnp.ones_like(dst, dtype=feat.dtype), dst, num_segments=N_NODES)
        d_invsqrt = jnp.power(jnp.clip(deg, 1.0, None), -0.5)[:, None]
        h = THETA[0] * feat
        for k in range(1, len(THETA)):
            scaled = feat * d_invsqrt
            agg = jax.ops.segment_sum(scaled[src], dst, num_segments=N_NODES)
            feat = feat - agg * d_invsqrt
            h = h + THETA[k] * feat
        return h

    def _L1_gnn_ref(x, edge_index, W, att_src, att_dst, bias):
        import jax, jax.numpy as jnp
        import numpy as np
        N, E, DIN, H, C = (3125, 50000, 128, 8, 16)
        NEG_SLOPE = 0.2
        n = x.shape[0]
        h = (x @ W).reshape(n, H, C)
        a_src = jnp.einsum('nhc,hc->nh', h, att_src)
        a_dst = jnp.einsum('nhc,hc->nh', h, att_dst)
        loop = jnp.arange(n, dtype=edge_index.dtype)
        src = jnp.concatenate([edge_index[0], loop])
        dst = jnp.concatenate([edge_index[1], loop])
        e = jax.nn.leaky_relu(a_src[src] + a_dst[dst], NEG_SLOPE)
        m = jax.ops.segment_max(e, dst, num_segments=n)
        m = jnp.where(jnp.isfinite(m), m, 0.0)
        ex = jnp.exp(e - m[dst])
        denom = jax.ops.segment_sum(ex, dst, num_segments=n)
        alpha = ex / denom[dst]
        msg = h[src] * alpha[:, :, None]
        out = jax.ops.segment_sum(msg, dst, num_segments=n)
        return out.reshape(n, H * C) + bias

    def _L2_gnn_ref(x, edge_index, edge_type, edge_attr, W1, b1, W2, b2, W3, b3):
        import jax, jax.numpy as jnp
        import numpy as np
        N_TYPES = 4
        NEG_SLOPE = 0.01

        def _conv(x, row, col, edge_type, edge_weight, W, b):
            N = x.shape[0]
            deg = jax.ops.segment_sum(jnp.ones(col.shape[0], dtype=x.dtype), col, num_segments=N)
            deg_inv_sqrt = jnp.where(deg > 0, deg ** (-0.5), jnp.zeros((), x.dtype))
            norm = deg_inv_sqrt[row] * deg_inv_sqrt[col] * edge_weight
            xw = jnp.einsum('ni,tio->tno', x, W)
            x_j = xw[edge_type, col] * norm[:, None]
            out = jax.ops.segment_sum(x_j, row, num_segments=N) + b
            return jax.nn.leaky_relu(out, negative_slope=NEG_SLOPE)
        row, col = (edge_index[0], edge_index[1])
        z1 = _conv(x, row, col, edge_type, edge_attr, W1, b1)
        z2 = _conv(z1, row, col, edge_type, edge_attr, W2, b2)
        z3 = _conv(z2, row, col, edge_type, edge_attr, W3, b3)
        return (x + z1 + z2 + z3) / 4

    def _L3_gnn_ref(nodes, edges, edge_index, conservation_scores, distances, Wq, bq, Wk, bk, Wv, bv, We, be, Wc1, bc1, Wc2, bc2, Wd1, bd1, Wd2, bd2, Wo, bo, gamma, beta):
        import jax, jax.numpy as jnp
        import numpy as np
        N_NODES, N_EDGES = (50000, 25000)
        NODE_DIM, EDGE_DIM, HIDDEN, HEADS = (128, 64, 128, 8)
        HEAD_DIM = HIDDEN // HEADS
        N = nodes.shape[0]
        src, tgt = (edge_index[0], edge_index[1])
        q = (nodes @ Wq + bq).reshape(N, HEADS, HEAD_DIM)
        k = (nodes @ Wk + bk).reshape(N, HEADS, HEAD_DIM)
        v = (nodes @ Wv + bv).reshape(N, HEADS, HEAD_DIM)
        scores = jnp.einsum('ehd,ehd->eh', q[src], k[tgt]) / np.sqrt(HEAD_DIM)
        scores = scores + edges @ We + be
        cons = jax.nn.sigmoid(jax.nn.relu(conservation_scores @ Wc1 + bc1) @ Wc2 + bc2)
        scores = scores * cons[tgt]
        scores = scores + jax.nn.relu(distances @ Wd1 + bd1) @ Wd2 + bd2
        seg_max = jax.ops.segment_max(scores, tgt, num_segments=N)
        w = jnp.exp(scores - seg_max[tgt])
        seg_sum = jax.ops.segment_sum(w, tgt, num_segments=N)
        weights = w / seg_sum[tgt]
        attended = weights[..., None] * v[tgt]
        agg = jax.ops.segment_sum(attended, tgt, num_segments=N).reshape(N, HIDDEN)
        out = agg @ Wo + bo
        x = nodes + out
        mu = jnp.mean(x, axis=-1, keepdims=True)
        var = jnp.var(x, axis=-1, keepdims=True)
        return (x - mu) / jnp.sqrt(var + 1e-05) * gamma + beta
    edge_index = jnp.stack([src, dst])
    h = jnp.maximum(_layernorm(x, axis=-1), 0.0)
    x = x + _L0_gnn_ref(h, src, dst)
    h = jnp.maximum(_layernorm(x, axis=-1), 0.0)
    x = x + _L1_gnn_ref(h, edge_index, L1_gnn_W, L1_gnn_att_src, L1_gnn_att_dst, L1_gnn_bias)
    h = jnp.maximum(_layernorm(x, axis=-1), 0.0)
    x = x + _L2_gnn_ref(h, edge_index, edge_type_4, edge_weight, L2_gnn_W1, L2_gnn_b1, L2_gnn_W2, L2_gnn_b2, L2_gnn_W3, L2_gnn_b3)
    h = jnp.maximum(_layernorm(x, axis=-1), 0.0)
    x = x + _L3_gnn_ref(h, edge_attr_64, edge_index, node_vec1, edge_weight1, L3_gnn_Wq, L3_gnn_bq, L3_gnn_Wk, L3_gnn_bk, L3_gnn_Wv, L3_gnn_bv, L3_gnn_We, L3_gnn_be, L3_gnn_Wc1, L3_gnn_bc1, L3_gnn_Wc2, L3_gnn_bc2, L3_gnn_Wd1, L3_gnn_bd1, L3_gnn_Wd2, L3_gnn_bd2, L3_gnn_Wo, L3_gnn_bo, L3_gnn_gamma, L3_gnn_beta)
    return x

_drawn_inputs = setup_inputs


def setup_inputs(seed=0):
    import zlib

    import numpy as np

    out = dict(_drawn_inputs(seed))
    spreads = {'L1_gnn_bias': (0.0, 0.1),
     'L2_gnn_b1': (0.0, 0.8),
     'L2_gnn_b2': (0.0, 2.0),
     'L2_gnn_b3': (0.0, 2.0),
     'L3_gnn_gamma': (1.0, 0.6),
     'L3_gnn_beta': (0.0, 2.0)}
    factors = {'edge_attr_64': 200.0,
     'edge_weight': 8.0,
     'edge_weight1': 200.0,
     'node_vec1': 64.0,
     'L2_gnn_W1': 4.536,
     'L2_gnn_W2': 8.0,
     'L2_gnn_W3': 8.0,
     'L3_gnn_Wq': 64.0,
     'L3_gnn_bq': 64.0,
     'L3_gnn_Wk': 64.0,
     'L3_gnn_bk': 64.0,
     'L3_gnn_bv': 200.0,
     'L3_gnn_We': 200.0,
     'L3_gnn_be': 64.0,
     'L3_gnn_Wc1': 200.0,
     'L3_gnn_bc1': 64.0,
     'L3_gnn_Wc2': 200.0,
     'L3_gnn_bc2': 64.0,
     'L3_gnn_Wd1': 200.0,
     'L3_gnn_bd1': 200.0,
     'L3_gnn_Wd2': 200.0,
     'L3_gnn_bd2': 64.0,
     'L1_gnn_att_dst': 61.442,
     'L3_gnn_Wv': 56.929,
     'L3_gnn_Wo': 44.642,
     'L3_gnn_bo': 64.0}
    for name, (base, spread) in spreads.items():
        noise = np.random.default_rng([zlib.crc32(name.encode()), seed]).standard_normal(out[name].shape)
        drawn = base * np.exp(spread * noise) if base else spread * noise
        out[name] = jnp.asarray(drawn.astype(out[name].dtype))
    for name, factor in factors.items():
        out[name] = (out[name] * factor).astype(out[name].dtype)
    return out
```

```python
import concourse.bass as bass
import numpy as np
from concourse import mybir
from contextlib import ExitStack

F32 = mybir.dt.float32
I32 = mybir.dt.int32
ALU = mybir.AluOpType
ACT = mybir.ActivationFunctionType
AXX = mybir.AxisListType.X

P = 128
N = 3125
D = 128
W = -(-N // P)
NP = W * P
E = 100000
SB = 8
EP = max(p for p in range(1, P + 1) if E % (p * 2 * SB) == 0)
EC = E // EP
HEADS = 8
C = D // HEADS
CH = 16
TILES_MIN = -(-E // P) + W
G = 4
TG = -(-TILES_MIN // CH)
while (TG * CH) % (2 * G) or TG % 3:
    TG += 1
T = TG * CH
SLOTS = T * P
L = TG * P
RD = 18
RS = 4
TYPES = 4
BIG = 1e38
EPS = 1e-5
THETA = (0.5, 0.3, 0.2, 0.1)


class Chain:

    def __init__(self, engine, sem):
        self.engine, self.sem, self.n = engine, sem, 0

    def __call__(self, instruction):
        instruction.then_inc(self.sem, 1)
        self.n += 1
        self.engine.wait_ge(self.sem, self.n)


class Core:

    def __init__(self, nc):
        self.nc, self.held = nc, []

    def sb(self, ctx, name, shape, dt=F32):
        return ctx.enter_context(self.nc.sbuf_tensor(name, shape, dt))

    def sem(self, name):
        handle = self.nc.alloc_semaphore(name=name)
        self.held[-1].append(handle)
        return handle

    def pool_dma_sems(self, name):
        return [self.nc.alloc_semaphore(name=f"{name}{h}") for h in range(2)]


def own_semaphores(stage):
    def run(k, *args, **kwargs):
        k.held.append([])
        stage(k, *args, **kwargs)
        mine = k.held.pop()
        with k.nc.Block() as block:
            @block.gpsimd
            def _(pool):
                for handle in mine:
                    pool.sem_clear(handle)
        for handle in mine:
            k.nc.release_semaphore(handle)
    return run


def bc(ap, shape):
    return ap.to_broadcast(shape)


def rows_in(ap):
    return ap.rearrange("(w p) c -> p w c", p=P)


def by_edge(ap):
    return ap.rearrange("(p e) -> p e", e=EC)


@own_semaphores
def setup(k, io):
    nc = k.nc
    s_load, s_io, s_v = k.sem("x_loaded"), k.sem("iotas_made"), k.sem("setup_steps")
    s_id, s_ones = k.sem("identity_made"), k.sem("ones_made")
    with nc.Block() as block:
        @block.sync
        def _(sp):
            full = N // P
            sp.wait_ge(s_v, 1)
            sp.dma_start(k.x[:, 0:full, :], rows_in(io["x"][0:full * P, :])).then_inc(s_load, 16)
            sp.dma_start(k.x[0:N - full * P, full, :], io["x"][full * P:N, :]).then_inc(s_load, 16)
            sp.wait_ge(s_load, 32)

        @block.gpsimd
        def _(pool):
            pool.iota(k.iota[:, :], [[1, P]], base=0, channel_multiplier=0,
                      allow_small_or_imprecise_dtypes=True).then_inc(s_io, 1)
            pool.iota(k.tile_no[:, :], [[1, T]], base=0, channel_multiplier=0,
                      allow_small_or_imprecise_dtypes=True).then_inc(s_io, 1)
            pool.iota(k.pid[:, :], [[1, 1]], base=0, channel_multiplier=1,
                      allow_small_or_imprecise_dtypes=True).then_inc(s_io, 1)

        @block.vector
        def _(v):
            v.memset(k.x[:, :, :], 0.0).then_inc(s_v, 1)
            v.memset(k.ones[:, :], 1.0).then_inc(s_ones, 1)
            v.memset(k.eps[:, :], EPS).then_inc(s_ones, 1)
            v.wait_ge(s_io, 3)
            v.tensor_scalar(k.ident[:, :], k.iota[:, :], k.pid[:, 0:1], None, ALU.is_equal).then_inc(s_id, 1)
            v.tensor_scalar(k.before[:, :], k.iota[:, :], k.pid[:, 0:1], None, ALU.is_gt).then_inc(s_id, 1)
            v.wait_ge(s_id, 2)
            v.wait_ge(s_ones, 2)


@own_semaphores
def layernorm(k, tag, src, dst, relu=True, gamma=None, beta=None):
    nc = k.nc
    with ExitStack() as ctx:
        stat = k.sb(ctx, f"{tag}_stat", [P, 4, W])
        sq = k.sb(ctx, f"{tag}_sq", [P, W, D])
        s_v, s_var, s_std = k.sem(f"{tag}_v"), k.sem(f"{tag}_var"), k.sem(f"{tag}_std")
        wide = [P, W, D]
        with nc.Block() as block:
            @block.vector
            def _(v):
                step = Chain(v, s_v)
                step(v.tensor_reduce(stat[:, 0, :], src[:, :, :], AXX, ALU.add))
                step(v.tensor_scalar(stat[:, 1, :], stat[:, 0, :], 1.0 / D, None, ALU.mult))
                step(v.tensor_tensor(dst[:, :, :], src[:, :, :],
                                     bc(stat[:, 1, :].unsqueeze(2), wide), ALU.subtract))
                step(v.tensor_tensor(sq[:, :, :], dst[:, :, :], dst[:, :, :], ALU.mult))
                v.tensor_reduce(stat[:, 2, :], sq[:, :, :], AXX, ALU.add).then_inc(s_var, 1)
                v.wait_ge(s_std, 1)
                step(v.reciprocal(stat[:, 0, :], stat[:, 3, :]))
                step(v.tensor_tensor(dst[:, :, :], dst[:, :, :],
                                     bc(stat[:, 0, :].unsqueeze(2), wide), ALU.mult))
                if relu:
                    step(v.tensor_scalar(dst[:, :, :], dst[:, :, :], 0.0, None, ALU.max))
                if gamma is not None:
                    step(v.tensor_tensor(dst[:, :, :], dst[:, :, :],
                                         bc(gamma[:, :].unsqueeze(1), wide), ALU.mult))
                    step(v.tensor_tensor(dst[:, :, :], dst[:, :, :],
                                         bc(beta[:, :].unsqueeze(1), wide), ALU.add))

            @block.scalar
            def _(act):
                act.wait_ge(s_var, 1)
                act.activation(stat[:, 3, :], stat[:, 2, :], ACT.Sqrt, bias=k.eps[:, 0:1],
                               scale=1.0 / D).then_inc(s_std, 1)


@own_semaphores
def edge_terms(k, io, rec):
    nc = k.nc
    A = 64
    H1 = 16
    pairs = SB // 2
    with ExitStack() as ctx:
        attr = k.sb(ctx, "attr", [EP, 2, SB, A])
        attr_t = k.sb(ctx, "attr_t", [P, 2, pairs, EP])
        we2 = k.sb(ctx, "we_twice", [P, 2, HEADS])
        be = k.sb(ctx, "be_all", [P, HEADS])
        wd1 = k.sb(ctx, "wd1_all", [P, H1])
        bd1 = k.sb(ctx, "bd1_all", [P, H1])
        wd2 = k.sb(ctx, "wd2_all", [P, H1 * HEADS])
        bd2 = k.sb(ctx, "bd2_all", [P, HEADS])
        dist = k.sb(ctx, "dist", [EP, EC])
        hid = k.sb(ctx, "dist_hidden", [EP, 2, EC])
        dterm = k.sb(ctx, "dist_term", [EP, HEADS, EC])
        s_we0, s_w = k.sem("we_cleared"), k.sem("edge_weights_loaded")
        two = lambda name: [k.sem(f"{name}0"), k.sem(f"{name}1")]
        s_at, s_tr, s_cp, s_mm, s_ev = map(two, ("attr_loaded", "attr_transposed", "attr_t_copied",
                                                 "attr_terms_done", "attr_terms_kept"))
        s_h, s_ac = k.sem("hidden_ready"), k.sem("dist_steps")
        loads = 8
        with nc.Block() as block:
            @block.vector
            def _(v):
                v.memset(we2[:, :, :], 0.0).then_inc(s_we0, 1)
                v.wait_ge(s_w, 16 * loads)
                with v.Fori(0, EC // SB // 2) as i:
                    for half in range(2):
                        v.wait_ge(s_tr[half], i + 1)
                        v.nop(nofuse=True)
                        v.tensor_copy(attr_t[:, half, :, :],
                                      k.ps[2 * half][:, 0:pairs * EP].rearrange("p (a b) -> p a b", b=EP))\
                            .then_inc(s_cp[half], 1)
                        v.wait_ge(s_mm[half], i + 1)
                        v.nop(nofuse=True)
                        v.tensor_tensor(rec[:, bass.ds((i * 2 + half) * SB, SB), 2:10],
                                        k.ps[2 * half + 1][0:EP, 0:SB * HEADS].rearrange("p (e h) -> p e h", h=HEADS),
                                        bc(be[0:EP, :].unsqueeze(1), [EP, SB, HEADS]), ALU.add)\
                            .then_inc(s_ev[half], 1)
                for h in range(HEADS):
                    v.tensor_copy(dterm[:, h, :], bc(bd2[0:EP, h:h + 1], [EP, EC])).then_inc(s_ac, 1)
                done = HEADS
                for j in range(H1):
                    v.wait_ge(s_h, j + 1)
                    for h in range(HEADS):
                        v.wait_ge(s_ac, done - HEADS + 1)
                        v.scalar_tensor_tensor(dterm[:, h, :], hid[:, j % 2, :],
                                               wd2[0:EP, j * HEADS + h:j * HEADS + h + 1],
                                               dterm[:, h, :], ALU.mult, ALU.add).then_inc(s_ac, 1)
                        done += 1
                v.wait_ge(s_ac, done)
                v.tensor_copy(rec[:, :, 10:18], dterm[:, :, :].rearrange("p h e -> p e h")).then_inc(s_ac, 1)

            @block.scalar
            def _(act):
                act.wait_ge(s_w, 16 * loads)
                for j in range(H1):
                    if j >= 2:
                        act.wait_ge(s_ac, HEADS * j)
                    act.activation(hid[:, j % 2, :], dist[:, :], ACT.Relu, bias=bd1[0:EP, j:j + 1],
                                   scale=wd1[0:EP, j:j + 1]).then_inc(s_h, 1)

            @block.tensor
            def _(pe):
                pe.wait_ge(s_w, 16 * loads)
                with pe.Fori(0, EC // SB // 2) as i:
                    for half in range(2):
                        pe.wait_ge(s_at[half], i * 16 + 16)
                        pe.wait_ge(s_ev[half], i)
                        pe.nop(nofuse=True)
                        for a in range(pairs):
                            ins = pe.transpose(k.ps[2 * half][:, a * EP:(a + 1) * EP],
                                               attr[:, half, 2 * a:2 * a + 2, :].rearrange("p a b -> p (a b)"),
                                               k.ident[0:EP, 0:EP])
                        ins.then_inc(s_tr[half], 1)
                    for half in range(2):
                        pe.wait_ge(s_cp[half], i + 1)
                        pe.nop(nofuse=True)
                        for a in range(pairs):
                            ins = pe.matmul(k.ps[2 * half + 1][0:EP, a * 16:(a + 1) * 16],
                                            attr_t[:, half, a, :],
                                            we2[:, :, :].rearrange("p a b -> p (a b)"), start=True, stop=True)
                        ins.then_inc(s_mm[half], 1)

            @block.sync
            def _(sp):
                sp.wait_ge(s_we0, 1)
                sp.dma_start(we2[0:A, 0, :], io["L3_gnn_We"]).then_inc(s_w, 16)
                sp.dma_start(we2[A:2 * A, 1, :], io["L3_gnn_We"]).then_inc(s_w, 16)
                for dst, name in ((be, "L3_gnn_be"), (bd1, "L3_gnn_bd1"), (bd2, "L3_gnn_bd2")):
                    sp.dma_start(dst[:, :], io[name].partition_broadcast(P)).then_inc(s_w, 16)
                sp.dma_start(wd1[:, :], io["L3_gnn_Wd1"].rearrange("a b -> (a b)").partition_broadcast(P))\
                    .then_inc(s_w, 16)
                sp.dma_start(wd2[:, :], io["L3_gnn_Wd2"].rearrange("a b -> (a b)").partition_broadcast(P))\
                    .then_inc(s_w, 16)
                sp.dma_start(dist[:, :], by_edge(io["edge_weight1"].rearrange("e a -> (e a)"))).then_inc(s_w, 16)
                a_v = io["edge_attr_64"].rearrange("(p e) a -> p e a", e=EC)
                with sp.Fori(0, EC // SB // 2) as i:
                    for half in range(2):
                        sp.wait_ge(s_tr[half], i)
                        sp.nop(nofuse=True)
                        sp.dma_start(attr[:, half, :, :], a_v[:, bass.ds((i * 2 + half) * SB, SB), :])\
                            .then_inc(s_at[half], 16)


@own_semaphores
def places(k, tag, key, buckets, pos, whole_tiles, win=None):
    nc = k.nc
    with ExitStack() as ctx:
        hit = k.sb(ctx, f"{tag}_hit", [EP, EC])
        rank = k.sb(ctx, f"{tag}_rank", [EP, EC])
        one = k.sb(ctx, f"{tag}_one", [EP, EC])
        posf = k.sb(ctx, f"{tag}_posf", [EP, EC])
        count = k.sb(ctx, f"{tag}_count", [EP, buckets])
        total = k.sb(ctx, f"{tag}_total", [P, buckets])
        tiles = k.sb(ctx, f"{tag}_tiles", [P, buckets], I32)
        size = k.sb(ctx, f"{tag}_size", [P, buckets])
        start = k.sb(ctx, f"{tag}_start", [P, buckets])
        base = k.sb(ctx, f"{tag}_base", [P, buckets])
        s_v, s_one, s_count, s_sum = (k.sem(f"{tag}_v"), k.sem(f"{tag}_one_set"),
                                      k.sem(f"{tag}_counted"), k.sem(f"{tag}_summed"))
        s_hit, s_rank, s_pick = k.sem(f"{tag}_hits"), k.sem(f"{tag}_ranks"), k.sem(f"{tag}_picks")
        with nc.Block() as block:
            @block.vector
            def _(v):
                step = Chain(v, s_v)
                v.memset(one[:, :], 1.0).then_inc(s_one, 1)
                v.memset(posf[:, :], 0.0).then_inc(s_one, 1)
                with v.Fori(0, buckets) as b:
                    v.wait_ge(s_count, b)
                    v.tensor_scalar(hit[:, :], key, k.iota[0:EP, bass.ds(b, 1)], None, ALU.is_equal,
                                    ALU.add, accum_out=count[:, bass.ds(b, 1)]).then_inc(s_count, 1)
                v.wait_ge(s_sum, 1)
                step(v.tensor_copy(total[:, :], k.ps[0][:, 0:buckets]))
                if whole_tiles:
                    step(v.tensor_scalar(tiles[:, :], total[:, :], float(P - 1), None, ALU.add))
                    step(v.tensor_scalar(tiles[:, :], tiles[:, :], 7, None, ALU.arith_shift_right))
                    step(v.tensor_copy(size[:, :], tiles[:, :]))
                else:
                    step(v.tensor_copy(size[:, :], total[:, :]))
                v.wait_ge(s_one, 2)
                step(v.tensor_tensor_scan(start[:, :], k.ones[:, 0:buckets], size[:, :], 0.0,
                                          ALU.mult, ALU.add))
                step(v.tensor_tensor(start[:, :], start[:, :], size[:, :], ALU.subtract))
                step(v.tensor_scalar(base[:, :], start[:, :], float(P if whole_tiles else 1), -1.0,
                                     ALU.mult, ALU.add))
                step(v.tensor_tensor(base[:, :], base[:, :], k.ps[1][:, 0:buckets], ALU.add))
                with v.Fori(0, buckets) as b:
                    v.wait_ge(s_pick, b)
                    v.tensor_scalar(hit[:, :], key, k.iota[0:EP, bass.ds(b, 1)], None, ALU.is_equal)\
                        .then_inc(s_hit, 1)
                    v.wait_ge(s_hit, b + 1)
                    v.tensor_copy(count[:, 0:1], base[0:EP, bass.ds(b, 1)]).then_inc(s_rank, 1)
                    v.wait_ge(s_rank, b * 2 + 1)
                    v.tensor_tensor_scan(rank[:, :], one[:, :], hit[:, :], count[:, 0:1],
                                         ALU.mult, ALU.add).then_inc(s_rank, 1)
                    v.wait_ge(s_rank, b * 2 + 2)
                    v.nop(nofuse=True)
                    v.copy_predicated(posf[:, :], hit[:, :].bitcast(I32), rank[:, :]).then_inc(s_pick, 1)
                v.wait_ge(s_pick, buckets)
                step(v.tensor_copy(pos, posf[:, :]))
                if win is not None:
                    step(v.memset(win[:, :], -1.0))
                    for b in range(buckets):
                        step(v.scalar_tensor_tensor(win[:, :], k.tile_no[:, :], start[:, b:b + 1],
                                                    win[:, :], ALU.is_ge, ALU.add))

            @block.tensor
            def _(pe):
                pe.wait_ge(s_count, buckets)
                pe.matmul(k.ps[0][:, 0:buckets], k.ones[0:EP, :], count[:, :], start=True, stop=True)
                pe.matmul(k.ps[1][:, 0:buckets], k.before[0:EP, :], count[:, :], start=True, stop=True)\
                    .then_inc(s_sum, 1)


@own_semaphores
def scatter(k, tag, rec, width, pos, table):
    nc = k.nc
    with ExitStack() as ctx:
        st_rec = k.sb(ctx, f"{tag}_st_rec", [EP, 2, SB, width])
        st_pos = k.sb(ctx, f"{tag}_st_pos", [EP, 2, SB], I32)
        s_rec = [k.sem(f"{tag}_rec_staged{h}") for h in range(2)]
        s_pos = [k.sem(f"{tag}_pos_staged{h}") for h in range(2)]
        s_out = k.pool_dma_sems(f"{tag}_scattered")
        steps = EC // SB // 2
        with nc.Block() as block:
            @block.scalar
            def _(act):
                with act.Fori(0, steps) as i:
                    for h in range(2):
                        act.wait_ge(s_out[h], i * (16 * SB))
                        act.nop(nofuse=True)
                        act.copy(st_rec[:, h, :, :], rec[:, bass.ds((i * 2 + h) * SB, SB), :])\
                            .then_inc(s_rec[h], 1)

            @block.gpsimd
            def _(pool):
                with pool.Fori(0, steps) as i:
                    for h in range(2):
                        pool.wait_ge(s_out[h], i * (16 * SB))
                        pool.nop(nofuse=True)
                        pool.tensor_copy(st_pos[:, h, :], pos[:, bass.ds((i * 2 + h) * SB, SB)])\
                            .then_inc(s_pos[h], 1)
                        pool.wait_ge(s_pos[h], i + 1)
                        pool.wait_ge(s_rec[h], i + 1)
                        pool.nop(nofuse=True)
                        for e in range(SB):
                            pool.indirect_dma_start(
                                table, bass.IndirectOffsetOnAxis(ap=st_pos[:, h, e:e + 1], axis=0),
                                st_rec[:, h, e, :], None).then_inc(s_out[h], 16)
                for h in range(2):
                    pool.wait_ge(s_out[h], steps * 16 * SB)


@own_semaphores
def fill_pads(k, tag, table, width, dst_column):
    nc = k.nc
    with ExitStack() as ctx:
        pad = k.sb(ctx, f"{tag}_pad", [P, TG, width])
        s_p, s_out = k.sem(f"{tag}_pad_made"), k.sem(f"{tag}_pads_out")
        with nc.Block() as block:
            @block.vector
            def _(v):
                v.memset(pad[:, :, :], 0.0).then_inc(s_p, 1)
                v.wait_ge(s_p, 1)
                v.memset(pad[:, :, dst_column:dst_column + 1], -1.0).then_inc(s_p, 1)

            @block.sync
            def _(sp):
                sp.wait_ge(s_p, 2)
                view = table.rearrange("(c p e) r -> c p e r", c=CH, e=TG)
                for c in range(CH):
                    sp.dma_start(view[c], pad[:, :, :]).then_inc(s_out, 16)
                sp.wait_ge(s_out, 16 * CH)


@own_semaphores
def keys(k, tag, node, low, high):
    nc = k.nc
    with ExitStack() as ctx:
        tmp = k.sb(ctx, f"{tag}_tmp", [EP, EC], I32)
        s_v = k.sem(f"{tag}_v")
        with nc.Block() as block:
            @block.vector
            def _(v):
                step = Chain(v, s_v)
                step(v.tensor_scalar(tmp[:, :], node, P - 1, None, ALU.bitwise_and))
                if low is not None:
                    step(v.tensor_copy(low, tmp[:, :]))
                step(v.tensor_scalar(tmp[:, :], node, 7, None, ALU.arith_shift_right))
                if high is not None:
                    step(v.tensor_copy(high, tmp[:, :]))


@own_semaphores
def sort_by_dst(k, io):
    nc = k.nc
    with ExitStack() as ctx:
        rec = k.sb(ctx, "rec_dst", [EP, EC, RD])
        s_ld, s_cv = k.sem("src_dst_loaded"), k.sem("src_dst_in_records")
        edge_terms(k, io, rec)
        pos = k.sb(ctx, "pos_dst", [EP, EC], I32)
        key = k.sb(ctx, "key_dst", [EP, EC])
        node = k.sb(ctx, "node_dst", [EP, 2, EC], I32)
        with nc.Block() as block:
            @block.sync
            def _(sp):
                sp.dma_start(node[:, 0, :], by_edge(io["src"])).then_inc(s_ld, 16)
                sp.dma_start(node[:, 1, :], by_edge(io["dst"])).then_inc(s_ld, 16)

            @block.vector
            def _(v):
                v.wait_ge(s_ld, 32)
                v.tensor_copy(rec[:, :, 0], node[:, 0, :]).then_inc(s_cv, 1)
                v.tensor_copy(rec[:, :, 1], node[:, 1, :]).then_inc(s_cv, 1)
                v.wait_ge(s_cv, 2)
        keys(k, "keys_a", node[:, 1, :], key[:, :], None)
        places(k, "sort_a", key[:, :], P, pos[:, :], False)
        scatter(k, "move_a", rec, RD, pos, k.list_a)
        s_back, s_int = k.sem("half_sorted_back"), k.sem("half_sorted_dst")
        with nc.Block() as block:
            @block.sync
            def _(sp):
                sp.dma_start(rec[:, :, :], k.list_a.rearrange("(p e) r -> p e r", e=EC)).then_inc(s_back, 16)

            @block.vector
            def _(v):
                v.wait_ge(s_back, 16)
                v.tensor_copy(node[:, 1, :], rec[:, :, 1]).then_inc(s_int, 1)
                v.wait_ge(s_int, 1)
        keys(k, "keys_b", node[:, 1, :], None, key[:, :])
        places(k, "sort_b", key[:, :], W, pos[:, :], True, k.win_dst)
        scatter(k, "move_b", rec, RD, pos, k.list_dst)


@own_semaphores
def sort_by_src(k, io):
    nc = k.nc
    with ExitStack() as ctx:
        rec = k.sb(ctx, "rec_src", [EP, EC, RS])
        pos = k.sb(ctx, "pos_src", [EP, EC], I32)
        key = k.sb(ctx, "key_src", [EP, EC])
        node = k.sb(ctx, "node_src", [EP, 3, EC], I32)
        wgt = k.sb(ctx, "weight_src", [EP, EC])
        s_ld, s_cv = k.sem("typed_edges_loaded"), k.sem("typed_edges_in_records")
        with nc.Block() as block:
            @block.sync
            def _(sp):
                for n, name in enumerate(("src", "dst", "edge_type_4")):
                    sp.dma_start(node[:, n, :], by_edge(io[name])).then_inc(s_ld, 16)
                sp.dma_start(wgt[:, :], by_edge(io["edge_weight"])).then_inc(s_ld, 16)

            @block.vector
            def _(v):
                step = Chain(v, s_cv)
                v.wait_ge(s_ld, 64)
                step(v.memset(rec[:, :, :], 0.0))
                step(v.tensor_copy(key[:, :], node[:, 2, :]))
                step(v.tensor_copy(rec[:, :, 3], node[:, 1, :]))
                step(v.scalar_tensor_tensor(rec[:, :, 0], rec[:, :, 3], float(TYPES), key[:, :],
                                            ALU.mult, ALU.add))
                step(v.tensor_copy(rec[:, :, 1], node[:, 0, :]))
                step(v.tensor_copy(rec[:, :, 2], wgt[:, :]))
        keys(k, "keys_c", node[:, 0, :], None, key[:, :])
        places(k, "sort_c", key[:, :], W, pos[:, :], True, k.win_src)
        scatter(k, "move_c", rec, RS, pos, k.list_src)


@own_semaphores
def read_list(k, tag, table, width, index, loc, extra, win, win_i):
    nc = k.nc
    with ExitStack() as ctx:
        buf = k.sb(ctx, f"{tag}_buf", [P, T, 4])
        s_ld, s_v = k.sem(f"{tag}_loaded"), k.sem(f"{tag}_v")
        with nc.Block() as block:
            @block.sync
            def _(sp):
                sp.dma_start(buf[:, :, :], table.rearrange("(t p) r -> p t r", p=P)[:, :, 0:4]).then_inc(s_ld, 16)

            @block.vector
            def _(v):
                step = Chain(v, s_v)
                v.wait_ge(s_ld, 16)
                step(v.tensor_copy(index[:, :], buf[:, :, 0]))
                step(v.scalar_tensor_tensor(loc[:, 0:T], win[:, :], -float(P), buf[:, :, 1],
                                            ALU.mult, ALU.add))
                step(v.memset(loc[:, T:T + G], -1.0))
                if extra is not None:
                    step(v.tensor_copy(extra[:, 0:T], buf[:, :, 2]))
                    step(v.memset(extra[:, T:T + G], 0.0))
                step(v.tensor_copy(win_i[:, :], win[0:1, :]))
@own_semaphores
def window_sums(k, tag, acc, loc, win_i, cols, table=None, index=None, weight=None, values=None,
                stream=None, shares=None):
    nc = k.nc
    steps = T // (2 * G)
    with ExitStack() as ctx:
        hot = k.sb(ctx, f"{tag}_hot", [P, 2, G, P])
        two = lambda name: [k.sem(f"{tag}_{name}{h}") for h in range(2)]
        s_hot, s_mm, s_idx, s_row, s_msg = map(two, ("hot", "summed", "index_staged", "rows", "messages"))
        if table is not None:
            s_row = k.pool_dma_sems(f"{tag}_gathered")
        s_z, s_add = k.sem(f"{tag}_cleared"), k.sem(f"{tag}_added")
        rows = msg = st = None
        if table is not None:
            rows = k.sb(ctx, f"{tag}_rows", [P, 2, G, cols])
            st = k.sb(ctx, f"{tag}_st", [P, 2, G], I32)
        if stream is not None:
            rows = k.sb(ctx, f"{tag}_rows", [P, 2, G, D])
            msg = k.sb(ctx, f"{tag}_msg", [P, 2, G, cols])
        with nc.Block() as block:
            if table is not None:
                @block.gpsimd
                def _(pool):
                    with pool.Fori(0, steps) as i:
                        for h in range(2):
                            pool.wait_ge(s_mm[h], i)
                            pool.nop(nofuse=True)
                            pool.tensor_copy(st[:, h, :], index[:, bass.ds((i * 2 + h) * G, G)])\
                                .then_inc(s_idx[h], 1)
                            pool.wait_ge(s_idx[h], i + 1)
                            pool.nop(nofuse=True)
                            for g in range(G):
                                pool.indirect_dma_start(
                                    rows[:, h, g, :], None, table,
                                    bass.IndirectOffsetOnAxis(ap=st[:, h, g:g + 1], axis=0)).then_inc(s_row[h], 16)
            if stream is not None:
                @block.sync
                def _(sp):
                    with sp.Fori(0, steps) as i:
                        for h in range(2):
                            sp.wait_ge(s_msg[h], i)
                            sp.nop(nofuse=True)
                            sp.dma_start(rows[:, h, :, :],
                                         stream[bass.ds(i * 2 + h, 1), :, :, :].rearrange("a p g c -> (a p) g c"))\
                                .then_inc(s_row[h], 16)

            @block.vector
            def _(v):
                def one_hots(i, h):
                    for g in range(G):
                        at = (i * 2 + h) * G + g
                        if weight is not None:
                            v.tensor_scalar(hot[:, h, g, :], k.iota[:, :], loc[:, bass.ds(at, 1)],
                                            weight[:, bass.ds(at, 1)], ALU.is_equal, ALU.mult).then_inc(s_hot[h], 1)
                        else:
                            v.tensor_scalar(hot[:, h, g, :], k.iota[:, :], loc[:, bass.ds(at, 1)], None,
                                            ALU.is_equal).then_inc(s_hot[h], 1)

                def messages(i, h):
                    if stream is None:
                        return
                    v.wait_ge(s_row[h], i * 16 + 16)
                    v.wait_ge(s_mm[h], i)
                    v.nop(nofuse=True)
                    at = bass.ds((i * 2 + h) * G, G)
                    n = shares[0].shape[2]
                    for j, share in enumerate(shares):
                        v.tensor_copy(msg[:, h, :, D + j * n:D + (j + 1) * n], share[:, at, :]).then_inc(s_add_msg, 1)
                    v.tensor_tensor(msg[:, h, :, 0:D].rearrange("p g (a c) -> p g a c", c=C),
                                    rows[:, h, :, :].rearrange("p g (a c) -> p g a c", c=C),
                                    bc(shares[0][:, at, :].unsqueeze(3), [P, G, HEADS, C]), ALU.mult)\
                        .then_inc(s_msg[h], 1)

                def adds(i, h):
                    to = [v.value_load(win_i[0:1, bass.ds((i * 2 + h) * G + g, 1)], min_val=0,
                                       max_val=W - 1) for g in range(G)]
                    v.wait_ge(s_mm[h], i + 1)
                    for g in range(G):
                        v.wait_ge(s_add, (i * 2 + h) * G + g)
                        part = acc[:, bass.ds(to[g] * cols, cols)]
                        v.tensor_tensor(part, part, k.ps[h * G + g][:, 0:cols], ALU.add).then_inc(s_add, 1)

                s_add_msg = k.sem(f"{tag}_shares_copied") if stream is not None else None
                v.memset(acc[:, :], 0.0).then_inc(s_z, 1)
                v.wait_ge(s_z, 1)
                one_hots(0, 0)
                with v.Fori(0, steps) as i:
                    messages(i, 0)
                    one_hots(i, 1)
                    adds(i, 0)
                    messages(i, 1)
                    one_hots(i + 1, 0)
                    adds(i, 1)

            @block.tensor
            def _(pe):
                with pe.Fori(0, steps) as i:
                    for h in range(2):
                        pe.wait_ge(s_hot[h], (i + 1) * G)
                        if table is not None:
                            pe.wait_ge(s_row[h], (i + 1) * (16 * G))
                        if stream is not None:
                            pe.wait_ge(s_msg[h], i + 1)
                        pe.wait_ge(s_add, (i * 2 + h) * G)
                        pe.nop(nofuse=True)
                        for g in range(G):
                            rhs = (msg if msg is not None else rows)[:, h, g, :] if rows is not None else \
                                values[:, bass.ds((i * 2 + h) * G + g, 1), :].rearrange("p a c -> p (a c)")
                            ins = pe.matmul(k.ps[h * G + g][:, 0:cols], hot[:, h, g, :], rhs,
                                            start=True, stop=True)
                        ins.then_inc(s_mm[h], 1)


@own_semaphores
def project(k, tag, src, weights, cols, keep):
    nc = k.nc
    U = 5
    with ExitStack() as ctx:
        st = k.sb(ctx, f"{tag}_st", [P, U, D])
        st_t = k.sb(ctx, f"{tag}_st_t", [P, U, P])
        s_st, s_tr, s_cp, s_mm, s_kept = (k.sem(f"{tag}_staged"), k.sem(f"{tag}_transposed"),
                                          k.sem(f"{tag}_copied"), k.sem(f"{tag}_product"), k.sem(f"{tag}_kept"))
        with nc.Block() as block:
            @block.scalar
            def _(act):
                with act.Fori(0, W // U) as i:
                    act.wait_ge(s_tr, i)
                    act.nop(nofuse=True)
                    act.copy(st[:, :, :], src[:, bass.ds(i * U, U), :]).then_inc(s_st, 1)

            @block.vector
            def _(v):
                with v.Fori(0, W // U) as i:
                    v.wait_ge(s_tr, i + 1)
                    v.wait_ge(s_mm, i)
                    v.nop(nofuse=True)
                    v.tensor_copy(st_t[:, 0:4, :], k.ps[0][:, :].rearrange("p (a b) -> p a b", b=P)).then_inc(s_cp, 1)
                    v.tensor_copy(st_t[:, 4, :], k.ps[1][:, 0:P]).then_inc(s_cp, 1)
                    v.wait_ge(s_mm, i + 1)
                    v.nop(nofuse=True)
                    for u in range(U):
                        keep(v, i * U + u, k.ps[2 + u][:, 0:cols]).then_inc(s_kept, 1)

            @block.tensor
            def _(pe):
                with pe.Fori(0, W // U) as i:
                    pe.wait_ge(s_st, i + 1)
                    pe.wait_ge(s_cp, i * 2)
                    pe.nop(nofuse=True)
                    for u in range(U):
                        ins = pe.transpose(k.ps[u // 4][:, (u % 4) * P:(u % 4 + 1) * P], st[:, u, :], k.ident[:, :])
                    ins.then_inc(s_tr, 1)
                    pe.wait_ge(s_cp, i * 2 + 2)
                    pe.wait_ge(s_kept, i * U)
                    pe.nop(nofuse=True)
                    for u in range(U):
                        ins = pe.matmul(k.ps[2 + u][:, 0:cols], st_t[:, u, :], weights, start=True, stop=True)
                    ins.then_inc(s_mm, 1)


@own_semaphores
def vector_steps(k, tag, steps, loads=(), stores=()):
    nc = k.nc
    s_ld, s_v, s_st = k.sem(f"{tag}_loads"), k.sem(f"{tag}_v"), k.sem(f"{tag}_stores")
    done = {}
    with nc.Block() as block:
        @block.vector
        def _(v):
            step = Chain(v, s_v)
            if loads:
                v.wait_ge(s_ld, 16 * len(loads))
            steps(v, step)
            done["n"] = step.n

        @block.sync
        def _(sp):
            for dst, src in loads:
                sp.dma_start(dst, src).then_inc(s_ld, 16)
            if stores:
                sp.wait_ge(s_v, done["n"])
            for dst, src in stores:
                sp.dma_start(dst, src).then_inc(s_st, 16)
            if stores:
                sp.wait_ge(s_st, 16 * len(stores))


@own_semaphores
def edge_rows(k, tag, table_src, cols_src, table_dst, cols_dst, consume, keep_rows=None):
    nc = k.nc
    steps = T // (2 * G)
    with ExitStack() as ctx:
        a = k.sb(ctx, f"{tag}_by_src", [P, 2, G, cols_src])
        b = k.sb(ctx, f"{tag}_by_dst", [P, 2, G, cols_dst])
        st = k.sb(ctx, f"{tag}_st", [P, 2, 2, G], I32)
        two = lambda name: [k.sem(f"{tag}_{name}{h}") for h in range(2)]
        s_st, s_done, s_kept = map(two, ("staged", "consumed", "kept"))
        s_row = k.pool_dma_sems(f"{tag}_gathered")
        scratch = {}
        with nc.Block() as block:
            @block.gpsimd
            def _(pool):
                with pool.Fori(0, steps) as i:
                    for h in range(2):
                        at = bass.ds((i * 2 + h) * G, G)
                        pool.wait_ge(s_done[h], i)
                        if keep_rows is not None:
                            pool.wait_ge(s_kept[h], i * 16)
                        pool.nop(nofuse=True)
                        pool.tensor_copy(st[:, h, 0, :], k.src_i[:, at]).then_inc(s_st[h], 1)
                        pool.tensor_copy(st[:, h, 1, :], k.dst_i[:, at]).then_inc(s_st[h], 1)
                        pool.wait_ge(s_st[h], i * 2 + 2)
                        pool.nop(nofuse=True)
                        for g in range(G):
                            pool.indirect_dma_start(
                                a[:, h, g, :], None, table_src,
                                bass.IndirectOffsetOnAxis(ap=st[:, h, 0, g:g + 1], axis=0)).then_inc(s_row[h], 16)
                            pool.indirect_dma_start(
                                b[:, h, g, :], None, table_dst,
                                bass.IndirectOffsetOnAxis(ap=st[:, h, 1, g:g + 1], axis=0)).then_inc(s_row[h], 16)

            @block.vector
            def _(v):
                with v.Fori(0, steps) as i:
                    for h in range(2):
                        v.wait_ge(s_row[h], (i + 1) * (32 * G))
                        v.nop(nofuse=True)
                        consume(v, (i * 2 + h), a[:, h, :, :], b[:, h, :, :]).then_inc(s_done[h], 1)

            if keep_rows is not None:
                @block.sync
                def _(sp):
                    with sp.Fori(0, steps) as i:
                        for h in range(2):
                            sp.wait_ge(s_row[h], (i + 1) * (32 * G))
                            sp.nop(nofuse=True)
                            sp.dma_start(keep_rows[bass.ds(i * 2 + h, 1), :, :, :].rearrange("a p g c -> (a p) g c"),
                                         a[:, h, :, 0:D]).then_inc(s_kept[h], 16)
                    for h in range(2):
                        sp.wait_ge(s_kept[h], 16 * steps)


@own_semaphores
def across(k, tag, src, dst, forward, broadcast=False):
    nc = k.nc
    U = 3
    with ExitStack() as ctx:
        st = k.sb(ctx, f"{tag}_st", [P, U, P])
        s_st, s_tr, s_cp = k.sem(f"{tag}_staged"), k.sem(f"{tag}_transposed"), k.sem(f"{tag}_copied")

        def slots_side(buf, i):
            if broadcast:
                ap = buf.rearrange("p (c g) -> p c g", g=TG)[:, :, bass.ds(i * U, U)]
                return bc(ap.rearrange("p c g -> p g c").unsqueeze(3), [P, U, CH, HEADS])
            ap = buf.rearrange("p (c g) h -> p c g h", g=TG)[:, :, bass.ds(i * U, U), :]
            return ap.rearrange("p c g h -> p g c h")

        with nc.Block() as block:
            @block.scalar
            def _(act):
                with act.Fori(0, TG // U) as i:
                    act.wait_ge(s_tr, i)
                    act.nop(nofuse=True)
                    if forward:
                        act.copy(st[:, :, :].rearrange("p g (c h) -> p g c h", h=HEADS),
                                 slots_side(src, i)).then_inc(s_st, 1)
                    else:
                        act.copy(st[:, :, :].rearrange("p g e -> p (g e)"),
                                 src[:, bass.ds(i * (U * P), U * P)]).then_inc(s_st, 1)

            @block.tensor
            def _(pe):
                with pe.Fori(0, TG // U) as i:
                    pe.wait_ge(s_st, i + 1)
                    pe.wait_ge(s_cp, i)
                    pe.nop(nofuse=True)
                    for u in range(U):
                        ins = pe.transpose(k.ps[0][:, u * P:(u + 1) * P], st[:, u, :], k.ident[:, :])
                    ins.then_inc(s_tr, 1)

            @block.vector
            def _(v):
                with v.Fori(0, TG // U) as i:
                    v.wait_ge(s_tr, i + 1)
                    v.nop(nofuse=True)
                    if forward:
                        v.tensor_copy(dst[:, bass.ds(i * (U * P), U * P)], k.ps[0][:, 0:U * P]).then_inc(s_cp, 1)
                    else:
                        v.tensor_copy(slots_side(dst, i),
                                      k.ps[0][:, 0:U * P].rearrange("p (g c h) -> p g c h", g=U, h=HEADS))\
                            .then_inc(s_cp, 1)


@own_semaphores
def segment_max(k, tag, val):
    nc = k.nc
    with ExitStack() as ctx:
        vt = k.sb(ctx, f"{tag}_vt", [P, L])
        out = k.sb(ctx, f"{tag}_out", [P, L])
        wall = k.sb(ctx, f"{tag}_wall", [P, L + 1])
        ends = k.sb(ctx, f"{tag}_ends", [P, 2])
        rows = k.sb(ctx, f"{tag}_rows", [1, 7, HEADS, CH])
        carry = k.sb(ctx, f"{tag}_carry", [P, 2])
        across(k, f"{tag}_dst", k.dst_f, out[:, :], True, broadcast=True)
        across(k, f"{tag}_val", val, vt[:, :], True)
        s_v, s_v2, s_pe = k.sem(f"{tag}_v"), k.sem(f"{tag}_v2"), k.sem(f"{tag}_pe")
        FIRST, LAST, VAL, WALL, IN, SCAN, BACK = range(7)

        with nc.Block() as block:
            @block.vector
            def _(v):
                step = Chain(v, s_v)
                step(v.tensor_copy(ends[:, 0:1], out[:, 0:1]))
                step(v.tensor_copy(ends[:, 1:2], out[:, L - 1:L]))
                step(v.tensor_tensor(wall[:, 1:L], out[:, 1:L], out[:, 0:L - 1], ALU.not_equal))
                step(v.memset(wall[:, 0:1], 0.0))
                step(v.memset(wall[:, L:L + 1], 0.0))
                step(v.tensor_scalar(wall[:, 1:L], wall[:, 1:L], -BIG, None, ALU.mult))
                step(v.tensor_tensor_scan(out[:, :], wall[:, 0:L], vt[:, :], -BIG, ALU.add, ALU.max))
                v.nop(nofuse=True).then_inc(s_v2, 1)

                def chunks(row):
                    return rows[0:1, row, :, :]

                def border(a, b, at):
                    here, there = (slice(1, CH), slice(0, CH - 1))
                    if a == FIRST:
                        here, there = there, here
                    step(v.memset(chunks(at), -BIG))
                    step(v.tensor_tensor(rows[0:1, at, :, here], rows[0:1, b, :, here],
                                         rows[0:1, a, :, there], ALU.not_equal))
                    step(v.tensor_scalar(rows[0:1, at, :, here], rows[0:1, at, :, here], -BIG, None, ALU.mult))
                    return here, there

                def carried(n, a, b, order):
                    v.wait_ge(s_pe, 1 + 2 * n)
                    if n == 0:
                        for q, row in enumerate((FIRST, LAST)):
                            step(v.tensor_copy(chunks(row), k.ps[1][0:1, q * P:(q + 1) * P]
                                               .rearrange("p (c h) -> p h c", h=HEADS)))
                    step(v.tensor_copy(chunks(VAL), k.ps[2][0:1, n * P:(n + 1) * P]
                                       .rearrange("p (c h) -> p h c", h=HEADS)))
                    border(a, a, WALL)
                    flat = lambda row: rows[0:1, row, :, :].rearrange("p h c -> p (h c)")[:, ::order]
                    step(v.tensor_tensor_scan(flat(SCAN), flat(WALL), flat(VAL), -BIG, ALU.add, ALU.max))
                    here, there = border(a, b, IN)
                    step(v.tensor_tensor(rows[0:1, IN, :, here], rows[0:1, IN, :, here],
                                         rows[0:1, SCAN, :, there], ALU.add))
                    step(v.tensor_copy(rows[0:1, BACK, :, :].rearrange("p h c -> p (h c)")
                                       .rearrange("p (c h) -> p c h", h=HEADS),
                                       rows[0:1, IN, :, :].rearrange("p h c -> p c h")))
                    v.nop(nofuse=True).then_inc(s_v2, 1)
                    v.wait_ge(s_pe, 2 + 2 * n)
                    step(v.tensor_scalar(carry[:, n:n + 1], k.ps[3][:, n:n + 1], -BIG, None, ALU.max))

                carried(0, LAST, FIRST, 1)
                step(v.tensor_tensor_scan(out[:, :], wall[:, 0:L], vt[:, :], carry[:, 0:1], ALU.add, ALU.max))
                step(v.tensor_tensor_scan(vt[:, ::-1], wall[:, L:0:-1], out[:, ::-1], -BIG, ALU.add, ALU.max))
                v.nop(nofuse=True).then_inc(s_v2, 1)
                carried(1, FIRST, LAST, -1)
                step(v.tensor_tensor_scan(vt[:, ::-1], wall[:, L:0:-1], out[:, ::-1], carry[:, 1:2],
                                          ALU.add, ALU.max))

            @block.tensor
            def _(pe):
                for n, last in ((0, out[:, L - 1:L]), (1, vt[:, 0:1])):
                    pe.wait_ge(s_v2, 1 + 2 * n)
                    if n == 0:
                        for q in range(2):
                            pe.matmul(k.ps[1][0:1, q * P:(q + 1) * P], ends[:, q:q + 1], k.ident[:, :],
                                      start=True, stop=True)
                    pe.matmul(k.ps[2][0:1, n * P:(n + 1) * P], last, k.ident[:, :], start=True, stop=True)\
                        .then_inc(s_pe, 1)
                    pe.wait_ge(s_v2, 2 + 2 * n)
                    pe.matmul(k.ps[3][:, n:n + 1], rows[0:1, BACK, :, :].rearrange("p h c -> p (h c)"),
                              k.ones[0:1, 0:1], start=True, stop=True).then_inc(s_pe, 1)
        across(k, f"{tag}_back", vt[:, :], val, False)


@own_semaphores
def layer_filter(k, io):
    nc = k.nc
    with ExitStack() as ctx:
        h = k.sb(ctx, "l0_h", [P, W, D])
        layernorm(k, "ln0", k.x, h)
        scaled = k.sb(ctx, "l0_scaled", [P, W, D])
        acc = k.sb(ctx, "l0_acc", [P, W * D])
        tmp = k.sb(ctx, "l0_degree_tmp", [P, 4, W])
        table = nc.dram_tensor("l0_table", [NP, D], F32).ap()
        wide = [P, W, D]
        window_sums(k, "degree", k.deg[:, :], k.loc, k.win_i, 1, values=k.ones_slots)
        s_c, s_s = k.sem("l0_clipped"), k.sem("l0_root")
        s_n = k.sem("l0_deg_steps")
        with nc.Block() as block:
            @block.vector
            def _(v):
                v.tensor_scalar(tmp[:, 0, :], k.deg[:, :], 1.0, None, ALU.max).then_inc(s_c, 1)
                v.wait_ge(s_s, 1)
                step = Chain(v, s_n)
                step(v.reciprocal(k.dinv[:, :], tmp[:, 1, :]))
                step(v.tensor_scalar(k.no_edge[:, :], k.deg[:, :], 0.0, None, ALU.is_equal))
                step(v.tensor_scalar(tmp[:, 2, :], k.deg[:, :], 0.0, None, ALU.is_gt))
                step(v.tensor_tensor(k.dinv0[:, :], k.dinv[:, :], tmp[:, 2, :], ALU.mult))
                step(v.reciprocal(k.inv_deg[:, :], tmp[:, 0, :]))

            @block.scalar
            def _(act):
                act.wait_ge(s_c, 1)
                act.activation(tmp[:, 1, :], tmp[:, 0, :], ACT.Sqrt).then_inc(s_s, 1)
        dinv = bc(k.dinv[:, :].unsqueeze(2), wide)

        def first(v, step):
            step(v.scalar_tensor_tensor(k.x[:, :, :], h[:, :, :], THETA[0], k.x[:, :, :], ALU.mult, ALU.add))
            step(v.tensor_tensor(scaled[:, :, :], h[:, :, :], dinv, ALU.mult))
        vector_steps(k, "l0_first", first, stores=[(rows_in(table), scaled[:, :, :])])
        for r in range(1, len(THETA)):
            window_sums(k, f"l0_sum{r}", acc[:, :], k.loc, k.win_i, D, table=table, index=k.src_i)
            acc_v = acc[:, :].rearrange("p (w d) -> p w d", d=D)

            def update(v, step):
                step(v.tensor_tensor(scaled[:, :, :], acc_v, dinv, ALU.mult))
                step(v.tensor_tensor(h[:, :, :], h[:, :, :], scaled[:, :, :], ALU.subtract))
                step(v.scalar_tensor_tensor(k.x[:, :, :], h[:, :, :], THETA[r], k.x[:, :, :], ALU.mult, ALU.add))
                if r + 1 < len(THETA):
                    step(v.tensor_tensor(scaled[:, :, :], h[:, :, :], dinv, ALU.mult))
            vector_steps(k, f"l0_update{r}", update,
                         stores=[(rows_in(table), scaled[:, :, :])] if r + 1 < len(THETA) else ())


@own_semaphores
def layer_gat(k, io):
    nc = k.nc
    wide = [P, W, D]
    SLOPE = 0.2
    AD = 2 * HEADS + 1
    t_src = nc.dram_tensor("l1_by_src", [NP, D + HEADS], F32).ap()
    t_dst = nc.dram_tensor("l1_by_dst", [NP, AD], F32).ap()
    t_h = nc.dram_tensor("l1_h", [NP, D], F32).ap()
    kept = nc.dram_tensor("l1_rows", [T // G, P, G, D], F32).ap()
    with ExitStack() as ctx:
        h = k.sb(ctx, "l1_ln", [P, W, D])
        layernorm(k, "ln1", k.x, h)
        by_src = k.sb(ctx, "l1_src_rows", [P, W, D + HEADS])
        by_dst = k.sb(ctx, "l1_dst_rows", [P, W, AD])
        w = k.sb(ctx, "l1_w", [P, D])
        att = k.sb(ctx, "l1_att", [P, 2, D])
        tmp = k.sb(ctx, "l1_tmp", [P, W, D])
        loads = [(w[:, :], io["L1_gnn_W"]),
                 (att[:, 0, :], io["L1_gnn_att_src"].rearrange("h c -> (h c)").partition_broadcast(P)),
                 (att[:, 1, :], io["L1_gnn_att_dst"].rearrange("h c -> (h c)").partition_broadcast(P))]
        vector_steps(k, "l1_load", lambda v, step: None, loads=loads)
        project(k, "l1_h", h, w[:, :], D, lambda v, n, ps: v.tensor_copy(
            by_src[:, bass.ds(n, 1), 0:D].rearrange("p a d -> p (a d)"), ps))
        heads = lambda ap: ap.rearrange("p w (h c) -> p w h c", c=C)

        def scores(v, step):
            for q, dst in ((0, by_src[:, :, D:D + HEADS]), (1, by_dst[:, :, 0:HEADS])):
                step(v.tensor_tensor(tmp[:, :, :], by_src[:, :, 0:D], bc(att[:, q, :].unsqueeze(1), wide), ALU.mult))
                step(v.tensor_reduce(dst, heads(tmp[:, :, :]), AXX, ALU.add))
            own = by_dst[:, :, HEADS:2 * HEADS]
            step(v.tensor_tensor(own, by_src[:, :, D:D + HEADS], by_dst[:, :, 0:HEADS], ALU.add))
            step(v.scalar_tensor_tensor(own, own, SLOPE, own, ALU.mult, ALU.max))
            step(v.tensor_copy(by_dst[:, :, 2 * HEADS], k.inv_deg[:, :]))
        vector_steps(k, "l1_scores", scores, stores=[(rows_in(t_src), by_src[:, :, :]),
                                                     (rows_in(t_dst), by_dst[:, :, :])])
    with ExitStack() as ctx:
        e = k.sb(ctx, "l1_e", [P, T, HEADS])
        own = k.sb(ctx, "l1_own", [P, T, HEADS + 1])
        top = k.sb(ctx, "l1_top", [P, T, HEADS])
        s_c = k.sem("l1_own_copied")

        def consume(v, n, a, b):
            at = bass.ds(n * G, G)
            v.tensor_copy(own[:, at, :], b[:, :, HEADS:AD]).then_inc(s_c, 1)
            return v.tensor_tensor(e[:, at, :], a[:, :, D:D + HEADS], b[:, :, 0:HEADS], ALU.add)
        edge_rows(k, "l1_edges", t_src, D + HEADS, t_dst, AD, consume, keep_rows=kept)

        def leaky(v, step):
            step(v.scalar_tensor_tensor(e[:, :, :], e[:, :, :], SLOPE, e[:, :, :], ALU.mult, ALU.max))
            step(v.tensor_tensor(top[:, :, :], e[:, :, :], own[:, :, 0:HEADS], ALU.max))
        vector_steps(k, "l1_leaky", leaky)
        segment_max(k, "l1_max", top[:, :, :])
        s_a, s_b, s_c2 = k.sem("l1_less_top"), k.sem("l1_exp"), k.sem("l1_own_shared")
        with nc.Block() as block:
            @block.vector
            def _(v):
                v.tensor_tensor(e[:, :, :], e[:, :, :], top[:, :, :], ALU.subtract).then_inc(s_a, 1)
                v.tensor_tensor(own[:, :, 0:HEADS], own[:, :, 0:HEADS], top[:, :, :], ALU.subtract).then_inc(s_a, 1)
                v.wait_ge(s_b, 2)
                v.tensor_tensor(top[:, :, :], own[:, :, 0:HEADS], bc(own[:, :, HEADS:HEADS + 1], [P, T, HEADS]),
                                ALU.mult).then_inc(s_c2, 1)

            @block.scalar
            def _(act):
                act.wait_ge(s_a, 1)
                act.activation(e[:, :, :], e[:, :, :], ACT.Exp).then_inc(s_b, 1)
                act.wait_ge(s_a, 2)
                act.activation(own[:, :, 0:HEADS], own[:, :, 0:HEADS], ACT.Exp).then_inc(s_b, 1)
        acc = k.sb(ctx, "l1_acc", [P, W * (D + 2 * HEADS)])
        window_sums(k, "l1_sum", acc[:, :], k.loc, k.win_i, D + 2 * HEADS, stream=kept,
                    shares=(e[:, :, :], top[:, :, :]))
        acc_v = acc[:, :].rearrange("p (w d) -> p w d", d=D + 2 * HEADS)
        h2 = k.sb(ctx, "l1_h_back", [P, W, D])
        bias = k.sb(ctx, "l1_bias", [P, D])

        def finish(v, step):
            msg, den, loop = acc_v[:, :, 0:D], acc_v[:, :, D:D + HEADS], acc_v[:, :, D + HEADS:]
            per_head = lambda ap: bc(ap.unsqueeze(3), [P, W, HEADS, C])
            step(v.tensor_tensor(loop, loop, bc(k.no_edge[:, :].unsqueeze(2), [P, W, HEADS]), ALU.add))
            step(v.tensor_tensor(den, den, loop, ALU.add))
            step(v.reciprocal(den, den))
            step(v.tensor_tensor(heads(h2[:, :, :]), heads(h2[:, :, :]), per_head(loop), ALU.mult))
            step(v.tensor_tensor(h2[:, :, :], h2[:, :, :], msg, ALU.add))
            step(v.tensor_tensor(heads(h2[:, :, :]), heads(h2[:, :, :]), per_head(den), ALU.mult))
            step(v.tensor_tensor(h2[:, :, :], h2[:, :, :], bc(bias[:, :].unsqueeze(1), wide), ALU.add))
            step(v.tensor_tensor(k.x[:, :, :], k.x[:, :, :], h2[:, :, :], ALU.add))
        vector_steps(k, "l1_finish", finish, loads=[(h2[:, :, :], rows_in(t_src)[:, :, 0:D]),
                                                    (bias[:, :], io["L1_gnn_bias"].partition_broadcast(P))])


@own_semaphores
def layer_relational(k, io):
    nc = k.nc
    wide = [P, W, D]
    SLOPE = 0.01
    table = nc.dram_tensor("l2_table", [NP, TYPES * D], F32).ap()
    with ExitStack() as ctx:
        index = k.sb(ctx, "l2_index", [P, T], I32)
        loc = k.sb(ctx, "l2_loc", [P, T + G])
        wgt = k.sb(ctx, "l2_weight", [P, T + G])
        win_i = k.sb(ctx, "l2_win_i", [1, T], I32)
        read_list(k, "read_src", k.list_src, RS, index, loc, wgt, k.win_src, win_i)
        z = k.sb(ctx, "l2_z", [P, W, D])
        total = k.sb(ctx, "l2_total", [P, W, D])
        acc = k.sb(ctx, "l2_acc", [P, W * D])
        rows = k.sb(ctx, "l2_rows", [P, W, TYPES * D])
        w = k.sb(ctx, "l2_w", [P, TYPES, D])
        bias = k.sb(ctx, "l2_bias", [P, D])
        layernorm(k, "ln2", k.x, z)
        vector_steps(k, "l2_start", lambda v, step: step(v.tensor_copy(total[:, :, :], z[:, :, :])))
        dinv = bc(k.dinv0[:, :].unsqueeze(2), wide)
        acc_v = acc[:, :].rearrange("p (w d) -> p w d", d=D)
        for r in range(3):
            vector_steps(k, f"l2_load{r}", lambda v, step: None,
                         loads=[(w[:, :, :], io[f"L2_gnn_W{r + 1}"].rearrange("t i o -> i t o")),
                                (bias[:, :], io[f"L2_gnn_b{r + 1}"].partition_broadcast(P))])
            project(k, f"l2_xw{r}", z, w[:, :, :].rearrange("p t o -> p (t o)"), TYPES * D,
                    lambda v, n, ps: v.tensor_scalar(rows[:, bass.ds(n, 1), :].rearrange("p a d -> p (a d)"), ps,
                                                     k.dinv0[:, bass.ds(n, 1)], None, ALU.mult))
            vector_steps(k, f"l2_store{r}", lambda v, step: step(v.memset(acc[:, 0:1], 0.0)),
                         stores=[(rows_in(table), rows[:, :, :])])
            window_sums(k, f"l2_sum{r}", acc[:, :], loc, win_i, D,
                        table=table.rearrange("n (t o) -> (n t) o", t=TYPES), index=index, weight=wgt)

            def update(v, step):
                step(v.tensor_tensor(z[:, :, :], acc_v, dinv, ALU.mult))
                step(v.tensor_tensor(z[:, :, :], z[:, :, :], bc(bias[:, :].unsqueeze(1), wide), ALU.add))
                step(v.scalar_tensor_tensor(z[:, :, :], z[:, :, :], SLOPE, z[:, :, :], ALU.mult, ALU.max))
                step(v.tensor_tensor(total[:, :, :], total[:, :, :], z[:, :, :], ALU.add))
                if r == 2:
                    step(v.scalar_tensor_tensor(k.x[:, :, :], total[:, :, :], 0.25, k.x[:, :, :],
                                                ALU.mult, ALU.add))
            vector_steps(k, f"l2_update{r}", update)


@own_semaphores
def layer_attention(k, io, out):
    nc = k.nc
    wide = [P, W, D]
    HC = 32
    t_q = nc.dram_tensor("l3_q", [NP, D], F32).ap()
    t_k = nc.dram_tensor("l3_k", [NP, D + HEADS], F32).ap()
    with ExitStack() as outer:
        h = k.sb(outer, "l3_h", [P, W, D])
        val = k.sb(outer, "l3_v", [P, W, D])
        wo = k.sb(outer, "l3_wo", [P, D])
        vecs = k.sb(outer, "l3_vecs", [P, 3, D])
        layernorm(k, "ln3", k.x, h)
        with ExitStack() as ctx:
            wqkv = k.sb(ctx, "l3_wqkv", [P, 3, D])
            b = k.sb(ctx, "l3_bqkv", [P, 3 * D])
            qkv = k.sb(ctx, "l3_qkv", [P, W, 3 * D])
            krow = k.sb(ctx, "l3_k_rows", [P, W, D + HEADS])
            wc1 = k.sb(ctx, "l3_wc1", [P, 3, HC])
            wc2 = k.sb(ctx, "l3_wc2", [P, HC, HEADS])
            bc2 = k.sb(ctx, "l3_bc2", [P, HEADS])
            nv = k.sb(ctx, "l3_node_vec", [P, W, 1])
            hid = k.sb(ctx, "l3_cons_hidden", [P, HC, W])
            con = k.sb(ctx, "l3_cons", [P, HEADS, W])
            full = N // P
            s_z = k.sem("l3_node_vec_cleared")
            with nc.Block() as block:
                @block.vector
                def _(v):
                    v.memset(nv[:, :, :], 0.0).then_inc(s_z, 1)
                    v.wait_ge(s_z, 1)
            flat = lambda name: io[name].rearrange("a b -> (a b)").partition_broadcast(P)
            vec = lambda name: io[name].partition_broadcast(P)
            loads = [(wqkv[:, n, :], io[f"L3_gnn_W{c}"]) for n, c in enumerate("qkv")]
            loads += [(b[:, n * D:(n + 1) * D], vec(f"L3_gnn_b{c}")) for n, c in enumerate("qkv")]
            loads += [(wo[:, :], io["L3_gnn_Wo"]), (vecs[:, 0, :], vec("L3_gnn_bo")),
                      (vecs[:, 1, :], vec("L3_gnn_gamma")), (vecs[:, 2, :], vec("L3_gnn_beta")),
                      (wc1[:, 0, :], flat("L3_gnn_Wc1")), (wc1[:, 1, :], vec("L3_gnn_bc1")),
                      (wc2[:, :, :].rearrange("p a b -> p (a b)"), flat("L3_gnn_Wc2")), (bc2[:, :], vec("L3_gnn_bc2")),
                      (nv[:, 0:full, :], rows_in(io["node_vec1"][0:full * P, :])),
                      (nv[0:N - full * P, full, :], io["node_vec1"][full * P:N, :])]

            def cons(v, step):
                for j in range(HC):
                    step(v.tensor_scalar(hid[:, j, :], nv[:, :, 0], wc1[:, 0, j:j + 1], wc1[:, 1, j:j + 1],
                                         ALU.mult, ALU.add))
                step(v.tensor_scalar(hid[:, :, :], hid[:, :, :], 0.0, None, ALU.max))
                for hd in range(HEADS):
                    step(v.tensor_copy(con[:, hd, :], bc(bc2[:, hd:hd + 1], [P, W])))
                    for j in range(HC):
                        step(v.scalar_tensor_tensor(con[:, hd, :], hid[:, j, :], wc2[:, j, hd:hd + 1],
                                                    con[:, hd, :], ALU.mult, ALU.add))
            with nc.allow_non_contiguous_dma(reason="one number for each node, once"):
                vector_steps(k, "l3_cons", cons, loads=loads)
            s_sig = k.sem("l3_sigmoid")
            with nc.Block() as block:
                @block.scalar
                def _(act):
                    act.activation(con[:, :, :], con[:, :, :], ACT.Sigmoid).then_inc(s_sig, 1)
                    act.wait_ge(s_sig, 1)
            project(k, "l3_qkv", h, wqkv[:, :, :].rearrange("p t o -> p (t o)"), 3 * D,
                    lambda v, n, ps: v.tensor_tensor(qkv[:, bass.ds(n, 1), :].rearrange("p a d -> p (a d)"),
                                                     ps, b[:, :], ALU.add))

            def rows(v, step):
                step(v.tensor_copy(val[:, :, :], qkv[:, :, 2 * D:3 * D]))
                step(v.tensor_copy(krow[:, :, 0:D], qkv[:, :, D:2 * D]))
                step(v.tensor_copy(krow[:, :, D:D + HEADS], con[:, :, :].rearrange("p h w -> p w h")))
            vector_steps(k, "l3_rows", rows, stores=[(rows_in(t_q), qkv[:, :, 0:D]), (rows_in(t_k), krow[:, :, :])])
        with ExitStack() as ctx:
            s = k.sb(ctx, "l3_scores", [P, T, HEADS])
            cns = k.sb(ctx, "l3_cons_slots", [P, T, HEADS])
            s_p, s_c = k.sem("l3_products"), k.sem("l3_cons_copied")

            def consume(v, n, a, b):
                at = bass.ds(n * G, G)
                v.tensor_copy(cns[:, at, :], b[:, :, D:D + HEADS]).then_inc(s_c, 1)
                v.tensor_tensor(a, a, b[:, :, 0:D], ALU.mult).then_inc(s_p, 1)
                v.wait_ge(s_p, n + 1)
                return v.tensor_reduce(s[:, at, :], a.rearrange("p g (h c) -> p g h c", c=C),
                                       AXX, ALU.add)
            edge_rows(k, "l3_edges", t_q, D, t_k, D + HEADS, consume)
            with ExitStack() as inner:
                terms = k.sb(inner, "l3_terms", [P, T, 2 * HEADS])

                def score(v, step):
                    step(v.scalar_tensor_tensor(s[:, :, :], s[:, :, :], float(C) ** -0.5, terms[:, :, 0:HEADS],
                                                ALU.mult, ALU.add))
                    step(v.tensor_tensor(s[:, :, :], s[:, :, :], cns[:, :, :], ALU.mult))
                    step(v.tensor_tensor(s[:, :, :], s[:, :, :], terms[:, :, HEADS:], ALU.add))
                    step(v.tensor_copy(cns[:, :, :], s[:, :, :]))
                vector_steps(k, "l3_score", score,
                             loads=[(terms[:, :, :], k.list_dst.rearrange("(t p) r -> p t r", p=P)[:, :, 2:RD])])
            segment_max(k, "l3_max", cns[:, :, :])
            s_a, s_b = k.sem("l3_less_top"), k.sem("l3_exp")
            with nc.Block() as block:
                @block.vector
                def _(v):
                    v.tensor_tensor(s[:, :, :], s[:, :, :], cns[:, :, :], ALU.subtract).then_inc(s_a, 1)

                @block.scalar
                def _(act):
                    act.wait_ge(s_a, 1)
                    act.activation(s[:, :, :], s[:, :, :], ACT.Exp).then_inc(s_b, 1)
                    act.wait_ge(s_b, 1)
            acc = k.sb(ctx, "l3_acc", [P, W * HEADS])
            window_sums(k, "l3_sum", acc[:, :], k.loc, k.win_i, HEADS, values=s)
            acc_v = acc[:, :].rearrange("p (w h) -> p w h", h=HEADS)
            inv = k.sb(ctx, "l3_inv", [P, W, HEADS])

            def weigh(v, step):
                step(v.tensor_tensor(inv[:, :, :], acc_v, bc(k.no_edge[:, :].unsqueeze(2), [P, W, HEADS]), ALU.add))
                step(v.reciprocal(inv[:, :, :], inv[:, :, :]))
                step(v.tensor_tensor(inv[:, :, :], inv[:, :, :], acc_v, ALU.mult))
                heads = val[:, :, :].rearrange("p w (h c) -> p w h c", c=C)
                step(v.tensor_tensor(heads, heads, bc(inv[:, :, :].unsqueeze(3), [P, W, HEADS, C]), ALU.mult))
            vector_steps(k, "l3_weigh", weigh)
        y = k.sb(outer, "l3_y", [P, W, D])
        project(k, "l3_out", val, wo[:, :], D,
                lambda v, n, ps: v.tensor_tensor(y[:, bass.ds(n, 1), :].rearrange("p a d -> p (a d)"), ps,
                                                 vecs[:, 0, :], ALU.add))
        vector_steps(k, "l3_residual", lambda v, step: step(v.tensor_tensor(y[:, :, :], y[:, :, :], h[:, :, :],
                                                                             ALU.add)))
        layernorm(k, "ln4", y, h, relu=False, gamma=vecs[:, 1, :], beta=vecs[:, 2, :])
        full = N // P
        vector_steps(k, "l3_finish",
                     lambda v, step: step(v.tensor_tensor(k.x[:, :, :], k.x[:, :, :], h[:, :, :], ALU.add)),
                     stores=[(rows_in(out[0:full * P, :]), k.x[:, 0:full, :]),
                             (out[full * P:N, :], k.x[0:N - full * P, full, :])])


def program(nc, io, out):
    with ExitStack() as ctx:
        k = Core(nc)
        k.moved = [ctx.enter_context(nc.semaphore(f"moved_by_pool{h}")) for h in range(2)]
        k.ps = [ctx.enter_context(nc.psum_tensor(f"bank{b}", [P, 512], F32)) for b in range(8)]
        k.x = k.sb(ctx, "x_sb", [P, W, D])
        k.iota = k.sb(ctx, "iota", [P, P])
        k.tile_no = k.sb(ctx, "tile_no", [P, T])
        k.pid = k.sb(ctx, "pid", [P, 1])
        k.ones = k.sb(ctx, "ones", [P, P])
        k.eps = k.sb(ctx, "eps", [P, 1])
        k.ident = k.sb(ctx, "ident", [P, P])
        k.before = k.sb(ctx, "before", [P, P])
        k.win_dst = k.sb(ctx, "win_dst", [P, T])
        k.win_src = k.sb(ctx, "win_src", [P, T])
        k.src_i = k.sb(ctx, "src_i", [P, T], I32)
        k.dst_i = k.sb(ctx, "dst_i", [P, T], I32)
        k.dst_f = k.sb(ctx, "dst_f", [P, T])
        k.loc = k.sb(ctx, "loc", [P, T + G])
        k.win_i = k.sb(ctx, "win_dst_i", [1, T], I32)
        k.deg, k.dinv, k.dinv0, k.inv_deg, k.no_edge = (
            k.sb(ctx, name, [P, W]) for name in ("deg", "dinv", "dinv0", "inv_deg", "no_edge"))
        list_a = nc.dram_tensor("half_sorted", [E, RD], F32)
        k.list_a = list_a.ap()
        k.list_dst = nc.dram_tensor("by_dst", [SLOTS, RD], F32).ap()
        k.list_src = nc.dram_tensor("by_src", [SLOTS, RS], F32).ap()
        setup(k, io)
        fill_pads(k, "dst", k.list_dst, RD, 1)
        fill_pads(k, "src", k.list_src, RS, 1)
        sort_by_dst(k, io)
        sort_by_src(k, io)
        read_list(k, "read_dst", k.list_dst, RD, k.src_i, k.loc, None, k.win_dst, k.win_i)
        vector_steps(k, "dst_index", lambda v, step: (
            step(v.scalar_tensor_tensor(k.dst_f[:, :], k.win_dst[:, :], float(P), k.loc[:, 0:T], ALU.mult, ALU.add)),
            step(v.tensor_scalar(k.dst_i[:, :], k.dst_f[:, :], 0.0, None, ALU.max))))
        with ExitStack() as inner:
            ones_slots = k.sb(inner, "ones_slots", [P, T, 1])
            k.ones_slots = ones_slots
            vector_steps(k, "ones_slots_v", lambda v, step: step(v.memset(ones_slots[:, :, :], 1.0)))
            layer_filter(k, io)
        layer_gat(k, io)
        layer_relational(k, io)
        layer_attention(k, io, out)


_INS = ['x', 'src', 'dst', 'edge_attr_64', 'edge_type_4', 'edge_weight', 'edge_weight1', 'node_vec1',
        'L1_gnn_W', 'L1_gnn_att_src', 'L1_gnn_att_dst', 'L1_gnn_bias',
        'L2_gnn_W1', 'L2_gnn_b1', 'L2_gnn_W2', 'L2_gnn_b2', 'L2_gnn_W3', 'L2_gnn_b3',
        'L3_gnn_Wq', 'L3_gnn_bq', 'L3_gnn_Wk', 'L3_gnn_bk', 'L3_gnn_Wv', 'L3_gnn_bv', 'L3_gnn_We', 'L3_gnn_be',
        'L3_gnn_Wc1', 'L3_gnn_bc1', 'L3_gnn_Wc2', 'L3_gnn_bc2', 'L3_gnn_Wd1', 'L3_gnn_bd1', 'L3_gnn_Wd2',
        'L3_gnn_bd2', 'L3_gnn_Wo', 'L3_gnn_bo', 'L3_gnn_gamma', 'L3_gnn_beta']


def kernel(**inputs):
    import numpy as _np
    import concourse.bacc as _bacc
    from concourse import mybir as _mybir
    from concourse.bass_utils import run_bass_kernel_spmd as _run

    nc = _bacc.Bacc("TRN2", target_bir_lowering=False, num_devices=1)
    arrays, io = {}, {}
    for name in _INS:
        a = _np.ascontiguousarray(inputs[name])
        arrays[f"in_{name}"] = a
        io[name] = nc.dram_tensor(f"in_{name}", a.shape, _mybir.dt.from_np(a.dtype), kind="ExternalInput").ap()
    out = nc.dram_tensor("out_x", (N, D), F32, kind="ExternalOutput").ap()
    program(nc, io, out)
    r = _run(nc, [arrays], core_ids=[0])
    return r.results[0]["out_x"]
```

```python
import concourse.bass as bass
import numpy as np
from concourse import mybir
from contextlib import ExitStack

F32 = mybir.dt.float32
I32 = mybir.dt.int32
ALU = mybir.AluOpType
ACT = mybir.ActivationFunctionType
AXX = mybir.AxisListType.X

P = 128
N = 3125
D = 128
W = -(-N // P)
NP = W * P
E = 100000
SB = 8
EP = max(p for p in range(1, P + 1) if E % (p * SB * 4) == 0)
EC = E // EP
HEADS = 8
C = D // HEADS
CH = 16
TILES_MIN = -(-E // P) + W
G = 4
R = 4
PSUM_BANK = 512
TG = -(-TILES_MIN // CH)
while (TG * CH) % (R * G) or TG % 3:
    TG += 1
T = TG * CH
SLOTS = T * P
L = TG * P
RD = 18
RS = 4
TYPES = 4
BIG = 1e38
EPS = 1e-5
THETA = (0.5, 0.3, 0.2, 0.1)


class Chain:

    def __init__(self, engine, sem):
        self.engine, self.sem, self.n = engine, sem, 0

    def __call__(self, instruction):
        instruction.then_inc(self.sem, 1)
        self.n += 1
        self.engine.wait_ge(self.sem, self.n)


class Core:

    def __init__(self, nc):
        self.nc, self.held = nc, []

    def sb(self, ctx, name, shape, dt=F32):
        return ctx.enter_context(self.nc.sbuf_tensor(name, shape, dt))

    def sem(self, name):
        handle = self.nc.alloc_semaphore(name=name)
        self.held[-1].append(handle)
        return handle

    def pool_dma_sems(self, name, places=R):
        return [self.nc.alloc_semaphore(name=f"{name}{h}") for h in range(places)]


def own_semaphores(stage):
    def run(k, *args, **kwargs):
        k.held.append([])
        stage(k, *args, **kwargs)
        mine = k.held.pop()
        with k.nc.Block() as block:
            @block.gpsimd
            def _(pool):
                for handle in mine:
                    pool.sem_clear(handle)
        for handle in mine:
            k.nc.release_semaphore(handle)
    return run


def in_one_block(k, *stages):
    with k.nc.Block() as block:
        engines = {"sync": block.sync, "gpsimd": block.gpsimd, "vector": block.vector,
                   "scalar": block.scalar, "tensor": block.tensor}
        for name in engines:
            bodies = [stage[name] for stage in stages if name in stage]
            if bodies:
                @engines[name]
                def _(engine):
                    for body in bodies:
                        body(engine)


def bc(ap, shape):
    return ap.to_broadcast(shape)


def rows_in(ap):
    return ap.rearrange("(w p) c -> p w c", p=P)


def by_edge(ap):
    return ap.rearrange("(p e) -> p e", e=EC)


@own_semaphores
def setup(k, io):
    nc = k.nc
    s_load, s_io, s_v = k.sem("x_loaded"), k.sem("iotas_made"), k.sem("setup_steps")
    s_id, s_ones = k.sem("identity_made"), k.sem("ones_made")
    with nc.Block() as block:
        @block.sync
        def _(sp):
            full = N // P
            sp.wait_ge(s_v, 1)
            sp.dma_start(k.x[:, 0:full, :], rows_in(io["x"][0:full * P, :])).then_inc(s_load, 16)
            sp.dma_start(k.x[0:N - full * P, full, :], io["x"][full * P:N, :]).then_inc(s_load, 16)
            sp.wait_ge(s_load, 32)

        @block.gpsimd
        def _(pool):
            pool.iota(k.iota[:, :], [[1, P]], base=0, channel_multiplier=0,
                      allow_small_or_imprecise_dtypes=True).then_inc(s_io, 1)
            pool.iota(k.tile_no[:, :], [[1, T]], base=0, channel_multiplier=0,
                      allow_small_or_imprecise_dtypes=True).then_inc(s_io, 1)
            pool.iota(k.pid[:, :], [[1, 1]], base=0, channel_multiplier=1,
                      allow_small_or_imprecise_dtypes=True).then_inc(s_io, 1)

        @block.vector
        def _(v):
            v.memset(k.x[:, :, :], 0.0).then_inc(s_v, 1)
            v.memset(k.ones[:, :], 1.0).then_inc(s_ones, 1)
            v.memset(k.eps[:, :], EPS).then_inc(s_ones, 1)
            v.wait_ge(s_io, 3)
            v.tensor_scalar(k.ident[:, :], k.iota[:, :], k.pid[:, 0:1], None, ALU.is_equal).then_inc(s_id, 1)
            v.tensor_scalar(k.before[:, :], k.iota[:, :], k.pid[:, 0:1], None, ALU.is_gt).then_inc(s_id, 1)
            v.wait_ge(s_id, 2)
            v.wait_ge(s_ones, 2)


@own_semaphores
def layernorm(k, tag, src, dst, relu=True, gamma=None, beta=None):
    nc = k.nc
    with ExitStack() as ctx:
        stat = k.sb(ctx, f"{tag}_stat", [P, 4, W])
        sq = k.sb(ctx, f"{tag}_sq", [P, W, D])
        s_v, s_var, s_std = k.sem(f"{tag}_v"), k.sem(f"{tag}_var"), k.sem(f"{tag}_std")
        wide = [P, W, D]
        with nc.Block() as block:
            @block.vector
            def _(v):
                step = Chain(v, s_v)
                step(v.tensor_reduce(stat[:, 0, :], src[:, :, :], AXX, ALU.add))
                step(v.tensor_scalar(stat[:, 1, :], stat[:, 0, :], 1.0 / D, None, ALU.mult))
                step(v.tensor_tensor(dst[:, :, :], src[:, :, :],
                                     bc(stat[:, 1, :].unsqueeze(2), wide), ALU.subtract))
                step(v.tensor_tensor(sq[:, :, :], dst[:, :, :], dst[:, :, :], ALU.mult))
                v.tensor_reduce(stat[:, 2, :], sq[:, :, :], AXX, ALU.add).then_inc(s_var, 1)
                v.wait_ge(s_std, 1)
                step(v.reciprocal(stat[:, 0, :], stat[:, 3, :]))
                step(v.tensor_tensor(dst[:, :, :], dst[:, :, :],
                                     bc(stat[:, 0, :].unsqueeze(2), wide), ALU.mult))
                if relu:
                    step(v.tensor_scalar(dst[:, :, :], dst[:, :, :], 0.0, None, ALU.max))
                if gamma is not None:
                    step(v.tensor_tensor(dst[:, :, :], dst[:, :, :],
                                         bc(gamma[:, :].unsqueeze(1), wide), ALU.mult))
                    step(v.tensor_tensor(dst[:, :, :], dst[:, :, :],
                                         bc(beta[:, :].unsqueeze(1), wide), ALU.add))

            @block.scalar
            def _(act):
                act.wait_ge(s_var, 1)
                act.activation(stat[:, 3, :], stat[:, 2, :], ACT.Sqrt, bias=k.eps[:, 0:1],
                               scale=1.0 / D).then_inc(s_std, 1)


def edge_terms(k, io, ctx, rec):
    A = 64
    H1 = 16
    pairs = SB // 2
    attr = k.sb(ctx, "attr", [EP, 2, SB, A])
    attr_t = k.sb(ctx, "attr_t", [P, 2, pairs, EP])
    we2 = k.sb(ctx, "we_twice", [P, 2, HEADS])
    be = k.sb(ctx, "be_all", [P, HEADS])
    wd1 = k.sb(ctx, "wd1_all", [P, H1])
    bd1 = k.sb(ctx, "bd1_all", [P, H1])
    wd2 = k.sb(ctx, "wd2_all", [P, H1 * HEADS])
    bd2 = k.sb(ctx, "bd2_all", [P, HEADS])
    dist = k.sb(ctx, "dist", [EP, EC])
    hid = k.sb(ctx, "dist_hidden", [EP, 2, EC])
    dterm = k.sb(ctx, "dist_term", [EP, HEADS, EC])
    s_we0, s_w = k.sem("we_cleared"), k.sem("edge_weights_loaded")
    two = lambda name: [k.sem(f"{name}0"), k.sem(f"{name}1")]
    s_at, s_tr, s_cp, s_mm, s_ev = map(two, ("attr_loaded", "attr_transposed", "attr_t_copied",
                                             "attr_terms_done", "attr_terms_kept"))
    s_h, s_ac = k.sem("hidden_ready"), k.sem("dist_steps")
    loads = 8
    def vector(v):
        v.memset(we2[:, :, :], 0.0).then_inc(s_we0, 1)
        v.wait_ge(s_w, 16 * loads)
        with v.Fori(0, EC // SB // 2) as i:
            for half in range(2):
                v.wait_ge(s_tr[half], i + 2)
                v.nop(nofuse=True)
                v.tensor_copy(attr_t[:, half, :, :],
                              k.ps[2 * half][:, 0:pairs * EP].rearrange("p (a b) -> p a b", b=EP))\
                    .then_inc(s_cp[half], 1)
                v.wait_ge(s_mm[half], i + 1)
                v.nop(nofuse=True)
                v.tensor_tensor(rec[:, bass.ds((i * 2 + half) * SB, SB), 2:10],
                                k.ps[2 * half + 1][0:EP, 0:SB * HEADS].rearrange("p (e h) -> p e h", h=HEADS),
                                bc(be[0:EP, :].unsqueeze(1), [EP, SB, HEADS]), ALU.add)\
                    .then_inc(s_ev[half], 1)
        for h in range(HEADS):
            v.tensor_copy(dterm[:, h, :], bc(bd2[0:EP, h:h + 1], [EP, EC])).then_inc(s_ac, 1)
        done = HEADS
        for j in range(H1):
            v.wait_ge(s_h, j + 1)
            for h in range(HEADS):
                v.wait_ge(s_ac, done - HEADS + 1)
                v.scalar_tensor_tensor(dterm[:, h, :], hid[:, j % 2, :],
                                       wd2[0:EP, j * HEADS + h:j * HEADS + h + 1],
                                       dterm[:, h, :], ALU.mult, ALU.add).then_inc(s_ac, 1)
                done += 1
        v.wait_ge(s_ac, done)
        v.tensor_copy(rec[:, :, 10:18], dterm[:, :, :].rearrange("p h e -> p e h")).then_inc(s_ac, 1)

    def scalar(act):
        act.wait_ge(s_w, 16 * loads)
        for j in range(H1):
            if j >= 2:
                act.wait_ge(s_ac, HEADS * j)
            act.activation(hid[:, j % 2, :], dist[:, :], ACT.Relu, bias=bd1[0:EP, j:j + 1],
                           scale=wd1[0:EP, j:j + 1]).then_inc(s_h, 1)

    def tensor(pe):
        for s in s_tr + s_ev:
            pe.sem_inc(s, 1)
        pe.wait_ge(s_w, 16 * loads)
        with pe.Fori(0, EC // SB // 2) as i:
            for half in range(2):
                pe.wait_ge(s_at[half], i * 16 + 16)
                pe.wait_ge(s_ev[half], i + 1)
                pe.nop(nofuse=True)
                for a in range(pairs):
                    ins = pe.transpose(k.ps[2 * half][:, a * EP:(a + 1) * EP],
                                       attr[:, half, 2 * a:2 * a + 2, :].rearrange("p a b -> p (a b)"),
                                       k.ident[0:EP, 0:EP])
                ins.then_inc(s_tr[half], 1)
            for half in range(2):
                pe.wait_ge(s_cp[half], i + 1)
                pe.nop(nofuse=True)
                for a in range(pairs):
                    ins = pe.matmul(k.ps[2 * half + 1][0:EP, a * 16:(a + 1) * 16],
                                    attr_t[:, half, a, :],
                                    we2[:, :, :].rearrange("p a b -> p (a b)"), start=True, stop=True)
                ins.then_inc(s_mm[half], 1)

    def sync(sp):
        sp.wait_ge(s_we0, 1)
        sp.dma_start(we2[0:A, 0, :], io["L3_gnn_We"]).then_inc(s_w, 16)
        sp.dma_start(we2[A:2 * A, 1, :], io["L3_gnn_We"]).then_inc(s_w, 16)
        for dst, name in ((be, "L3_gnn_be"), (bd1, "L3_gnn_bd1"), (bd2, "L3_gnn_bd2")):
            sp.dma_start(dst[:, :], io[name].partition_broadcast(P)).then_inc(s_w, 16)
        sp.dma_start(wd1[:, :], io["L3_gnn_Wd1"].rearrange("a b -> (a b)").partition_broadcast(P))\
            .then_inc(s_w, 16)
        sp.dma_start(wd2[:, :], io["L3_gnn_Wd2"].rearrange("a b -> (a b)").partition_broadcast(P))\
            .then_inc(s_w, 16)
        sp.dma_start(dist[:, :], by_edge(io["edge_weight1"].rearrange("e a -> (e a)"))).then_inc(s_w, 16)
        a_v = io["edge_attr_64"].rearrange("(p e) a -> p e a", e=EC)
        with sp.Fori(0, EC // SB // 2) as i:
            for half in range(2):
                sp.wait_ge(s_tr[half], i + 1)
                sp.nop(nofuse=True)
                sp.dma_start(attr[:, half, :, :], a_v[:, bass.ds((i * 2 + half) * SB, SB), :])\
                    .then_inc(s_at[half], 16)
    return {"vector": vector, "scalar": scalar, "tensor": tensor, "sync": sync}


def places(k, tag, ctx, key, buckets, pos, whole_tiles, win=None, bounds=None):
    hit = k.sb(ctx, f"{tag}_hit", [EP, EC])
    rank = k.sb(ctx, f"{tag}_rank", [EP, EC])
    one = k.sb(ctx, f"{tag}_one", [EP, EC])
    posf = k.sb(ctx, f"{tag}_posf", [EP, EC])
    count = k.sb(ctx, f"{tag}_count", [EP, buckets])
    total = k.sb(ctx, f"{tag}_total", [P, buckets])
    tiles = k.sb(ctx, f"{tag}_tiles", [P, buckets], I32)
    size = k.sb(ctx, f"{tag}_size", [P, buckets])
    start = k.sb(ctx, f"{tag}_start", [P, buckets])
    base = k.sb(ctx, f"{tag}_base", [P, buckets])
    s_v, s_one, s_count, s_sum = (k.sem(f"{tag}_v"), k.sem(f"{tag}_one_set"),
                                  k.sem(f"{tag}_counted"), k.sem(f"{tag}_summed"))
    s_hit, s_rank, s_pick = k.sem(f"{tag}_hits"), k.sem(f"{tag}_ranks"), k.sem(f"{tag}_picks")
    def vector(v):
        step = Chain(v, s_v)
        v.sem_inc(s_count, 1)
        v.sem_inc(s_pick, 1)
        v.memset(one[:, :], 1.0).then_inc(s_one, 1)
        v.memset(posf[:, :], 0.0).then_inc(s_one, 1)
        with v.Fori(0, buckets) as b:
            v.wait_ge(s_count, b + 1)
            v.tensor_scalar(hit[:, :], key, k.iota[0:EP, bass.ds(b, 1)], None, ALU.is_equal,
                            ALU.add, accum_out=count[:, bass.ds(b, 1)]).then_inc(s_count, 1)
        v.wait_ge(s_sum, 1)
        step(v.tensor_copy(total[:, :], k.ps[0][:, 0:buckets]))
        if whole_tiles:
            step(v.tensor_scalar(tiles[:, :], total[:, :], float(P - 1), None, ALU.add))
            step(v.tensor_scalar(tiles[:, :], tiles[:, :], 7, None, ALU.arith_shift_right))
            step(v.tensor_scalar(size[:, :], tiles[:, :], 1.0, None, ALU.max))
        else:
            step(v.tensor_copy(size[:, :], total[:, :]))
        v.wait_ge(s_one, 2)
        step(v.tensor_tensor_scan(start[:, :], k.ones[:, 0:buckets], size[:, :], 0.0,
                                  ALU.mult, ALU.add))
        step(v.tensor_tensor(start[:, :], start[:, :], size[:, :], ALU.subtract))
        step(v.tensor_scalar(base[:, :], start[:, :], float(P if whole_tiles else 1), -1.0,
                             ALU.mult, ALU.add))
        step(v.tensor_tensor(base[:, :], base[:, :], k.ps[1][:, 0:buckets], ALU.add))
        with v.Fori(0, buckets) as b:
            v.wait_ge(s_pick, b + 1)
            v.tensor_scalar(hit[:, :], key, k.iota[0:EP, bass.ds(b, 1)], None, ALU.is_equal)\
                .then_inc(s_hit, 1)
            v.wait_ge(s_hit, b + 1)
            v.tensor_copy(count[:, 0:1], base[0:EP, bass.ds(b, 1)]).then_inc(s_rank, 1)
            v.wait_ge(s_rank, b * 2 + 1)
            v.tensor_tensor_scan(rank[:, :], one[:, :], hit[:, :], count[:, 0:1],
                                 ALU.mult, ALU.add).then_inc(s_rank, 1)
            v.wait_ge(s_rank, b * 2 + 2)
            v.nop(nofuse=True)
            v.copy_predicated(posf[:, :], hit[:, :].bitcast(I32), rank[:, :]).then_inc(s_pick, 1)
        v.wait_ge(s_pick, buckets + 1)
        step(v.tensor_copy(pos, posf[:, :]))
        if bounds is not None:
            step(v.tensor_copy(bounds[:, 0:buckets], start[0:1, :]))
            step(v.tensor_tensor(bounds[:, buckets:buckets + 1], start[0:1, buckets - 1:],
                                 size[0:1, buckets - 1:], ALU.add))
        if win is not None:
            step(v.memset(win[:, :], -1.0))
            for b in range(buckets):
                step(v.scalar_tensor_tensor(win[:, :], k.tile_no[:, :], start[:, b:b + 1],
                                            win[:, :], ALU.is_ge, ALU.add))

    def tensor(pe):
        pe.wait_ge(s_count, buckets + 1)
        pe.matmul(k.ps[0][:, 0:buckets], k.ones[0:EP, :], count[:, :], start=True, stop=True)
        pe.matmul(k.ps[1][:, 0:buckets], k.before[0:EP, :], count[:, :], start=True, stop=True)\
            .then_inc(s_sum, 1)
    return {"vector": vector, "tensor": tensor}


def scatter(k, tag, ctx, rec, width, pos, table, ready=None):
    st_rec = k.sb(ctx, f"{tag}_st_rec", [EP, R, SB, width])
    st_pos = k.sb(ctx, f"{tag}_st_pos", [EP, R, SB], I32)
    s_st = [k.sem(f"{tag}_staged{r}") for r in range(R)]
    s_out = k.pool_dma_sems(f"{tag}_scattered")
    steps = EC // (SB * R)

    def gpsimd(pool):
        if ready is not None:
            pool.wait_ge(ready, 1)

        def stage(n, r):
            at = bass.ds(n * SB, SB)
            pool.tensor_copy(st_pos[:, r, :], pos[:, at]).then_inc(s_st[r], 1)
            pool.tensor_copy(st_rec[:, r, :, :], rec[:, at, :]).then_inc(s_st[r], 1)

        def send(r):
            for e in range(SB):
                pool.indirect_dma_start(table, bass.IndirectOffsetOnAxis(ap=st_pos[:, r, e:e + 1], axis=0),
                                        st_rec[:, r, e, :], None).then_inc(s_out[r], 16)
        for r in range(R):
            stage(r, r)
        for r in range(R):
            pool.wait_ge(s_st[r], 2)
            send(r)
        with pool.Fori(1, steps) as i:
            for r in range(R):
                pool.wait_ge(s_out[r], i * (16 * SB))
                pool.nop(nofuse=True)
                stage(i * R + r, r)
                pool.wait_ge(s_st[r], i * 2 + 2)
                pool.nop(nofuse=True)
                send(r)
        for r in range(R):
            pool.wait_ge(s_out[r], steps * 16 * SB)
    return {"gpsimd": gpsimd}


@own_semaphores
def fill_pads(k, tag, table, width, dst_column):
    nc = k.nc
    with ExitStack() as ctx:
        pad = k.sb(ctx, f"{tag}_pad", [P, TG, width])
        s_p, s_out = k.sem(f"{tag}_pad_made"), k.sem(f"{tag}_pads_out")
        with nc.Block() as block:
            @block.vector
            def _(v):
                v.memset(pad[:, :, :], 0.0).then_inc(s_p, 1)
                v.wait_ge(s_p, 1)
                v.memset(pad[:, :, dst_column:dst_column + 1], -1.0).then_inc(s_p, 1)

            @block.sync
            def _(sp):
                sp.wait_ge(s_p, 2)
                view = table.rearrange("(c p e) r -> c p e r", c=CH, e=TG)
                for c in range(CH):
                    sp.dma_start(view[c], pad[:, :, :]).then_inc(s_out, 16)
                sp.wait_ge(s_out, 16 * CH)


def low_part(v, step, low, tmp, node):
    step(v.tensor_scalar(tmp, node, P - 1, None, ALU.bitwise_and))
    step(v.tensor_copy(low, tmp))


def high_part(v, step, high, tmp, node):
    step(v.tensor_scalar(tmp, node, P.bit_length() - 1, None, ALU.arith_shift_right))
    step(v.tensor_copy(high, tmp))


def degrees(k, ctx, low, high):
    U = 16
    bf16 = mybir.dt.bfloat16
    iota = k.sb(ctx, "iota_bf16", [EP, P], bf16)
    lo16 = k.sb(ctx, "low_bf16", [EP, EC], bf16)
    hi16 = k.sb(ctx, "high_bf16", [EP, EC], bf16)
    hot_lo = k.sb(ctx, "degree_hot_low", [EP, 2, U, P], bf16)
    hot_hi = k.sb(ctx, "degree_hot_high", [EP, 2, U, W], bf16)
    zero = k.sb(ctx, "degree_zero", [1, P], bf16)
    s_v, s_hot = k.sem("degree_v"), [k.sem(f"degree_hot{h}") for h in range(2)]
    s_mm = [k.sem(f"degree_summed{h}") for h in range(2)]

    def vector(v):
        step = Chain(v, s_v)
        step(v.tensor_copy(iota[:, :], k.iota[0:EP, :]))
        step(v.tensor_copy(lo16[:, :], low))
        step(v.tensor_copy(hi16[:, :], high))
        step(v.memset(zero[:, :], 0.0))
        with v.Fori(0, EC // U // 2) as i:
            for h in range(2):
                at = bass.ds((i * 2 + h) * U, U)
                v.wait_ge(s_mm[h], i + 1)
                v.nop(nofuse=True)
                for hot, part, n in ((hot_lo, lo16, P), (hot_hi, hi16, W)):
                    v.tensor_tensor(hot[:, h, :, :], bc(part[:, at].unsqueeze(2), [EP, U, n]),
                                    bc(iota[:, 0:n].unsqueeze(1), [EP, U, n]), ALU.is_equal).then_inc(s_hot[h], 1)
        for h in range(2):
            v.wait_ge(s_mm[h], EC // U // 2 + 1 + h)
        step(v.tensor_copy(k.deg[:, :], k.ps[7][:, 0:W]))

    def tensor(pe):
        for s in s_mm:
            pe.sem_inc(s, 1)
        pe.wait_ge(s_v, 4)
        pe.matmul(k.ps[7][:, 0:W], zero[:, :], zero[:, 0:W], start=True, stop=False)
        with pe.Fori(0, EC // U // 2) as i:
            for h in range(2):
                pe.wait_ge(s_hot[h], i * 2 + 2)
                pe.nop(nofuse=True)
                for u in range(U):
                    ins = pe.matmul(k.ps[7][:, 0:W], hot_lo[:, h, u, :], hot_hi[:, h, u, :], start=False, stop=False)
                ins.then_inc(s_mm[h], 1)
        pe.matmul(k.ps[7][:, 0:W], zero[:, :], zero[:, 0:W], start=False, stop=True).then_inc(s_mm[1], 1)
    return {"vector": vector, "tensor": tensor}


def count_matrix(k, ctx):
    bf16, f16 = mybir.dt.bfloat16, mybir.dt.float16
    HALF = NP // 2
    buf = k.sb(ctx, "cm_list", [P, T, RS])
    loc = k.sb(ctx, "cm_loc", [P, T])
    dst = k.sb(ctx, "cm_dst", [P, T])
    iota = k.sb(ctx, "cm_iota", [P, NP], f16)
    iota_p = k.sb(ctx, "cm_iota_p", [P, P], f16)
    hot_dst = k.sb(ctx, "cm_hot_dst", [P, 2, NP], bf16)
    hot_src = k.sb(ctx, "cm_hot_src", [P, 2, P], bf16)
    zero = k.sb(ctx, "cm_zero", [1, PSUM_BANK], bf16)
    row = k.sb(ctx, "cm_row", [P, NP])
    s_ld, s_v, s_io = k.sem("cm_list_loaded"), k.sem("cm_v"), k.sem("cm_iota_made")
    s_hot, s_used, s_sum = k.sem("cm_hot"), k.sem("cm_used"), k.sem("cm_window_summed")
    s_row, s_out = k.sem("cm_row_copied"), k.sem("cm_row_stored")
    banks = [(b, b * PSUM_BANK, min(PSUM_BANK, NP - b * PSUM_BANK)) for b in range(-(-NP // PSUM_BANK))]
    B = len(banks)
    at = lambda ap, n: ap[:, bass.ds(n, 1), :].rearrange("p a c -> p (a c)")

    def sync(sp):
        sp.dma_start(buf[:, :, :], k.list_src.rearrange("(t p) r -> p t r", p=P)).then_inc(s_ld, 16)
        with sp.Fori(0, W) as w:
            sp.wait_ge(s_row, (w + 2) * B)
            sp.nop(nofuse=True)
            sp.dma_start(k.counts[bass.ds(w, 1), :, :].rearrange("a p c -> (a p) c"), row[:, :]).then_inc(s_out, 16)
        sp.wait_ge(s_out, 16 * W + 16)

    def gpsimd(pool):
        pool.iota(iota[:, :], [[1, NP]], base=-HALF, channel_multiplier=0,
                  allow_small_or_imprecise_dtypes=True).then_inc(s_io, 1)
        pool.iota(iota_p[:, :], [[1, P]], base=0, channel_multiplier=0,
                  allow_small_or_imprecise_dtypes=True).then_inc(s_io, 1)

    def vector(v):
        tiles = v.value_load(k.bounds_src[0:1, W:W + 1], min_val=W, max_val=T)
        step = Chain(v, s_v)
        step(v.memset(zero[:, :], 0.0))
        v.wait_ge(s_ld, 16)
        step(v.scalar_tensor_tensor(loc[:, :], k.win_src[:, :], -float(P), buf[:, :, 1], ALU.mult, ALU.add))
        step(v.tensor_scalar(dst[:, :], buf[:, :, 3], -float(HALF), None, ALU.add))
        v.wait_ge(s_io, 2)
        with v.Fori(0, tiles) as t:
            v.wait_ge(s_used, t + 1)
            v.nop(nofuse=True)
            half = t % 2
            v.tensor_scalar(at(hot_dst, half), iota[:, :], dst[:, bass.ds(t, 1)], None, ALU.is_equal).then_inc(s_hot, 1)
            v.tensor_scalar(at(hot_src, half), iota_p[:, :], loc[:, bass.ds(t, 1)], None, ALU.is_equal)\
                .then_inc(s_hot, 1)

    def scalar(act):
        act.sem_inc(s_row, B)
        act.sem_inc(s_out, 16)
        with act.Fori(0, W) as w:
            act.wait_ge(s_out, w * 16 + 16)
            act.nop(nofuse=True)
            for b, col, n in banks:
                act.wait_ge(s_sum, w * B + b + 1)
                act.nop(nofuse=True)
                act.copy(row[:, col:col + n], k.ps[b][:, 0:n]).then_inc(s_row, 1)

    def tensor(pe):
        pe.wait_ge(s_v, 1)
        pe.sem_inc(s_used, 2)
        with pe.Fori(0, W) as w:
            first = pe.value_load(k.bounds_src[0:1, bass.ds(w, 1)], min_val=0, max_val=T)
            behind = pe.value_load(k.bounds_src[0:1, bass.ds(w + 1, 1)], min_val=1, max_val=T)
            for b, col, n in banks:
                pe.wait_ge(s_row, w * B + b + 1)
                pe.nop(nofuse=True)
                pe.matmul(k.ps[b][:, 0:n], zero[:, 0:P], zero[:, 0:n], start=True, stop=False)
            with pe.Fori(first, behind) as t:
                pe.wait_ge(s_hot, t * 2 + 2)
                pe.nop(nofuse=True)
                half = t % 2
                for b, col, n in banks:
                    ins = pe.matmul(k.ps[b][:, 0:n], at(hot_src, half),
                                    hot_dst[:, bass.ds(half, 1), col:col + n].rearrange("p a c -> p (a c)"),
                                    start=False, stop=False)
                ins.then_inc(s_used, 1)
            for b, col, n in banks:
                pe.matmul(k.ps[b][:, 0:n], zero[:, 0:P], zero[:, 0:n], start=False, stop=True).then_inc(s_sum, 1)
    return {"sync": sync, "gpsimd": gpsimd, "vector": vector, "scalar": scalar, "tensor": tensor}


@own_semaphores
def src_places(k, io, rec, pos):
    with ExitStack() as ctx:
        key = k.sb(ctx, "key_src", [EP, EC])
        node = k.sb(ctx, "node_src", [EP, 3, EC], I32)
        tmp = k.sb(ctx, "tmp_src", [EP, EC], I32)
        wgt = k.sb(ctx, "weight_src", [EP, EC])
        s_ld, s_cv = k.sem("typed_edges_loaded"), k.sem("typed_edges_in_records")

        def sync(sp):
            for n, name in enumerate(("src", "dst", "edge_type_4")):
                sp.dma_start(node[:, n, :], by_edge(io[name])).then_inc(s_ld, 16)
            sp.dma_start(wgt[:, :], by_edge(io["edge_weight"])).then_inc(s_ld, 16)

        def vector(v):
            step = Chain(v, s_cv)
            v.wait_ge(s_ld, 64)
            step(v.tensor_copy(key[:, :], node[:, 2, :]))
            step(v.tensor_copy(rec[:, :, 3], node[:, 1, :]))
            step(v.scalar_tensor_tensor(rec[:, :, 0], rec[:, :, 3], float(TYPES), key[:, :], ALU.mult, ALU.add))
            step(v.tensor_copy(rec[:, :, 1], node[:, 0, :]))
            step(v.tensor_copy(rec[:, :, 2], wgt[:, :]))
            high_part(v, step, key[:, :], tmp[:, :], node[:, 0, :])
        in_one_block(k, {"sync": sync, "vector": vector},
                     places(k, "sort_src", ctx, key[:, :], W, pos[:, :], True, k.win_src, k.bounds_src))


@own_semaphores
def sort_both(k, io):
    nc = k.nc
    with ExitStack() as outer:
        rec = k.sb(outer, "rec_dst", [EP, EC, RD])
        pos = k.sb(outer, "pos_dst", [EP, EC], I32)
        key = k.sb(outer, "key_dst", [EP, EC])
        node = k.sb(outer, "node_dst", [EP, EC], I32)
        tmp = k.sb(outer, "tmp_dst", [EP, EC], I32)
        steps_back = k.sb(outer, "steps_back", [P, 2])
        unsorted = k.sb(outer, "unsorted", [1, 1], I32)
        with ExitStack() as ctx:
            rec_src = k.sb(ctx, "rec_src", [EP, EC, RS])
            pos_src = k.sb(ctx, "pos_src", [EP, EC], I32)
            src_places(k, io, rec_src, pos_src)
            low = k.sb(ctx, "low_dst", [EP, EC])
            behind = k.sb(ctx, "dst_behind", [EP, EC], I32)
            s_ld, s_z, s_cv, s_back, s_n = (k.sem("src_dst_loaded"), k.sem("behind_set"),
                                            k.sem("src_dst_in_records"), k.sem("steps_back_counted"),
                                            k.sem("steps_back_summed"))

            def sync(sp):
                sp.dma_start(tmp[:, :], by_edge(io["src"])).then_inc(s_ld, 16)
                sp.dma_start(node[:, :], by_edge(io["dst"])).then_inc(s_ld, 16)
                sp.wait_ge(s_z, 1)
                rest = (EP - 1) * EC
                sp.dma_start(behind[0:EP - 1, :], by_edge(io["dst"][1:rest + 1])).then_inc(s_ld, 16)
                sp.dma_start(behind[EP - 1:EP, 0:EC - 1],
                             io["dst"][rest + 1:E].rearrange("(p e) -> p e", p=1)).then_inc(s_ld, 16)

            def vector(v):
                v.memset(behind[:, :], NP).then_inc(s_z, 1)
                v.wait_ge(s_ld, 64)
                step = Chain(v, s_cv)
                step(v.tensor_copy(rec[:, :, 0], tmp[:, :]))
                step(v.tensor_copy(rec[:, :, 1], node[:, :]))
                step(v.tensor_copy(low[:, :], behind[:, :]))
                step(v.tensor_tensor(key[:, :], rec[:, :, 1], low[:, :], ALU.is_gt))
                v.tensor_reduce(steps_back[0:EP, 0:1], key[:, :], AXX, ALU.add).then_inc(s_back, 1)
                v.wait_ge(s_back, 1)
                v.wait_ge(s_n, 1)
                step(v.tensor_copy(unsorted[:, :], k.ps[6][0:1, 0:1]))
                low_part(v, step, low[:, :], tmp[:, :], node[:, :])
                high_part(v, step, key[:, :], tmp[:, :], node[:, :])

            def tensor(pe):
                pe.wait_ge(s_back, 1)
                pe.matmul(k.ps[6][:, 0:1], k.ones[0:EP, :], steps_back[0:EP, 0:1], start=True, stop=True).then_inc(s_n, 1)
            in_one_block(k, {"sync": sync, "vector": vector, "tensor": tensor},
                         scatter(k, "move_src", ctx, rec_src, RS, pos_src, k.list_src),
                         degrees(k, ctx, low[:, :], key[:, :]), edge_terms(k, io, ctx, rec))
        with ExitStack() as ctx:
            s_pos, s_v, s_list, s_back = (k.sem("half_places_made"), k.sem("half_v"), k.sem("half_sorted"),
                                          k.sem("half_sorted_back"))
            half = places(k, "sort_low", ctx, key[:, :], P, pos[:, :], False)
            move = scatter(k, "move_low", ctx, rec, RD, pos, k.list_a, ready=s_pos)

            def if_unsorted(body):
                def run(engine):
                    needed = engine.value_load(unsorted[0:1, 0:1], min_val=0, max_val=E)
                    with engine.If(needed):
                        body(engine)
                    with engine.Else():
                        engine.nop()
                    engine.nop(nofuse=True)
                return run

            def vector(v):
                step = Chain(v, s_v)
                low_part(v, step, key[:, :], tmp[:, :], node[:, :])
                half["vector"](v)
                v.nop(nofuse=True).then_inc(s_pos, 1)
                v.wait_ge(s_back, 16)
                step(v.tensor_copy(node[:, :], rec[:, :, 1]))
                high_part(v, step, key[:, :], tmp[:, :], node[:, :])

            def gpsimd(pool):
                move["gpsimd"](pool)
                pool.nop(nofuse=True).then_inc(s_list, 1)

            def sync(sp):
                sp.wait_ge(s_list, 1)
                sp.dma_start(rec[:, :, :], k.list_a.rearrange("(p e) r -> p e r", e=EC)).then_inc(s_back, 16)
                sp.wait_ge(s_back, 16)
            in_one_block(k, {"vector": if_unsorted(vector), "tensor": if_unsorted(half["tensor"]),
                             "gpsimd": if_unsorted(gpsimd), "sync": if_unsorted(sync)})
        with ExitStack() as ctx:
            in_one_block(k, places(k, "sort_dst", ctx, key[:, :], W, pos[:, :], True, k.win_dst))
        with ExitStack() as ctx:
            in_one_block(k, count_matrix(k, ctx), scatter(k, "move_dst", ctx, rec, RD, pos, k.list_dst))


@own_semaphores
def read_list(k, tag, table, width, index, loc, extra, win, win_i):
    nc = k.nc
    with ExitStack() as ctx:
        buf = k.sb(ctx, f"{tag}_buf", [P, T, 4])
        s_ld, s_v = k.sem(f"{tag}_loaded"), k.sem(f"{tag}_v")
        with nc.Block() as block:
            @block.sync
            def _(sp):
                sp.dma_start(buf[:, :, :], table.rearrange("(t p) r -> p t r", p=P)[:, :, 0:4]).then_inc(s_ld, 16)

            @block.vector
            def _(v):
                step = Chain(v, s_v)
                v.wait_ge(s_ld, 16)
                step(v.tensor_copy(index[:, :], buf[:, :, 0]))
                step(v.scalar_tensor_tensor(loc[:, 0:T], win[:, :], -float(P), buf[:, :, 1],
                                            ALU.mult, ALU.add))
                step(v.memset(loc[:, T:T + G], -1.0))
                if extra is not None:
                    step(v.tensor_copy(extra[:, 0:T], buf[:, :, 2]))
                    step(v.memset(extra[:, T:T + G], 0.0))
                step(v.tensor_copy(win_i[:, :], win[0:1, :]))
@own_semaphores
def window_sums(k, tag, acc, loc, win_i, cols, table=None, index=None, weight=None, values=None,
                stream=None, shares=None):
    nc = k.nc
    steps = T // (R * G)
    in_bank = PSUM_BANK // cols
    banks = -(-G // in_bank)
    assert banks * R <= 8

    def bank(r, g):
        at = g % in_bank * cols
        return k.ps[r * banks + g // in_bank][:, at:at + cols]

    with ExitStack() as ctx:
        hot = k.sb(ctx, f"{tag}_hot", [P, R, G, P])
        s_hot, s_used, s_idx, s_row, s_msg = ([k.sem(f"{tag}_{name}{r}") for r in range(R)] for name in
                                              ("hot", "summed", "index_staged", "rows", "messages"))
        s_z, s_add, s_shares = k.sem(f"{tag}_cleared"), k.sem(f"{tag}_added"), k.sem(f"{tag}_shares_copied")
        rows = msg = st = None
        if table is not None:
            s_row = k.pool_dma_sems(f"{tag}_gathered")
            rows = k.sb(ctx, f"{tag}_rows", [P, R, G, cols])
            st = k.sb(ctx, f"{tag}_st", [P, R, G], I32)
        if stream is not None:
            rows = k.sb(ctx, f"{tag}_rows", [P, R, G, D])
            msg = k.sb(ctx, f"{tag}_msg", [P, R, G, cols])
        with nc.Block() as block:
            if table is not None:
                @block.gpsimd
                def _(pool):
                    with pool.Fori(0, steps) as i:
                        for r in range(R):
                            pool.wait_ge(s_used[r], i + 1)
                            pool.nop(nofuse=True)
                            pool.tensor_copy(st[:, r, :], index[:, bass.ds((i * R + r) * G, G)])\
                                .then_inc(s_idx[r], 1)
                            pool.wait_ge(s_idx[r], i + 1)
                            pool.nop(nofuse=True)
                            for g in range(G):
                                pool.indirect_dma_start(
                                    rows[:, r, g, :], None, table,
                                    bass.IndirectOffsetOnAxis(ap=st[:, r, g:g + 1], axis=0)).then_inc(s_row[r], 16)
            if stream is not None:
                @block.sync
                def _(sp):
                    with sp.Fori(0, steps) as i:
                        for r in range(R):
                            sp.wait_ge(s_used[r], i + 1)
                            sp.nop(nofuse=True)
                            sp.dma_start(rows[:, r, :, :],
                                         stream[bass.ds(i * R + r, 1), :, :, :].rearrange("a p g c -> (a p) g c"))\
                                .then_inc(s_row[r], 16)

            @block.vector
            def _(v):
                def one_hots(n, r):
                    for g in range(G):
                        at = n * G + g
                        if weight is not None:
                            v.tensor_scalar(hot[:, r, g, :], k.iota[:, :], loc[:, bass.ds(at, 1)],
                                            weight[:, bass.ds(at, 1)], ALU.is_equal, ALU.mult).then_inc(s_hot[r], 1)
                        else:
                            v.tensor_scalar(hot[:, r, g, :], k.iota[:, :], loc[:, bass.ds(at, 1)], None,
                                            ALU.is_equal).then_inc(s_hot[r], 1)

                def messages(i, r):
                    if stream is None:
                        return
                    v.wait_ge(s_row[r], i * 16 + 16)
                    v.nop(nofuse=True)
                    at = bass.ds((i * R + r) * G, G)
                    n = shares[0].shape[2]
                    for j, share in enumerate(shares):
                        v.tensor_copy(msg[:, r, :, D + j * n:D + (j + 1) * n], share[:, at, :]).then_inc(s_msg[r], 1)
                    v.tensor_tensor(msg[:, r, :, 0:D].rearrange("p g (a c) -> p g a c", c=C),
                                    rows[:, r, :, :].rearrange("p g (a c) -> p g a c", c=C),
                                    bc(shares[0][:, at, :].unsqueeze(3), [P, G, HEADS, C]), ALU.mult)\
                        .then_inc(s_msg[r], 1)

                def adds(i, r):
                    to = [v.value_load(win_i[0:1, bass.ds((i * R + r) * G + g, 1)], min_val=0,
                                       max_val=W - 1) for g in range(G)]
                    v.wait_ge(s_used[r], i + 2)
                    for g in range(G):
                        v.wait_ge(s_add, (i * R + r + R) * G + g)
                        part = acc[:, bass.ds(to[g] * cols, cols)]
                        v.tensor_tensor(part, part, bank(r, g), ALU.add).then_inc(s_add, 1)

                v.memset(acc[:, :], 0.0).then_inc(s_z, 1)
                v.wait_ge(s_z, 1)
                one_hots(0, 0)
                with v.Fori(0, steps) as i:
                    for r in range(R):
                        messages(i, r)
                        one_hots(i * R + r + 1, (r + 1) % R)
                        adds(i, r)

            @block.tensor
            def _(pe):
                for s in s_used:
                    pe.sem_inc(s, 1)
                pe.sem_inc(s_add, R * G)
                with pe.Fori(0, steps) as i:
                    for r in range(R):
                        pe.wait_ge(s_hot[r], (i + 1) * G)
                        if table is not None:
                            pe.wait_ge(s_row[r], (i + 1) * (16 * G))
                        if stream is not None:
                            pe.wait_ge(s_msg[r], (i + 1) * (len(shares) + 1))
                        pe.wait_ge(s_add, (i * R + r + 1) * G)
                        pe.nop(nofuse=True)
                        for g in range(G):
                            rhs = (msg if msg is not None else rows)[:, r, g, :] if rows is not None else \
                                values[:, bass.ds((i * R + r) * G + g, 1), :].rearrange("p a c -> p (a c)")
                            ins = pe.matmul(bank(r, g), hot[:, r, g, :], rhs, start=True, stop=True)
                        ins.then_inc(s_used[r], 1)


@own_semaphores
def project(k, tag, src, weights, cols, keep):
    nc = k.nc
    U = 5
    with ExitStack() as ctx:
        st = k.sb(ctx, f"{tag}_st", [P, U, D])
        st_t = k.sb(ctx, f"{tag}_st_t", [P, U, P])
        s_st, s_tr, s_cp, s_mm, s_kept = (k.sem(f"{tag}_staged"), k.sem(f"{tag}_transposed"),
                                          k.sem(f"{tag}_copied"), k.sem(f"{tag}_product"), k.sem(f"{tag}_kept"))
        with nc.Block() as block:
            @block.scalar
            def _(act):
                with act.Fori(0, W // U) as i:
                    act.wait_ge(s_tr, i + 1)
                    act.nop(nofuse=True)
                    act.copy(st[:, :, :], src[:, bass.ds(i * U, U), :]).then_inc(s_st, 1)

            @block.vector
            def _(v):
                with v.Fori(0, W // U) as i:
                    v.wait_ge(s_tr, i + 2)
                    v.wait_ge(s_mm, i + 1)
                    v.nop(nofuse=True)
                    v.tensor_copy(st_t[:, 0:4, :], k.ps[0][:, :].rearrange("p (a b) -> p a b", b=P)).then_inc(s_cp, 1)
                    v.tensor_copy(st_t[:, 4, :], k.ps[1][:, 0:P]).then_inc(s_cp, 1)
                    v.wait_ge(s_mm, i + 2)
                    v.nop(nofuse=True)
                    for u in range(U):
                        keep(v, i * U + u, k.ps[2 + u][:, 0:cols]).then_inc(s_kept, 1)

            @block.tensor
            def _(pe):
                for s in (s_tr, s_mm, s_cp, s_kept):
                    pe.sem_inc(s, 1)
                with pe.Fori(0, W // U) as i:
                    pe.wait_ge(s_st, i + 1)
                    pe.wait_ge(s_cp, i * 2 + 1)
                    pe.nop(nofuse=True)
                    for u in range(U):
                        ins = pe.transpose(k.ps[u // 4][:, (u % 4) * P:(u % 4 + 1) * P], st[:, u, :], k.ident[:, :])
                    ins.then_inc(s_tr, 1)
                    pe.wait_ge(s_cp, i * 2 + 3)
                    pe.wait_ge(s_kept, i * U + 1)
                    pe.nop(nofuse=True)
                    for u in range(U):
                        ins = pe.matmul(k.ps[2 + u][:, 0:cols], st_t[:, u, :], weights, start=True, stop=True)
                    ins.then_inc(s_mm, 1)


@own_semaphores
def vector_steps(k, tag, steps, loads=(), stores=()):
    nc = k.nc
    s_ld, s_v, s_st = k.sem(f"{tag}_loads"), k.sem(f"{tag}_v"), k.sem(f"{tag}_stores")
    done = {}
    with nc.Block() as block:
        @block.vector
        def _(v):
            step = Chain(v, s_v)
            if loads:
                v.wait_ge(s_ld, 16 * len(loads))
            steps(v, step)
            done["n"] = step.n

        @block.sync
        def _(sp):
            for dst, src in loads:
                sp.dma_start(dst, src).then_inc(s_ld, 16)
            if stores:
                sp.wait_ge(s_v, done["n"])
            for dst, src in stores:
                sp.dma_start(dst, src).then_inc(s_st, 16)
            if stores:
                sp.wait_ge(s_st, 16 * len(stores))


@own_semaphores
def edge_rows(k, tag, table_src, cols_src, table_dst, cols_dst, consume, keep_rows=None):
    nc = k.nc
    steps = T // (R * G)
    with ExitStack() as ctx:
        a = k.sb(ctx, f"{tag}_by_src", [P, R, G, cols_src])
        b = k.sb(ctx, f"{tag}_by_dst", [P, R, G, cols_dst])
        st = k.sb(ctx, f"{tag}_st", [P, R, 2, G], I32)
        s_st, s_done, s_kept = ([k.sem(f"{tag}_{name}{r}") for r in range(R)] for name in
                                ("staged", "consumed", "kept"))
        s_row = k.pool_dma_sems(f"{tag}_gathered")
        scratch = {}
        with nc.Block() as block:
            @block.gpsimd
            def _(pool):
                with pool.Fori(0, steps) as i:
                    for r in range(R):
                        at = bass.ds((i * R + r) * G, G)
                        pool.wait_ge(s_done[r], i + 1)
                        if keep_rows is not None:
                            pool.wait_ge(s_kept[r], i * 16 + 1)
                        pool.nop(nofuse=True)
                        pool.tensor_copy(st[:, r, 0, :], k.src_i[:, at]).then_inc(s_st[r], 1)
                        pool.tensor_copy(st[:, r, 1, :], k.dst_i[:, at]).then_inc(s_st[r], 1)
                        pool.wait_ge(s_st[r], i * 2 + 2)
                        pool.nop(nofuse=True)
                        for g in range(G):
                            pool.indirect_dma_start(
                                a[:, r, g, :], None, table_src,
                                bass.IndirectOffsetOnAxis(ap=st[:, r, 0, g:g + 1], axis=0)).then_inc(s_row[r], 16)
                            pool.indirect_dma_start(
                                b[:, r, g, :], None, table_dst,
                                bass.IndirectOffsetOnAxis(ap=st[:, r, 1, g:g + 1], axis=0)).then_inc(s_row[r], 16)

            @block.vector
            def _(v):
                for s in s_done:
                    v.sem_inc(s, 1)
                with v.Fori(0, steps) as i:
                    for r in range(R):
                        v.wait_ge(s_row[r], (i + 1) * (32 * G))
                        v.nop(nofuse=True)
                        consume(v, (i * R + r), a[:, r, :, :], b[:, r, :, :]).then_inc(s_done[r], 1)

            if keep_rows is not None:
                @block.sync
                def _(sp):
                    for s in s_kept:
                        sp.sem_inc(s, 1)
                    with sp.Fori(0, steps) as i:
                        for r in range(R):
                            sp.wait_ge(s_row[r], (i + 1) * (32 * G))
                            sp.nop(nofuse=True)
                            sp.dma_start(keep_rows[bass.ds(i * R + r, 1), :, :, :].rearrange("a p g c -> (a p) g c"),
                                         a[:, r, :, 0:D]).then_inc(s_kept[r], 16)
                    for r in range(R):
                        sp.wait_ge(s_kept[r], 16 * steps + 1)


@own_semaphores
def across(k, tag, src, dst, forward, broadcast=False):
    nc = k.nc
    U = 3
    with ExitStack() as ctx:
        st = k.sb(ctx, f"{tag}_st", [P, U, P])
        s_st, s_tr, s_cp = k.sem(f"{tag}_staged"), k.sem(f"{tag}_transposed"), k.sem(f"{tag}_copied")

        def slots_side(buf, i):
            if broadcast:
                ap = buf.rearrange("p (c g) -> p c g", g=TG)[:, :, bass.ds(i * U, U)]
                return bc(ap.rearrange("p c g -> p g c").unsqueeze(3), [P, U, CH, HEADS])
            ap = buf.rearrange("p (c g) h -> p c g h", g=TG)[:, :, bass.ds(i * U, U), :]
            return ap.rearrange("p c g h -> p g c h")

        with nc.Block() as block:
            @block.scalar
            def _(act):
                with act.Fori(0, TG // U) as i:
                    act.wait_ge(s_tr, i + 1)
                    act.nop(nofuse=True)
                    if forward:
                        act.copy(st[:, :, :].rearrange("p g (c h) -> p g c h", h=HEADS),
                                 slots_side(src, i)).then_inc(s_st, 1)
                    else:
                        act.copy(st[:, :, :].rearrange("p g e -> p (g e)"),
                                 src[:, bass.ds(i * (U * P), U * P)]).then_inc(s_st, 1)

            @block.tensor
            def _(pe):
                for s in (s_tr, s_cp):
                    pe.sem_inc(s, 1)
                with pe.Fori(0, TG // U) as i:
                    pe.wait_ge(s_st, i + 1)
                    pe.wait_ge(s_cp, i + 1)
                    pe.nop(nofuse=True)
                    for u in range(U):
                        ins = pe.transpose(k.ps[0][:, u * P:(u + 1) * P], st[:, u, :], k.ident[:, :])
                    ins.then_inc(s_tr, 1)

            @block.vector
            def _(v):
                with v.Fori(0, TG // U) as i:
                    v.wait_ge(s_tr, i + 2)
                    v.nop(nofuse=True)
                    if forward:
                        v.tensor_copy(dst[:, bass.ds(i * (U * P), U * P)], k.ps[0][:, 0:U * P]).then_inc(s_cp, 1)
                    else:
                        v.tensor_copy(slots_side(dst, i),
                                      k.ps[0][:, 0:U * P].rearrange("p (g c h) -> p g c h", g=U, h=HEADS))\
                            .then_inc(s_cp, 1)


@own_semaphores
def segment_max(k, tag, val):
    nc = k.nc
    with ExitStack() as ctx:
        vt = k.sb(ctx, f"{tag}_vt", [P, L])
        out = k.sb(ctx, f"{tag}_out", [P, L])
        wall = k.sb(ctx, f"{tag}_wall", [P, L + 1])
        ends = k.sb(ctx, f"{tag}_ends", [P, 2])
        rows = k.sb(ctx, f"{tag}_rows", [1, 7, HEADS, CH])
        carry = k.sb(ctx, f"{tag}_carry", [P, 2])
        across(k, f"{tag}_dst", k.dst_f, out[:, :], True, broadcast=True)
        across(k, f"{tag}_val", val, vt[:, :], True)
        s_v, s_v2, s_pe = k.sem(f"{tag}_v"), k.sem(f"{tag}_v2"), k.sem(f"{tag}_pe")
        FIRST, LAST, VAL, WALL, IN, SCAN, BACK = range(7)

        with nc.Block() as block:
            @block.vector
            def _(v):
                step = Chain(v, s_v)
                step(v.tensor_copy(ends[:, 0:1], out[:, 0:1]))
                step(v.tensor_copy(ends[:, 1:2], out[:, L - 1:L]))
                step(v.tensor_tensor(wall[:, 1:L], out[:, 1:L], out[:, 0:L - 1], ALU.not_equal))
                step(v.memset(wall[:, 0:1], 0.0))
                step(v.memset(wall[:, L:L + 1], 0.0))
                step(v.tensor_scalar(wall[:, 1:L], wall[:, 1:L], -BIG, None, ALU.mult))
                step(v.tensor_tensor_scan(out[:, :], wall[:, 0:L], vt[:, :], -BIG, ALU.add, ALU.max))
                v.nop(nofuse=True).then_inc(s_v2, 1)

                def chunks(row):
                    return rows[0:1, row, :, :]

                def border(a, b, at):
                    here, there = (slice(1, CH), slice(0, CH - 1))
                    if a == FIRST:
                        here, there = there, here
                    step(v.memset(chunks(at), -BIG))
                    step(v.tensor_tensor(rows[0:1, at, :, here], rows[0:1, b, :, here],
                                         rows[0:1, a, :, there], ALU.not_equal))
                    step(v.tensor_scalar(rows[0:1, at, :, here], rows[0:1, at, :, here], -BIG, None, ALU.mult))
                    return here, there

                def carried(n, a, b, order):
                    v.wait_ge(s_pe, 1 + 2 * n)
                    if n == 0:
                        for q, row in enumerate((FIRST, LAST)):
                            step(v.tensor_copy(chunks(row), k.ps[1][0:1, q * P:(q + 1) * P]
                                               .rearrange("p (c h) -> p h c", h=HEADS)))
                    step(v.tensor_copy(chunks(VAL), k.ps[2][0:1, n * P:(n + 1) * P]
                                       .rearrange("p (c h) -> p h c", h=HEADS)))
                    border(a, a, WALL)
                    flat = lambda row: rows[0:1, row, :, :].rearrange("p h c -> p (h c)")[:, ::order]
                    step(v.tensor_tensor_scan(flat(SCAN), flat(WALL), flat(VAL), -BIG, ALU.add, ALU.max))
                    here, there = border(a, b, IN)
                    step(v.tensor_tensor(rows[0:1, IN, :, here], rows[0:1, IN, :, here],
                                         rows[0:1, SCAN, :, there], ALU.add))
                    step(v.tensor_copy(rows[0:1, BACK, :, :].rearrange("p h c -> p (h c)")
                                       .rearrange("p (c h) -> p c h", h=HEADS),
                                       rows[0:1, IN, :, :].rearrange("p h c -> p c h")))
                    v.nop(nofuse=True).then_inc(s_v2, 1)
                    v.wait_ge(s_pe, 2 + 2 * n)
                    step(v.tensor_scalar(carry[:, n:n + 1], k.ps[3][:, n:n + 1], -BIG, None, ALU.max))

                carried(0, LAST, FIRST, 1)
                step(v.tensor_tensor_scan(out[:, :], wall[:, 0:L], vt[:, :], carry[:, 0:1], ALU.add, ALU.max))
                step(v.tensor_tensor_scan(vt[:, ::-1], wall[:, L:0:-1], out[:, ::-1], -BIG, ALU.add, ALU.max))
                v.nop(nofuse=True).then_inc(s_v2, 1)
                carried(1, FIRST, LAST, -1)
                step(v.tensor_tensor_scan(vt[:, ::-1], wall[:, L:0:-1], out[:, ::-1], carry[:, 1:2],
                                          ALU.add, ALU.max))

            @block.tensor
            def _(pe):
                for n, last in ((0, out[:, L - 1:L]), (1, vt[:, 0:1])):
                    pe.wait_ge(s_v2, 1 + 2 * n)
                    if n == 0:
                        for q in range(2):
                            pe.matmul(k.ps[1][0:1, q * P:(q + 1) * P], ends[:, q:q + 1], k.ident[:, :],
                                      start=True, stop=True)
                    pe.matmul(k.ps[2][0:1, n * P:(n + 1) * P], last, k.ident[:, :], start=True, stop=True)\
                        .then_inc(s_pe, 1)
                    pe.wait_ge(s_v2, 2 + 2 * n)
                    pe.matmul(k.ps[3][:, n:n + 1], rows[0:1, BACK, :, :].rearrange("p h c -> p (h c)"),
                              k.ones[0:1, 0:1], start=True, stop=True).then_inc(s_pe, 1)
        across(k, f"{tag}_back", vt[:, :], val, False)


@own_semaphores
def count_product(k, tag, rows, acc):
    U = 5
    with ExitStack() as ctx:
        cnt = k.sb(ctx, f"{tag}_counts", [P, U, NP])
        st = k.sb(ctx, f"{tag}_rows", [P, U, D])
        zero = k.sb(ctx, f"{tag}_zero", [1, PSUM_BANK])
        sums = k.sb(ctx, f"{tag}_sums", [P, NP])
        s_z, s_all, s_cp, s_tr, s_kept = (k.sem(f"{tag}_zero_set"), k.sem(f"{tag}_summed"), k.sem(f"{tag}_copied"),
                                          k.sem(f"{tag}_transposed"), k.sem(f"{tag}_kept"))
        s_ld, s_st, s_used = ([k.sem(f"{tag}_{name}{u}") for u in range(U)] for name in ("loaded", "staged", "used"))
        banks = [(b, b * PSUM_BANK, min(PSUM_BANK, NP - b * PSUM_BANK)) for b in range(-(-NP // PSUM_BANK))]
        per = PSUM_BANK // P

        def sync(sp):
            with sp.Fori(0, W // U) as i:
                for u in range(U):
                    sp.wait_ge(s_used[u], i + 1)
                    sp.nop(nofuse=True)
                    sp.dma_start(cnt[:, u, :], k.counts[bass.ds(i * U + u, 1), :, :].rearrange("a p c -> (a p) c"))\
                        .then_inc(s_ld[u], 16)

        def scalar(act):
            with act.Fori(0, W // U) as i:
                for u in range(U):
                    act.wait_ge(s_used[u], i + 1)
                    act.nop(nofuse=True)
                    act.copy(st[:, u, :], rows[:, bass.ds(i * U + u, 1), :].rearrange("p a d -> p (a d)"))\
                        .then_inc(s_st[u], 1)
            act.wait_ge(s_all, 1)
            for b, col, n in banks:
                act.copy(sums[:, col:col + n], k.ps[b][:, 0:n]).then_inc(s_cp, 1)

        def vector(v):
            v.memset(zero[:, :], 0.0).then_inc(s_z, 1)
            for b, col, n in banks:
                v.wait_ge(s_tr, b + 1)
                v.tensor_copy(acc[:, b * per:b * per + n // P, :],
                              k.ps[b][:, 0:n].rearrange("p (w d) -> p w d", d=D)).then_inc(s_kept, 1)
            v.wait_ge(s_kept, len(banks))

        def tensor(pe):
            for s in s_used:
                pe.sem_inc(s, 1)
            pe.wait_ge(s_z, 1)
            for b, col, n in banks:
                pe.matmul(k.ps[b][:, 0:n], zero[:, 0:P], zero[:, 0:n], start=True, stop=False)
            with pe.Fori(0, W // U) as i:
                for u in range(U):
                    pe.wait_ge(s_ld[u], i * 16 + 16)
                    pe.wait_ge(s_st[u], i + 1)
                    pe.nop(nofuse=True)
                    for b, col, n in banks:
                        ins = pe.matmul(k.ps[b][:, 0:n], st[:, u, :], cnt[:, u, col:col + n], start=False, stop=False)
                    ins.then_inc(s_used[u], 1)
            for b, col, n in banks:
                ins = pe.matmul(k.ps[b][:, 0:n], zero[:, 0:P], zero[:, 0:n], start=False, stop=True)
            ins.then_inc(s_all, 1)
            for b, col, n in banks:
                pe.wait_ge(s_cp, b + 1)
                for w in range(n // P):
                    ins = pe.transpose(k.ps[b][:, w * P:(w + 1) * P], sums[:, col + w * P:col + (w + 1) * P],
                                       k.ident[:, :])
                ins.then_inc(s_tr, 1)
        in_one_block(k, {"sync": sync, "scalar": scalar, "vector": vector, "tensor": tensor})


@own_semaphores
def layer_filter(k, io):
    nc = k.nc
    with ExitStack() as ctx:
        h = k.sb(ctx, "l0_h", [P, W, D])
        layernorm(k, "ln0", k.x, h)
        scaled = k.sb(ctx, "l0_scaled", [P, W, D])
        acc = k.sb(ctx, "l0_acc", [P, W, D])
        tmp = k.sb(ctx, "l0_degree_tmp", [P, 4, W])
        wide = [P, W, D]
        s_c, s_s = k.sem("l0_clipped"), k.sem("l0_root")
        s_n = k.sem("l0_deg_steps")
        with nc.Block() as block:
            @block.vector
            def _(v):
                v.tensor_scalar(tmp[:, 0, :], k.deg[:, :], 1.0, None, ALU.max).then_inc(s_c, 1)
                v.wait_ge(s_s, 1)
                step = Chain(v, s_n)
                step(v.reciprocal(k.dinv[:, :], tmp[:, 1, :]))
                step(v.tensor_scalar(k.no_edge[:, :], k.deg[:, :], 0.0, None, ALU.is_equal))
                step(v.tensor_scalar(tmp[:, 2, :], k.deg[:, :], 0.0, None, ALU.is_gt))
                step(v.tensor_tensor(k.dinv0[:, :], k.dinv[:, :], tmp[:, 2, :], ALU.mult))
                step(v.reciprocal(k.inv_deg[:, :], tmp[:, 0, :]))

            @block.scalar
            def _(act):
                act.wait_ge(s_c, 1)
                act.activation(tmp[:, 1, :], tmp[:, 0, :], ACT.Sqrt).then_inc(s_s, 1)
        dinv = bc(k.dinv[:, :].unsqueeze(2), wide)

        def first(v, step):
            step(v.scalar_tensor_tensor(k.x[:, :, :], h[:, :, :], THETA[0], k.x[:, :, :], ALU.mult, ALU.add))
            step(v.tensor_tensor(scaled[:, :, :], h[:, :, :], dinv, ALU.mult))
        vector_steps(k, "l0_first", first)
        for r in range(1, len(THETA)):
            count_product(k, f"l0_sum{r}", scaled, acc)

            def update(v, step):
                step(v.tensor_tensor(acc[:, :, :], acc[:, :, :], dinv, ALU.mult))
                step(v.tensor_tensor(h[:, :, :], h[:, :, :], acc[:, :, :], ALU.subtract))
                step(v.scalar_tensor_tensor(k.x[:, :, :], h[:, :, :], THETA[r], k.x[:, :, :], ALU.mult, ALU.add))
                if r + 1 < len(THETA):
                    step(v.tensor_tensor(scaled[:, :, :], h[:, :, :], dinv, ALU.mult))
            vector_steps(k, f"l0_update{r}", update)


@own_semaphores
def layer_gat(k, io):
    nc = k.nc
    wide = [P, W, D]
    SLOPE = 0.2
    AD = 2 * HEADS + 1
    t_src = nc.dram_tensor("l1_by_src", [NP, D + HEADS], F32).ap()
    t_dst = nc.dram_tensor("l1_by_dst", [NP, AD], F32).ap()
    t_h = nc.dram_tensor("l1_h", [NP, D], F32).ap()
    kept = nc.dram_tensor("l1_rows", [T // G, P, G, D], F32).ap()
    with ExitStack() as ctx:
        h = k.sb(ctx, "l1_ln", [P, W, D])
        layernorm(k, "ln1", k.x, h)
        by_src = k.sb(ctx, "l1_src_rows", [P, W, D + HEADS])
        by_dst = k.sb(ctx, "l1_dst_rows", [P, W, AD])
        w = k.sb(ctx, "l1_w", [P, D])
        att = k.sb(ctx, "l1_att", [P, 2, D])
        tmp = k.sb(ctx, "l1_tmp", [P, W, D])
        loads = [(w[:, :], io["L1_gnn_W"]),
                 (att[:, 0, :], io["L1_gnn_att_src"].rearrange("h c -> (h c)").partition_broadcast(P)),
                 (att[:, 1, :], io["L1_gnn_att_dst"].rearrange("h c -> (h c)").partition_broadcast(P))]
        vector_steps(k, "l1_load", lambda v, step: None, loads=loads)
        project(k, "l1_h", h, w[:, :], D, lambda v, n, ps: v.tensor_copy(
            by_src[:, bass.ds(n, 1), 0:D].rearrange("p a d -> p (a d)"), ps))
        heads = lambda ap: ap.rearrange("p w (h c) -> p w h c", c=C)

        def scores(v, step):
            for q, dst in ((0, by_src[:, :, D:D + HEADS]), (1, by_dst[:, :, 0:HEADS])):
                step(v.tensor_tensor(tmp[:, :, :], by_src[:, :, 0:D], bc(att[:, q, :].unsqueeze(1), wide), ALU.mult))
                step(v.tensor_reduce(dst, heads(tmp[:, :, :]), AXX, ALU.add))
            own = by_dst[:, :, HEADS:2 * HEADS]
            step(v.tensor_tensor(own, by_src[:, :, D:D + HEADS], by_dst[:, :, 0:HEADS], ALU.add))
            step(v.scalar_tensor_tensor(own, own, SLOPE, own, ALU.mult, ALU.max))
            step(v.tensor_copy(by_dst[:, :, 2 * HEADS], k.inv_deg[:, :]))
        vector_steps(k, "l1_scores", scores, stores=[(rows_in(t_src), by_src[:, :, :]),
                                                     (rows_in(t_dst), by_dst[:, :, :])])
    with ExitStack() as ctx:
        e = k.sb(ctx, "l1_e", [P, T, HEADS])
        own = k.sb(ctx, "l1_own", [P, T, HEADS + 1])
        top = k.sb(ctx, "l1_top", [P, T, HEADS])
        s_c = k.sem("l1_own_copied")

        def consume(v, n, a, b):
            at = bass.ds(n * G, G)
            v.tensor_copy(own[:, at, :], b[:, :, HEADS:AD]).then_inc(s_c, 1)
            return v.tensor_tensor(e[:, at, :], a[:, :, D:D + HEADS], b[:, :, 0:HEADS], ALU.add)
        edge_rows(k, "l1_edges", t_src, D + HEADS, t_dst, AD, consume, keep_rows=kept)

        def leaky(v, step):
            step(v.scalar_tensor_tensor(e[:, :, :], e[:, :, :], SLOPE, e[:, :, :], ALU.mult, ALU.max))
            step(v.tensor_tensor(top[:, :, :], e[:, :, :], own[:, :, 0:HEADS], ALU.max))
        vector_steps(k, "l1_leaky", leaky)
        segment_max(k, "l1_max", top[:, :, :])
        s_a, s_b, s_c2 = k.sem("l1_less_top"), k.sem("l1_exp"), k.sem("l1_own_shared")
        with nc.Block() as block:
            @block.vector
            def _(v):
                v.tensor_tensor(e[:, :, :], e[:, :, :], top[:, :, :], ALU.subtract).then_inc(s_a, 1)
                v.tensor_tensor(own[:, :, 0:HEADS], own[:, :, 0:HEADS], top[:, :, :], ALU.subtract).then_inc(s_a, 1)
                v.wait_ge(s_b, 2)
                v.tensor_tensor(top[:, :, :], own[:, :, 0:HEADS], bc(own[:, :, HEADS:HEADS + 1], [P, T, HEADS]),
                                ALU.mult).then_inc(s_c2, 1)

            @block.scalar
            def _(act):
                act.wait_ge(s_a, 1)
                act.activation(e[:, :, :], e[:, :, :], ACT.Exp).then_inc(s_b, 1)
                act.wait_ge(s_a, 2)
                act.activation(own[:, :, 0:HEADS], own[:, :, 0:HEADS], ACT.Exp).then_inc(s_b, 1)
        acc = k.sb(ctx, "l1_acc", [P, W * (D + 2 * HEADS)])
        window_sums(k, "l1_sum", acc[:, :], k.loc, k.win_i, D + 2 * HEADS, stream=kept,
                    shares=(e[:, :, :], top[:, :, :]))
        acc_v = acc[:, :].rearrange("p (w d) -> p w d", d=D + 2 * HEADS)
        h2 = k.sb(ctx, "l1_h_back", [P, W, D])
        bias = k.sb(ctx, "l1_bias", [P, D])

        def finish(v, step):
            msg, den, loop = acc_v[:, :, 0:D], acc_v[:, :, D:D + HEADS], acc_v[:, :, D + HEADS:]
            per_head = lambda ap: bc(ap.unsqueeze(3), [P, W, HEADS, C])
            step(v.tensor_tensor(loop, loop, bc(k.no_edge[:, :].unsqueeze(2), [P, W, HEADS]), ALU.add))
            step(v.tensor_tensor(den, den, loop, ALU.add))
            step(v.reciprocal(den, den))
            step(v.tensor_tensor(heads(h2[:, :, :]), heads(h2[:, :, :]), per_head(loop), ALU.mult))
            step(v.tensor_tensor(h2[:, :, :], h2[:, :, :], msg, ALU.add))
            step(v.tensor_tensor(heads(h2[:, :, :]), heads(h2[:, :, :]), per_head(den), ALU.mult))
            step(v.tensor_tensor(h2[:, :, :], h2[:, :, :], bc(bias[:, :].unsqueeze(1), wide), ALU.add))
            step(v.tensor_tensor(k.x[:, :, :], k.x[:, :, :], h2[:, :, :], ALU.add))
        vector_steps(k, "l1_finish", finish, loads=[(h2[:, :, :], rows_in(t_src)[:, :, 0:D]),
                                                    (bias[:, :], io["L1_gnn_bias"].partition_broadcast(P))])


@own_semaphores
def layer_relational(k, io):
    nc = k.nc
    wide = [P, W, D]
    SLOPE = 0.01
    table = nc.dram_tensor("l2_table", [NP, TYPES * D], F32).ap()
    with ExitStack() as ctx:
        index = k.sb(ctx, "l2_index", [P, T], I32)
        loc = k.sb(ctx, "l2_loc", [P, T + G])
        wgt = k.sb(ctx, "l2_weight", [P, T + G])
        win_i = k.sb(ctx, "l2_win_i", [1, T], I32)
        read_list(k, "read_src", k.list_src, RS, index, loc, wgt, k.win_src, win_i)
        z = k.sb(ctx, "l2_z", [P, W, D])
        total = k.sb(ctx, "l2_total", [P, W, D])
        acc = k.sb(ctx, "l2_acc", [P, W * D])
        rows = k.sb(ctx, "l2_rows", [P, W, TYPES * D])
        w = k.sb(ctx, "l2_w", [P, TYPES, D])
        bias = k.sb(ctx, "l2_bias", [P, D])
        layernorm(k, "ln2", k.x, z)
        vector_steps(k, "l2_start", lambda v, step: step(v.tensor_copy(total[:, :, :], z[:, :, :])))
        dinv = bc(k.dinv0[:, :].unsqueeze(2), wide)
        acc_v = acc[:, :].rearrange("p (w d) -> p w d", d=D)
        for r in range(3):
            vector_steps(k, f"l2_load{r}", lambda v, step: None,
                         loads=[(w[:, :, :], io[f"L2_gnn_W{r + 1}"].rearrange("t i o -> i t o")),
                                (bias[:, :], io[f"L2_gnn_b{r + 1}"].partition_broadcast(P))])
            project(k, f"l2_xw{r}", z, w[:, :, :].rearrange("p t o -> p (t o)"), TYPES * D,
                    lambda v, n, ps: v.tensor_scalar(rows[:, bass.ds(n, 1), :].rearrange("p a d -> p (a d)"), ps,
                                                     k.dinv0[:, bass.ds(n, 1)], None, ALU.mult))
            vector_steps(k, f"l2_store{r}", lambda v, step: step(v.memset(acc[:, 0:1], 0.0)),
                         stores=[(rows_in(table), rows[:, :, :])])
            window_sums(k, f"l2_sum{r}", acc[:, :], loc, win_i, D,
                        table=table.rearrange("n (t o) -> (n t) o", t=TYPES), index=index, weight=wgt)

            def update(v, step):
                step(v.tensor_tensor(z[:, :, :], acc_v, dinv, ALU.mult))
                step(v.tensor_tensor(z[:, :, :], z[:, :, :], bc(bias[:, :].unsqueeze(1), wide), ALU.add))
                step(v.scalar_tensor_tensor(z[:, :, :], z[:, :, :], SLOPE, z[:, :, :], ALU.mult, ALU.max))
                step(v.tensor_tensor(total[:, :, :], total[:, :, :], z[:, :, :], ALU.add))
                if r == 2:
                    step(v.scalar_tensor_tensor(k.x[:, :, :], total[:, :, :], 0.25, k.x[:, :, :],
                                                ALU.mult, ALU.add))
            vector_steps(k, f"l2_update{r}", update)


@own_semaphores
def layer_attention(k, io, out):
    nc = k.nc
    wide = [P, W, D]
    HC = 32
    t_q = nc.dram_tensor("l3_q", [NP, D], F32).ap()
    t_k = nc.dram_tensor("l3_k", [NP, D + HEADS], F32).ap()
    with ExitStack() as outer:
        h = k.sb(outer, "l3_h", [P, W, D])
        val = k.sb(outer, "l3_v", [P, W, D])
        wo = k.sb(outer, "l3_wo", [P, D])
        vecs = k.sb(outer, "l3_vecs", [P, 3, D])
        layernorm(k, "ln3", k.x, h)
        with ExitStack() as ctx:
            wqkv = k.sb(ctx, "l3_wqkv", [P, 3, D])
            b = k.sb(ctx, "l3_bqkv", [P, 3 * D])
            qkv = k.sb(ctx, "l3_qkv", [P, W, 3 * D])
            krow = k.sb(ctx, "l3_k_rows", [P, W, D + HEADS])
            wc1 = k.sb(ctx, "l3_wc1", [P, 3, HC])
            wc2 = k.sb(ctx, "l3_wc2", [P, HC, HEADS])
            bc2 = k.sb(ctx, "l3_bc2", [P, HEADS])
            nv = k.sb(ctx, "l3_node_vec", [P, W, 1])
            hid = k.sb(ctx, "l3_cons_hidden", [P, HC, W])
            con = k.sb(ctx, "l3_cons", [P, HEADS, W])
            full = N // P
            s_z = k.sem("l3_node_vec_cleared")
            with nc.Block() as block:
                @block.vector
                def _(v):
                    v.memset(nv[:, :, :], 0.0).then_inc(s_z, 1)
                    v.wait_ge(s_z, 1)
            flat = lambda name: io[name].rearrange("a b -> (a b)").partition_broadcast(P)
            vec = lambda name: io[name].partition_broadcast(P)
            loads = [(wqkv[:, n, :], io[f"L3_gnn_W{c}"]) for n, c in enumerate("qkv")]
            loads += [(b[:, n * D:(n + 1) * D], vec(f"L3_gnn_b{c}")) for n, c in enumerate("qkv")]
            loads += [(wo[:, :], io["L3_gnn_Wo"]), (vecs[:, 0, :], vec("L3_gnn_bo")),
                      (vecs[:, 1, :], vec("L3_gnn_gamma")), (vecs[:, 2, :], vec("L3_gnn_beta")),
                      (wc1[:, 0, :], flat("L3_gnn_Wc1")), (wc1[:, 1, :], vec("L3_gnn_bc1")),
                      (wc2[:, :, :].rearrange("p a b -> p (a b)"), flat("L3_gnn_Wc2")), (bc2[:, :], vec("L3_gnn_bc2")),
                      (nv[:, 0:full, :], rows_in(io["node_vec1"][0:full * P, :])),
                      (nv[0:N - full * P, full, :], io["node_vec1"][full * P:N, :])]

            def cons(v, step):
                for j in range(HC):
                    step(v.tensor_scalar(hid[:, j, :], nv[:, :, 0], wc1[:, 0, j:j + 1], wc1[:, 1, j:j + 1],
                                         ALU.mult, ALU.add))
                step(v.tensor_scalar(hid[:, :, :], hid[:, :, :], 0.0, None, ALU.max))
                for hd in range(HEADS):
                    step(v.tensor_copy(con[:, hd, :], bc(bc2[:, hd:hd + 1], [P, W])))
                    for j in range(HC):
                        step(v.scalar_tensor_tensor(con[:, hd, :], hid[:, j, :], wc2[:, j, hd:hd + 1],
                                                    con[:, hd, :], ALU.mult, ALU.add))
            with nc.allow_non_contiguous_dma(reason="one number for each node, once"):
                vector_steps(k, "l3_cons", cons, loads=loads)
            s_sig = k.sem("l3_sigmoid")
            with nc.Block() as block:
                @block.scalar
                def _(act):
                    act.activation(con[:, :, :], con[:, :, :], ACT.Sigmoid).then_inc(s_sig, 1)
                    act.wait_ge(s_sig, 1)
            project(k, "l3_qkv", h, wqkv[:, :, :].rearrange("p t o -> p (t o)"), 3 * D,
                    lambda v, n, ps: v.tensor_tensor(qkv[:, bass.ds(n, 1), :].rearrange("p a d -> p (a d)"),
                                                     ps, b[:, :], ALU.add))

            def rows(v, step):
                step(v.tensor_copy(val[:, :, :], qkv[:, :, 2 * D:3 * D]))
                step(v.tensor_copy(krow[:, :, 0:D], qkv[:, :, D:2 * D]))
                step(v.tensor_copy(krow[:, :, D:D + HEADS], con[:, :, :].rearrange("p h w -> p w h")))
            vector_steps(k, "l3_rows", rows, stores=[(rows_in(t_q), qkv[:, :, 0:D]), (rows_in(t_k), krow[:, :, :])])
        with ExitStack() as ctx:
            s = k.sb(ctx, "l3_scores", [P, T, HEADS])
            cns = k.sb(ctx, "l3_cons_slots", [P, T, HEADS])
            s_p, s_c = k.sem("l3_products"), k.sem("l3_cons_copied")

            def consume(v, n, a, b):
                at = bass.ds(n * G, G)
                v.tensor_copy(cns[:, at, :], b[:, :, D:D + HEADS]).then_inc(s_c, 1)
                v.tensor_tensor(a, a, b[:, :, 0:D], ALU.mult).then_inc(s_p, 1)
                v.wait_ge(s_p, n + 1)
                return v.tensor_reduce(s[:, at, :], a.rearrange("p g (h c) -> p g h c", c=C),
                                       AXX, ALU.add)
            edge_rows(k, "l3_edges", t_q, D, t_k, D + HEADS, consume)
            with ExitStack() as inner:
                terms = k.sb(inner, "l3_terms", [P, T, 2 * HEADS])

                def score(v, step):
                    step(v.scalar_tensor_tensor(s[:, :, :], s[:, :, :], float(C) ** -0.5, terms[:, :, 0:HEADS],
                                                ALU.mult, ALU.add))
                    step(v.tensor_tensor(s[:, :, :], s[:, :, :], cns[:, :, :], ALU.mult))
                    step(v.tensor_tensor(s[:, :, :], s[:, :, :], terms[:, :, HEADS:], ALU.add))
                    step(v.tensor_copy(cns[:, :, :], s[:, :, :]))
                vector_steps(k, "l3_score", score,
                             loads=[(terms[:, :, :], k.list_dst.rearrange("(t p) r -> p t r", p=P)[:, :, 2:RD])])
            segment_max(k, "l3_max", cns[:, :, :])
            s_a, s_b = k.sem("l3_less_top"), k.sem("l3_exp")
            with nc.Block() as block:
                @block.vector
                def _(v):
                    v.tensor_tensor(s[:, :, :], s[:, :, :], cns[:, :, :], ALU.subtract).then_inc(s_a, 1)

                @block.scalar
                def _(act):
                    act.wait_ge(s_a, 1)
                    act.activation(s[:, :, :], s[:, :, :], ACT.Exp).then_inc(s_b, 1)
                    act.wait_ge(s_b, 1)
            acc = k.sb(ctx, "l3_acc", [P, W * HEADS])
            window_sums(k, "l3_sum", acc[:, :], k.loc, k.win_i, HEADS, values=s)
            acc_v = acc[:, :].rearrange("p (w h) -> p w h", h=HEADS)
            inv = k.sb(ctx, "l3_inv", [P, W, HEADS])

            def weigh(v, step):
                step(v.tensor_tensor(inv[:, :, :], acc_v, bc(k.no_edge[:, :].unsqueeze(2), [P, W, HEADS]), ALU.add))
                step(v.reciprocal(inv[:, :, :], inv[:, :, :]))
                step(v.tensor_tensor(inv[:, :, :], inv[:, :, :], acc_v, ALU.mult))
                heads = val[:, :, :].rearrange("p w (h c) -> p w h c", c=C)
                step(v.tensor_tensor(heads, heads, bc(inv[:, :, :].unsqueeze(3), [P, W, HEADS, C]), ALU.mult))
            vector_steps(k, "l3_weigh", weigh)
        y = k.sb(outer, "l3_y", [P, W, D])
        project(k, "l3_out", val, wo[:, :], D,
                lambda v, n, ps: v.tensor_tensor(y[:, bass.ds(n, 1), :].rearrange("p a d -> p (a d)"), ps,
                                                 vecs[:, 0, :], ALU.add))
        vector_steps(k, "l3_residual", lambda v, step: step(v.tensor_tensor(y[:, :, :], y[:, :, :], h[:, :, :],
                                                                             ALU.add)))
        layernorm(k, "ln4", y, h, relu=False, gamma=vecs[:, 1, :], beta=vecs[:, 2, :])
        full = N // P
        vector_steps(k, "l3_finish",
                     lambda v, step: step(v.tensor_tensor(k.x[:, :, :], k.x[:, :, :], h[:, :, :], ALU.add)),
                     stores=[(rows_in(out[0:full * P, :]), k.x[:, 0:full, :]),
                             (out[full * P:N, :], k.x[0:N - full * P, full, :])])


def program(nc, io, out):
    with ExitStack() as ctx:
        k = Core(nc)
        k.moved = [ctx.enter_context(nc.semaphore(f"moved_by_pool{h}")) for h in range(2)]
        k.ps = [ctx.enter_context(nc.psum_tensor(f"bank{b}", [P, 512], F32)) for b in range(8)]
        k.x = k.sb(ctx, "x_sb", [P, W, D])
        k.iota = k.sb(ctx, "iota", [P, P])
        k.tile_no = k.sb(ctx, "tile_no", [P, T])
        k.pid = k.sb(ctx, "pid", [P, 1])
        k.ones = k.sb(ctx, "ones", [P, P])
        k.eps = k.sb(ctx, "eps", [P, 1])
        k.ident = k.sb(ctx, "ident", [P, P])
        k.before = k.sb(ctx, "before", [P, P])
        k.win_dst = k.sb(ctx, "win_dst", [P, T])
        k.win_src = k.sb(ctx, "win_src", [P, T])
        k.src_i = k.sb(ctx, "src_i", [P, T], I32)
        k.dst_i = k.sb(ctx, "dst_i", [P, T], I32)
        k.dst_f = k.sb(ctx, "dst_f", [P, T])
        k.loc = k.sb(ctx, "loc", [P, T + G])
        k.win_i = k.sb(ctx, "win_dst_i", [1, T], I32)
        k.deg, k.dinv, k.dinv0, k.inv_deg, k.no_edge = (
            k.sb(ctx, name, [P, W]) for name in ("deg", "dinv", "dinv0", "inv_deg", "no_edge"))
        list_a = nc.dram_tensor("half_sorted", [E, RD], F32)
        k.list_a = list_a.ap()
        k.list_dst = nc.dram_tensor("by_dst", [SLOTS, RD], F32).ap()
        k.list_src = nc.dram_tensor("by_src", [SLOTS, RS], F32).ap()
        setup(k, io)
        fill_pads(k, "dst", k.list_dst, RD, 1)
        fill_pads(k, "src", k.list_src, RS, 1)
        k.counts = nc.dram_tensor("counts", [W, P, NP], F32).ap()
        k.bounds_src = k.sb(ctx, "bounds_src", [1, W + 1], I32)
        sort_both(k, io)
        read_list(k, "read_dst", k.list_dst, RD, k.src_i, k.loc, None, k.win_dst, k.win_i)
        vector_steps(k, "dst_index", lambda v, step: (
            step(v.scalar_tensor_tensor(k.dst_f[:, :], k.win_dst[:, :], float(P), k.loc[:, 0:T], ALU.mult, ALU.add)),
            step(v.tensor_scalar(k.dst_i[:, :], k.dst_f[:, :], 0.0, None, ALU.max))))
        layer_filter(k, io)
        layer_gat(k, io)
        layer_relational(k, io)
        layer_attention(k, io, out)


_INS = ['x', 'src', 'dst', 'edge_attr_64', 'edge_type_4', 'edge_weight', 'edge_weight1', 'node_vec1',
        'L1_gnn_W', 'L1_gnn_att_src', 'L1_gnn_att_dst', 'L1_gnn_bias',
        'L2_gnn_W1', 'L2_gnn_b1', 'L2_gnn_W2', 'L2_gnn_b2', 'L2_gnn_W3', 'L2_gnn_b3',
        'L3_gnn_Wq', 'L3_gnn_bq', 'L3_gnn_Wk', 'L3_gnn_bk', 'L3_gnn_Wv', 'L3_gnn_bv', 'L3_gnn_We', 'L3_gnn_be',
        'L3_gnn_Wc1', 'L3_gnn_bc1', 'L3_gnn_Wc2', 'L3_gnn_bc2', 'L3_gnn_Wd1', 'L3_gnn_bd1', 'L3_gnn_Wd2',
        'L3_gnn_bd2', 'L3_gnn_Wo', 'L3_gnn_bo', 'L3_gnn_gamma', 'L3_gnn_beta']


def kernel(**inputs):
    import numpy as _np
    import concourse.bacc as _bacc
    from concourse import mybir as _mybir
    from concourse.bass_utils import run_bass_kernel_spmd as _run

    nc = _bacc.Bacc("TRN2", target_bir_lowering=False, num_devices=1)
    arrays, io = {}, {}
    for name in _INS:
        a = _np.ascontiguousarray(inputs[name])
        arrays[f"in_{name}"] = a
        io[name] = nc.dram_tensor(f"in_{name}", a.shape, _mybir.dt.from_np(a.dtype), kind="ExternalInput").ap()
    out = nc.dram_tensor("out_x", (N, D), F32, kind="ExternalOutput").ap()
    program(nc, io, out)
    r = _run(nc, [arrays], core_ids=[0])
    return r.results[0]["out_x"]
```

```python
import concourse.bass as bass
from concourse import mybir
from contextlib import ExitStack

F32 = mybir.dt.float32
I32 = mybir.dt.int32
BF16 = mybir.dt.bfloat16
ALU = mybir.AluOpType
ACT = mybir.ActivationFunctionType
AXX = mybir.AxisListType.X

P = 128
N = 3125
D = 128
W = -(-N // P)
NP = W * P
E = 100000
SB = 8
EP = max(p for p in range(1, P + 1) if E % (p * SB * 4) == 0)
EC = E // EP
HEADS = 8
C = D // HEADS
CH = 16
TILES_MIN = -(-E // P) + W
G = 4
R = 4
PSUM_BANK = 512
TG = -(-TILES_MIN // CH)
while (TG * CH) % (R * G) or TG % 3:
    TG += 1
T = TG * CH
SLOTS = T * P
L = TG * P
RD = 18
RS = 4
TYPES = 4
SPENT = 30
BIG = 1e38
EPS = 1e-5
THETA = (0.5, 0.3, 0.2, 0.1)


class Chain:

    def __init__(self, engine, sem):
        self.engine, self.sem, self.n = engine, sem, 0

    def __call__(self, instruction):
        instruction.then_inc(self.sem, 1)
        self.n += 1
        self.engine.wait_ge(self.sem, self.n)


class Core:

    def __init__(self, nc):
        self.nc, self.held, self.spent = nc, [], []

    def sb(self, ctx, name, shape, dt=F32):
        return ctx.enter_context(self.nc.sbuf_tensor(name, shape, dt))

    def sem(self, name):
        handle = self.nc.alloc_semaphore(name=name)
        self.held[-1].append(handle)
        return handle

    def pool_dma_sems(self, name, places=R):
        return [self.nc.alloc_semaphore(name=f"{name}{h}") for h in range(places)]


def own_semaphores(stage):
    def run(k, *args, **kwargs):
        k.held.append([])
        stage(k, *args, **kwargs)
        k.spent += k.held.pop()
        if len(k.spent) >= SPENT:
            with k.nc.Block() as block:
                @block.gpsimd
                def _(pool):
                    for handle in k.spent:
                        pool.sem_clear(handle)
            for handle in k.spent:
                k.nc.release_semaphore(handle)
            k.spent = []
    return run


def in_one_block(k, *stages):
    with k.nc.Block() as block:
        engines = {"sync": block.sync, "gpsimd": block.gpsimd, "vector": block.vector,
                   "scalar": block.scalar, "tensor": block.tensor}
        for name in engines:
            bodies = [stage[name] for stage in stages if name in stage]
            if bodies:
                @engines[name]
                def _(engine):
                    for body in bodies:
                        body(engine)


def bc(ap, shape):
    return ap.to_broadcast(shape)


def windows_of(packed):
    return [packed // W ** g % W for g in range(G - 1)] + [packed // W ** (G - 1)]


def rows_in(ap):
    return ap.rearrange("(w p) c -> p w c", p=P)


def by_edge(ap):
    return ap.rearrange("(p e) -> p e", e=EC)


@own_semaphores
def setup(k, io):
    nc = k.nc
    s_load, s_io, s_v = k.sem("x_loaded"), k.sem("iotas_made"), k.sem("setup_steps")
    s_id, s_ones = k.sem("identity_made"), k.sem("ones_made")
    with nc.Block() as block:
        @block.sync
        def _(sp):
            full = N // P
            sp.wait_ge(s_v, 1)
            sp.dma_start(k.x[:, 0:full, :], rows_in(io["x"][0:full * P, :])).then_inc(s_load, 16)
            sp.dma_start(k.x[0:N - full * P, full, :], io["x"][full * P:N, :]).then_inc(s_load, 16)
            sp.wait_ge(s_load, 32)

        @block.gpsimd
        def _(pool):
            pool.iota(k.iota[:, :], [[1, P]], base=0, channel_multiplier=0,
                      allow_small_or_imprecise_dtypes=True).then_inc(s_io, 1)
            pool.iota(k.tile_no[:, :], [[1, T]], base=0, channel_multiplier=0,
                      allow_small_or_imprecise_dtypes=True).then_inc(s_io, 1)
            pool.iota(k.pid[:, :], [[1, 1]], base=0, channel_multiplier=1,
                      allow_small_or_imprecise_dtypes=True).then_inc(s_io, 1)

        @block.vector
        def _(v):
            v.memset(k.x[:, :, :], 0.0).then_inc(s_v, 1)
            v.memset(k.ones[:, :], 1.0).then_inc(s_ones, 1)
            v.memset(k.eps[:, :], EPS).then_inc(s_ones, 1)
            v.wait_ge(s_io, 3)
            v.tensor_scalar(k.ident[:, :], k.iota[:, :], k.pid[:, 0:1], None, ALU.is_equal).then_inc(s_id, 1)
            v.tensor_scalar(k.before[:, :], k.iota[:, :], k.pid[:, 0:1], None, ALU.is_gt).then_inc(s_id, 1)
            v.wait_ge(s_id, 2)
            v.tensor_copy(k.ident16[:, :], k.ident[:, :]).then_inc(s_id, 1)
            v.wait_ge(s_id, 3)
            v.wait_ge(s_ones, 2)


@own_semaphores
def layernorm(k, tag, src, dst, relu=True, gamma=None, beta=None):
    nc = k.nc
    with ExitStack() as ctx:
        stat = k.sb(ctx, f"{tag}_stat", [P, 4, W])
        sq = k.sb(ctx, f"{tag}_sq", [P, W, D])
        s_v, s_var, s_std = k.sem(f"{tag}_v"), k.sem(f"{tag}_var"), k.sem(f"{tag}_std")
        wide = [P, W, D]
        with nc.Block() as block:
            @block.vector
            def _(v):
                step = Chain(v, s_v)
                step(v.tensor_reduce(stat[:, 0, :], src[:, :, :], AXX, ALU.add))
                step(v.tensor_scalar(stat[:, 1, :], stat[:, 0, :], 1.0 / D, None, ALU.mult))
                step(v.tensor_tensor(dst[:, :, :], src[:, :, :],
                                     bc(stat[:, 1, :].unsqueeze(2), wide), ALU.subtract))
                step(v.tensor_tensor(sq[:, :, :], dst[:, :, :], dst[:, :, :], ALU.mult))
                v.tensor_reduce(stat[:, 2, :], sq[:, :, :], AXX, ALU.add).then_inc(s_var, 1)
                v.wait_ge(s_std, 1)
                step(v.reciprocal(stat[:, 0, :], stat[:, 3, :]))
                step(v.tensor_tensor(dst[:, :, :], dst[:, :, :],
                                     bc(stat[:, 0, :].unsqueeze(2), wide), ALU.mult))
                if relu:
                    step(v.tensor_scalar(dst[:, :, :], dst[:, :, :], 0.0, None, ALU.max))
                if gamma is not None:
                    step(v.tensor_tensor(dst[:, :, :], dst[:, :, :],
                                         bc(gamma[:, :].unsqueeze(1), wide), ALU.mult))
                    step(v.tensor_tensor(dst[:, :, :], dst[:, :, :],
                                         bc(beta[:, :].unsqueeze(1), wide), ALU.add))

            @block.scalar
            def _(act):
                act.wait_ge(s_var, 1)
                act.activation(stat[:, 3, :], stat[:, 2, :], ACT.Sqrt, bias=k.eps[:, 0:1],
                               scale=1.0 / D).then_inc(s_std, 1)


def edge_terms(k, io, ctx, rec):
    A = 64
    H1 = 16
    pairs = SB // 2
    attr = k.sb(ctx, "attr", [EP, 2, SB, A])
    attr_t = k.sb(ctx, "attr_t", [P, 2, pairs, EP])
    we2 = k.sb(ctx, "we_twice", [P, 2, HEADS])
    be = k.sb(ctx, "be_all", [P, HEADS])
    wd1 = k.sb(ctx, "wd1_all", [P, H1])
    bd1 = k.sb(ctx, "bd1_all", [P, H1])
    wd2 = k.sb(ctx, "wd2_all", [P, H1 * HEADS])
    bd2 = k.sb(ctx, "bd2_all", [P, HEADS])
    dist = k.sb(ctx, "dist", [EP, EC])
    hid = k.sb(ctx, "dist_hidden", [EP, 2, EC])
    dterm = k.sb(ctx, "dist_term", [EP, HEADS, EC])
    s_we0, s_w = k.sem("we_cleared"), k.sem("edge_weights_loaded")
    two = lambda name: [k.sem(f"{name}0"), k.sem(f"{name}1")]
    s_at, s_tr, s_cp, s_mm, s_ev = map(two, ("attr_loaded", "attr_transposed", "attr_t_copied",
                                             "attr_terms_done", "attr_terms_kept"))
    s_h, s_ac = k.sem("hidden_ready"), k.sem("dist_steps")
    loads = 8
    def vector(v):
        v.memset(we2[:, :, :], 0.0).then_inc(s_we0, 1)
        v.wait_ge(s_w, 16 * loads)
        with v.Fori(0, EC // SB // 2) as i:
            for half in range(2):
                v.wait_ge(s_tr[half], i + 2)
                v.nop(nofuse=True)
                v.tensor_copy(attr_t[:, half, :, :],
                              k.ps[2 * half][:, 0:pairs * EP].rearrange("p (a b) -> p a b", b=EP))\
                    .then_inc(s_cp[half], 1)
                v.wait_ge(s_mm[half], i + 1)
                v.nop(nofuse=True)
                v.tensor_tensor(rec[:, bass.ds((i * 2 + half) * SB, SB), 2:10],
                                k.ps[2 * half + 1][0:EP, 0:SB * HEADS].rearrange("p (e h) -> p e h", h=HEADS),
                                bc(be[0:EP, :].unsqueeze(1), [EP, SB, HEADS]), ALU.add)\
                    .then_inc(s_ev[half], 1)
        for h in range(HEADS):
            v.tensor_copy(dterm[:, h, :], bc(bd2[0:EP, h:h + 1], [EP, EC])).then_inc(s_ac, 1)
        done = HEADS
        for j in range(H1):
            if j >= 2:
                v.wait_ge(s_ac, HEADS * j)
            v.tensor_scalar(hid[:, j % 2, :], dist[:, :], wd1[0:EP, j:j + 1], bd1[0:EP, j:j + 1],
                            ALU.mult, ALU.add).then_inc(s_h, 1)
            v.wait_ge(s_h, j * 2 + 1)
            v.tensor_scalar(hid[:, j % 2, :], hid[:, j % 2, :], 0.0, None, ALU.max).then_inc(s_h, 1)
            v.wait_ge(s_h, j * 2 + 2)
            for h in range(HEADS):
                v.wait_ge(s_ac, done - HEADS + 1)
                v.scalar_tensor_tensor(dterm[:, h, :], hid[:, j % 2, :],
                                       wd2[0:EP, j * HEADS + h:j * HEADS + h + 1],
                                       dterm[:, h, :], ALU.mult, ALU.add).then_inc(s_ac, 1)
                done += 1
        v.wait_ge(s_ac, done)
        v.tensor_copy(rec[:, :, 10:18], dterm[:, :, :].rearrange("p h e -> p e h")).then_inc(s_ac, 1)

    def tensor(pe):
        for s in s_tr + s_ev:
            pe.sem_inc(s, 1)
        pe.wait_ge(s_w, 16 * loads)
        with pe.Fori(0, EC // SB // 2) as i:
            for half in range(2):
                pe.wait_ge(s_at[half], i * 16 + 16)
                pe.wait_ge(s_ev[half], i + 1)
                pe.nop(nofuse=True)
                for a in range(pairs):
                    ins = pe.transpose(k.ps[2 * half][:, a * EP:(a + 1) * EP],
                                       attr[:, half, 2 * a:2 * a + 2, :].rearrange("p a b -> p (a b)"),
                                       k.ident[0:EP, 0:EP])
                ins.then_inc(s_tr[half], 1)
            for half in range(2):
                pe.wait_ge(s_cp[half], i + 1)
                pe.nop(nofuse=True)
                for a in range(pairs):
                    ins = pe.matmul(k.ps[2 * half + 1][0:EP, a * 16:(a + 1) * 16],
                                    attr_t[:, half, a, :],
                                    we2[:, :, :].rearrange("p a b -> p (a b)"), start=True, stop=True)
                ins.then_inc(s_mm[half], 1)

    def sync(sp):
        sp.wait_ge(s_we0, 1)
        sp.dma_start(we2[0:A, 0, :], io["L3_gnn_We"]).then_inc(s_w, 16)
        sp.dma_start(we2[A:2 * A, 1, :], io["L3_gnn_We"]).then_inc(s_w, 16)
        for dst, name in ((be, "L3_gnn_be"), (bd1, "L3_gnn_bd1"), (bd2, "L3_gnn_bd2")):
            sp.dma_start(dst[:, :], io[name].partition_broadcast(P)).then_inc(s_w, 16)
        sp.dma_start(wd1[:, :], io["L3_gnn_Wd1"].rearrange("a b -> (a b)").partition_broadcast(P))\
            .then_inc(s_w, 16)
        sp.dma_start(wd2[:, :], io["L3_gnn_Wd2"].rearrange("a b -> (a b)").partition_broadcast(P))\
            .then_inc(s_w, 16)
        sp.dma_start(dist[:, :], by_edge(io["edge_weight1"].rearrange("e a -> (e a)"))).then_inc(s_w, 16)
        a_v = io["edge_attr_64"].rearrange("(p e) a -> p e a", e=EC)
        with sp.Fori(0, EC // SB // 2) as i:
            for half in range(2):
                sp.wait_ge(s_tr[half], i + 1)
                sp.nop(nofuse=True)
                sp.dma_start(attr[:, half, :, :], a_v[:, bass.ds((i * 2 + half) * SB, SB), :])\
                    .then_inc(s_at[half], 16)
    return {"vector": vector, "tensor": tensor, "sync": sync}


def conservation(k, io, ctx):
    HC = 32
    wc1 = k.sb(ctx, "cons_wc1", [P, 2, HC])
    wc2 = k.sb(ctx, "cons_wc2", [P, HC, HEADS])
    bc2 = k.sb(ctx, "cons_bc2", [P, HEADS])
    nv = k.sb(ctx, "cons_node_vec", [P, W, 1])
    hid = k.sb(ctx, "cons_hidden", [P, HC, W])
    s_z, s_ld, s_v, s_lin, s_sig = (k.sem("cons_cleared"), k.sem("cons_loaded"), k.sem("cons_v"),
                                    k.sem("cons_linear"), k.sem("cons_made"))
    full = N // P
    flat = lambda name: io[name].rearrange("a b -> (a b)").partition_broadcast(P)
    loads = [(wc1[:, 0, :], flat("L3_gnn_Wc1")), (wc1[:, 1, :], io["L3_gnn_bc1"].partition_broadcast(P)),
             (wc2[:, :, :].rearrange("p a b -> p (a b)"), flat("L3_gnn_Wc2")),
             (bc2[:, :], io["L3_gnn_bc2"].partition_broadcast(P)),
             (nv[:, 0:full, :], rows_in(io["node_vec1"][0:full * P, :])),
             (nv[0:N - full * P, full, :], io["node_vec1"][full * P:N, :])]

    def sync(sp):
        sp.wait_ge(s_z, 1)
        with k.nc.allow_non_contiguous_dma(reason="one number for each node, once"):
            for dst, src in loads:
                sp.dma_start(dst, src).then_inc(s_ld, 16)

    def vector(v):
        v.memset(nv[:, :, :], 0.0).then_inc(s_z, 1)
        v.wait_ge(s_ld, 16 * len(loads))
        step = Chain(v, s_v)
        wide = [P, HC, W]
        step(v.tensor_tensor(hid[:, :, :], bc(nv[:, :, 0].unsqueeze(1), wide), bc(wc1[:, 0, :].unsqueeze(2), wide),
                             ALU.mult))
        step(v.tensor_tensor(hid[:, :, :], hid[:, :, :], bc(wc1[:, 1, :].unsqueeze(2), wide), ALU.add))
        step(v.tensor_scalar(hid[:, :, :], hid[:, :, :], 0.0, None, ALU.max))
        step(v.tensor_copy(k.cons[:, :, :], bc(bc2[:, :].unsqueeze(2), [P, HEADS, W])))
        for j in range(HC):
            for hd in range(HEADS):
                if j > 0:
                    v.wait_ge(s_v, 4 + (j - 1) * HEADS + hd + 1)
                v.scalar_tensor_tensor(k.cons[:, hd, :], hid[:, j, :], wc2[:, j, hd:hd + 1], k.cons[:, hd, :],
                                       ALU.mult, ALU.add).then_inc(s_v, 1)
        v.wait_ge(s_v, 4 + HC * HEADS)
        v.nop(nofuse=True).then_inc(s_lin, 1)

    def scalar(act):
        act.wait_ge(s_lin, 1)
        act.activation(k.cons[:, :, :], k.cons[:, :, :], ACT.Sigmoid).then_inc(s_sig, 1)
        act.wait_ge(s_sig, 1)
    return {"sync": sync, "vector": vector, "scalar": scalar}


def places(k, tag, ctx, key, buckets, pos, whole_tiles, win=None, bounds=None, bank=0):
    hit = k.sb(ctx, f"{tag}_hit", [EP, EC])
    rank = k.sb(ctx, f"{tag}_rank", [EP, EC])
    one = k.sb(ctx, f"{tag}_one", [EP, EC])
    posf = k.sb(ctx, f"{tag}_posf", [EP, EC])
    where = k.sb(ctx, f"{tag}_where", [EP, EC], I32)
    count = k.sb(ctx, f"{tag}_count", [EP, buckets])
    total = k.sb(ctx, f"{tag}_total", [P, buckets])
    tiles = k.sb(ctx, f"{tag}_tiles", [P, buckets], I32)
    size = k.sb(ctx, f"{tag}_size", [P, buckets])
    start = k.sb(ctx, f"{tag}_start", [P, buckets])
    base = k.sb(ctx, f"{tag}_base", [P, buckets])
    s_v, s_one, s_count, s_sum = (k.sem(f"{tag}_v"), k.sem(f"{tag}_one_set"),
                                  k.sem(f"{tag}_counted"), k.sem(f"{tag}_summed"))
    s_hit, s_rank, s_pick = k.sem(f"{tag}_hits"), k.sem(f"{tag}_ranks"), k.sem(f"{tag}_picks")
    def vector(v):
        step = Chain(v, s_v)
        v.sem_inc(s_count, 1)
        v.sem_inc(s_pick, 1)
        v.memset(one[:, :], 1.0).then_inc(s_one, 1)
        v.memset(posf[:, :], 0.0).then_inc(s_one, 1)
        with v.Fori(0, buckets) as b:
            v.wait_ge(s_count, b + 1)
            v.tensor_scalar(hit[:, :], key, k.iota[0:EP, bass.ds(b, 1)], None, ALU.is_equal,
                            ALU.add, accum_out=count[:, bass.ds(b, 1)]).then_inc(s_count, 1)
        v.wait_ge(s_sum, 1)
        step(v.tensor_copy(total[:, :], k.ps[bank][:, 0:buckets]))
        if whole_tiles:
            step(v.tensor_scalar(tiles[:, :], total[:, :], float(P - 1), None, ALU.add))
            step(v.tensor_scalar(tiles[:, :], tiles[:, :], 7, None, ALU.arith_shift_right))
            step(v.tensor_scalar(size[:, :], tiles[:, :], 1.0, None, ALU.max))
        else:
            step(v.tensor_copy(size[:, :], total[:, :]))
        v.wait_ge(s_one, 2)
        step(v.tensor_tensor_scan(start[:, :], k.ones[:, 0:buckets], size[:, :], 0.0,
                                  ALU.mult, ALU.add))
        step(v.tensor_tensor(start[:, :], start[:, :], size[:, :], ALU.subtract))
        step(v.tensor_scalar(base[:, :], start[:, :], float(P if whole_tiles else 1), -1.0,
                             ALU.mult, ALU.add))
        step(v.tensor_tensor(base[:, :], base[:, :], k.ps[bank + 1][:, 0:buckets], ALU.add))
        with v.Fori(0, buckets) as b:
            v.wait_ge(s_pick, b + 1)
            v.tensor_scalar(hit[:, :], key, k.iota[0:EP, bass.ds(b, 1)], None, ALU.is_equal)\
                .then_inc(s_hit, 1)
            v.wait_ge(s_hit, b + 1)
            v.tensor_copy(count[:, 0:1], base[0:EP, bass.ds(b, 1)]).then_inc(s_rank, 1)
            v.wait_ge(s_rank, b * 2 + 1)
            v.tensor_tensor_scan(rank[:, :], one[:, :], hit[:, :], count[:, 0:1],
                                 ALU.mult, ALU.add).then_inc(s_rank, 1)
            v.wait_ge(s_rank, b * 2 + 2)
            v.nop(nofuse=True)
            v.copy_predicated(posf[:, :], hit[:, :].bitcast(I32), rank[:, :]).then_inc(s_pick, 1)
        v.wait_ge(s_pick, buckets + 1)
        step(v.tensor_copy(pos, posf[:, :]))
        if whole_tiles:
            step(v.tensor_scalar(where[:, :], pos, P.bit_length() - 1, None, ALU.arith_shift_right))
            step(v.tensor_copy(hit[:, :], where[:, :]))
            step(v.tensor_scalar(where[:, :], pos, P - 1, None, ALU.bitwise_and))
            step(v.tensor_copy(rank[:, :], where[:, :]))
            step(v.scalar_tensor_tensor(posf[:, :], rank[:, :], float(T), hit[:, :], ALU.mult, ALU.add))
            step(v.tensor_copy(pos, posf[:, :]))
        if bounds is not None:
            step(v.tensor_copy(bounds[:, 0:buckets], start[0:1, :]))
            step(v.tensor_tensor(bounds[:, buckets:buckets + 1], start[0:1, buckets - 1:],
                                 size[0:1, buckets - 1:], ALU.add))
        if win is not None:
            step(v.memset(win[:, :], -1.0))
            for b in range(buckets):
                step(v.scalar_tensor_tensor(win[:, :], k.tile_no[:, :], start[:, b:b + 1],
                                            win[:, :], ALU.is_ge, ALU.add))

    def tensor(pe):
        pe.wait_ge(s_count, buckets + 1)
        pe.matmul(k.ps[bank][:, 0:buckets], k.ones[0:EP, :], count[:, :], start=True, stop=True)
        pe.matmul(k.ps[bank + 1][:, 0:buckets], k.before[0:EP, :], count[:, :], start=True, stop=True)\
            .then_inc(s_sum, 1)
    return {"vector": vector, "tensor": tensor}


def scatter(k, tag, ctx, rec, width, pos, table, by_scalar=True, ready=None):
    st_rec = k.sb(ctx, f"{tag}_st_rec", [EP, R, SB, width])
    st_pos = k.sb(ctx, f"{tag}_st_pos", [EP, R, SB], I32)
    s_st = [k.sem(f"{tag}_staged{r}") for r in range(R)]
    s_out = k.pool_dma_sems(f"{tag}_scattered")
    steps = EC // (SB * R)

    def stage(copy, n, r):
        at = bass.ds(n * SB, SB)
        copy(st_pos[:, r, :], pos[:, at]).then_inc(s_st[r], 1)
        copy(st_rec[:, r, :, :], rec[:, at, :]).then_inc(s_st[r], 1)

    def scalar(act):
        if ready is not None:
            act.wait_ge(ready, 1)
        for r in range(R):
            stage(act.copy, r, r)
        with act.Fori(1, steps) as i:
            for r in range(R):
                act.wait_ge(s_out[r], i * (16 * SB))
                act.nop(nofuse=True)
                stage(act.copy, i * R + r, r)

    def send(pool, i, r):
        pool.wait_ge(s_st[r], i * 2 + 2)
        pool.nop(nofuse=True)
        for e in range(SB):
            pool.indirect_dma_start(table, bass.IndirectOffsetOnAxis(ap=st_pos[:, r, e:e + 1], axis=0),
                                    st_rec[:, r, e, :], None).then_inc(s_out[r], 16)

    def gpsimd(pool):
        if by_scalar:
            with pool.Fori(0, steps) as i:
                for r in range(R):
                    send(pool, i, r)
        else:
            for r in range(R):
                stage(pool.tensor_copy, r, r)
                send(pool, 0, r)
            with pool.Fori(1, steps) as i:
                for r in range(R):
                    pool.wait_ge(s_out[r], i * (16 * SB))
                    pool.nop(nofuse=True)
                    stage(pool.tensor_copy, i * R + r, r)
                    send(pool, i, r)
        for r in range(R):
            pool.wait_ge(s_out[r], steps * 16 * SB)
    if by_scalar:
        return {"scalar": scalar, "gpsimd": gpsimd}
    return {"gpsimd": gpsimd}


def fill_pads(k, tag, ctx, table, width, dst_column):
    pad = k.sb(ctx, f"{tag}_pad", [P, TG, width])
    s_p, s_out = k.sem(f"{tag}_pad_made"), k.sem(f"{tag}_pads_out")

    def gpsimd(pool):
        pool.memset(pad[:, :, :], 0.0).then_inc(s_p, 1)
        pool.wait_ge(s_p, 1)
        pool.memset(pad[:, :, dst_column:dst_column + 1], -1.0).then_inc(s_p, 1)

    def sync(sp):
        sp.wait_ge(s_p, 2)
        view = table.rearrange("(c p e) r -> c p e r", c=CH, e=TG)
        for c in range(CH):
            sp.dma_start(view[c], pad[:, :, :]).then_inc(s_out, 16)
        sp.wait_ge(s_out, 16 * CH)
    return {"gpsimd": gpsimd, "sync": sync}


def low_part(v, step, low, tmp, node):
    step(v.tensor_scalar(tmp, node, P - 1, None, ALU.bitwise_and))
    step(v.tensor_copy(low, tmp))


def high_part(v, step, high, tmp, node):
    step(v.tensor_scalar(tmp, node, P.bit_length() - 1, None, ALU.arith_shift_right))
    step(v.tensor_copy(high, tmp))


def degrees(k, ctx, low, high):
    U = 16
    iota = k.sb(ctx, "iota_bf16", [EP, P], BF16)
    lo16 = k.sb(ctx, "low_bf16", [EP, EC], BF16)
    hi16 = k.sb(ctx, "high_bf16", [EP, EC], BF16)
    hot_lo = k.sb(ctx, "degree_hot_low", [EP, 2, U, P], BF16)
    hot_hi = k.sb(ctx, "degree_hot_high", [EP, 2, U, W], BF16)
    zero = k.sb(ctx, "degree_zero", [1, P], BF16)
    s_v, s_hot = k.sem("degree_v"), [k.sem(f"degree_hot{h}") for h in range(2)]
    s_mm = [k.sem(f"degree_summed{h}") for h in range(2)]

    def vector(v):
        step = Chain(v, s_v)
        step(v.tensor_copy(iota[:, :], k.iota[0:EP, :]))
        step(v.tensor_copy(lo16[:, :], low))
        step(v.tensor_copy(hi16[:, :], high))
        step(v.memset(zero[:, :], 0.0))
        with v.Fori(0, EC // U // 2) as i:
            for h in range(2):
                at = bass.ds((i * 2 + h) * U, U)
                v.wait_ge(s_mm[h], i + 1)
                v.nop(nofuse=True)
                for hot, part, n in ((hot_lo, lo16, P), (hot_hi, hi16, W)):
                    v.tensor_tensor(hot[:, h, :, :], bc(part[:, at].unsqueeze(2), [EP, U, n]),
                                    bc(iota[:, 0:n].unsqueeze(1), [EP, U, n]), ALU.is_equal).then_inc(s_hot[h], 1)
        for h in range(2):
            v.wait_ge(s_mm[h], EC // U // 2 + 1 + h)
        step(v.tensor_copy(k.deg[:, :], k.ps[7][:, 0:W]))

    def tensor(pe):
        for s in s_mm:
            pe.sem_inc(s, 1)
        pe.wait_ge(s_v, 4)
        pe.matmul(k.ps[7][:, 0:W], zero[:, :], zero[:, 0:W], start=True, stop=False)
        with pe.Fori(0, EC // U // 2) as i:
            for h in range(2):
                pe.wait_ge(s_hot[h], i * 2 + 2)
                pe.nop(nofuse=True)
                for u in range(U):
                    ins = pe.matmul(k.ps[7][:, 0:W], hot_lo[:, h, u, :], hot_hi[:, h, u, :], start=False, stop=False)
                ins.then_inc(s_mm[h], 1)
        pe.matmul(k.ps[7][:, 0:W], zero[:, :], zero[:, 0:W], start=False, stop=True).then_inc(s_mm[1], 1)
    return {"vector": vector, "tensor": tensor}


def count_matrix(k, ctx):
    f16 = mybir.dt.float16
    HALF = NP // 2
    buf = k.sb(ctx, "cm_list", [P, T, RS])
    loc = k.sb(ctx, "cm_loc", [P, T])
    dst = k.sb(ctx, "cm_dst", [P, T])
    iota = k.sb(ctx, "cm_iota", [P, NP], f16)
    iota_p = k.sb(ctx, "cm_iota_p", [P, P], f16)
    places_ahead = 4
    hot_dst = k.sb(ctx, "cm_hot_dst", [P, places_ahead, NP], BF16)
    hot_src = k.sb(ctx, "cm_hot_src", [P, places_ahead, P], BF16)
    zero = k.sb(ctx, "cm_zero", [1, PSUM_BANK], BF16)
    row = k.sb(ctx, "cm_row", [P, NP])
    s_ld, s_v, s_io = k.sem("cm_list_loaded"), k.sem("cm_v"), k.sem("cm_iota_made")
    s_hot, s_used, s_sum = k.sem("cm_hot"), k.sem("cm_used"), k.sem("cm_window_summed")
    s_row, s_out = k.sem("cm_row_copied"), k.sem("cm_row_stored")
    banks = [(b, b * PSUM_BANK, min(PSUM_BANK, NP - b * PSUM_BANK)) for b in range(-(-NP // PSUM_BANK))]
    B = len(banks)
    at = lambda ap, n: ap[:, bass.ds(n, 1), :].rearrange("p a c -> p (a c)")

    def sync(sp):
        sp.dma_start(buf[:, :, :], k.list_src.rearrange("(p t) r -> p t r", p=P)).then_inc(s_ld, 16)
        with sp.Fori(0, W) as w:
            sp.wait_ge(s_row, (w + 2) * B)
            sp.nop(nofuse=True)
            sp.dma_start(k.counts[bass.ds(w, 1), :, :].rearrange("a p c -> (a p) c"), row[:, :]).then_inc(s_out, 16)
        sp.wait_ge(s_out, 16 * W + 16)

    def gpsimd(pool):
        pool.iota(iota[:, :], [[1, NP]], base=-HALF, channel_multiplier=0,
                  allow_small_or_imprecise_dtypes=True).then_inc(s_io, 1)
        pool.iota(iota_p[:, :], [[1, P]], base=0, channel_multiplier=0,
                  allow_small_or_imprecise_dtypes=True).then_inc(s_io, 1)

    def vector(v):
        tiles = v.value_load(k.bounds_src[0:1, W:W + 1], min_val=W, max_val=T)
        step = Chain(v, s_v)
        step(v.memset(zero[:, :], 0.0))
        v.wait_ge(s_ld, 16)
        step(v.scalar_tensor_tensor(loc[:, :], k.win_src[:, :], -float(P), buf[:, :, 1], ALU.mult, ALU.add))
        step(v.tensor_scalar(dst[:, :], buf[:, :, 3], -float(HALF), None, ALU.add))
        v.wait_ge(s_io, 2)
        with v.Fori(0, tiles) as t:
            v.wait_ge(s_used, t + 1)
            v.nop(nofuse=True)
            place = t % places_ahead
            v.tensor_scalar(at(hot_dst, place), iota[:, :], dst[:, bass.ds(t, 1)], None, ALU.is_equal)\
                .then_inc(s_hot, 1)
            v.tensor_scalar(at(hot_src, place), iota_p[:, :], loc[:, bass.ds(t, 1)], None, ALU.is_equal)\
                .then_inc(s_hot, 1)

    def scalar(act):
        act.sem_inc(s_row, B)
        act.sem_inc(s_out, 16)
        with act.Fori(0, W) as w:
            act.wait_ge(s_out, w * 16 + 16)
            act.nop(nofuse=True)
            for b, col, n in banks:
                act.wait_ge(s_sum, w * B + b + 1)
                act.nop(nofuse=True)
                act.copy(row[:, col:col + n], k.ps[b][:, 0:n]).then_inc(s_row, 1)

    def tensor(pe):
        pe.wait_ge(s_v, 1)
        pe.sem_inc(s_used, places_ahead)
        with pe.Fori(0, W) as w:
            first = pe.value_load(k.bounds_src[0:1, bass.ds(w, 1)], min_val=0, max_val=T)
            behind = pe.value_load(k.bounds_src[0:1, bass.ds(w + 1, 1)], min_val=1, max_val=T)
            for b, col, n in banks:
                pe.wait_ge(s_row, w * B + b + 1)
                pe.nop(nofuse=True)
                pe.matmul(k.ps[b][:, 0:n], zero[:, 0:P], zero[:, 0:n], start=True, stop=False)
            with pe.Fori(first, behind) as t:
                pe.wait_ge(s_hot, t * 2 + 2)
                pe.nop(nofuse=True)
                place = t % places_ahead
                for b, col, n in banks:
                    ins = pe.matmul(k.ps[b][:, 0:n], at(hot_src, place),
                                    hot_dst[:, bass.ds(place, 1), col:col + n].rearrange("p a c -> p (a c)"),
                                    start=False, stop=False)
                ins.then_inc(s_used, 1)
            for b, col, n in banks:
                pe.matmul(k.ps[b][:, 0:n], zero[:, 0:P], zero[:, 0:n], start=False, stop=True).then_inc(s_sum, 1)
    return {"sync": sync, "gpsimd": gpsimd, "vector": vector, "scalar": scalar, "tensor": tensor}


@own_semaphores
def src_places(k, io, rec, pos):
    with ExitStack() as ctx:
        key = k.sb(ctx, "key_src", [EP, EC])
        node = k.sb(ctx, "node_src", [EP, 3, EC], I32)
        tmp = k.sb(ctx, "tmp_src", [EP, EC], I32)
        wgt = k.sb(ctx, "weight_src", [EP, EC])
        s_ld, s_cv = k.sem("typed_edges_loaded"), k.sem("typed_edges_in_records")

        def sync(sp):
            for n, name in enumerate(("src", "dst", "edge_type_4")):
                sp.dma_start(node[:, n, :], by_edge(io[name])).then_inc(s_ld, 16)
            sp.dma_start(wgt[:, :], by_edge(io["edge_weight"])).then_inc(s_ld, 16)

        def vector(v):
            step = Chain(v, s_cv)
            v.wait_ge(s_ld, 64)
            step(v.tensor_copy(key[:, :], node[:, 2, :]))
            step(v.tensor_copy(rec[:, :, 3], node[:, 1, :]))
            step(v.scalar_tensor_tensor(rec[:, :, 0], rec[:, :, 3], float(TYPES), key[:, :], ALU.mult, ALU.add))
            step(v.tensor_copy(rec[:, :, 1], node[:, 0, :]))
            step(v.tensor_copy(rec[:, :, 2], wgt[:, :]))
            high_part(v, step, key[:, :], tmp[:, :], node[:, 0, :])
        in_one_block(k, {"sync": sync, "vector": vector},
                     places(k, "sort_src", ctx, key[:, :], W, pos[:, :], True, k.win_src, k.bounds_src),
                     fill_pads(k, "src", ctx, k.list_src, RS, 1), fill_pads(k, "dst", ctx, k.list_dst, RD, 1))


@own_semaphores
def sort_both(k, io):
    with ExitStack() as outer:
        rec = k.sb(outer, "rec_dst", [EP, EC, RD])
        pos = k.sb(outer, "pos_dst", [EP, EC], I32)
        key = k.sb(outer, "key_dst", [EP, EC])
        node = k.sb(outer, "node_dst", [EP, EC], I32)
        tmp = k.sb(outer, "tmp_dst", [EP, EC], I32)
        steps_back = k.sb(outer, "steps_back", [P, 2])
        unsorted = k.sb(outer, "unsorted", [1, 1], I32)
        with ExitStack() as ctx:
            rec_src = k.sb(ctx, "rec_src", [EP, EC, RS])
            pos_src = k.sb(ctx, "pos_src", [EP, EC], I32)
            src_places(k, io, rec_src, pos_src)
            low = k.sb(ctx, "low_dst", [EP, EC])
            behind = k.sb(ctx, "dst_behind", [EP, EC], I32)
            s_ld, s_z, s_cv, s_back, s_n = (k.sem("src_dst_loaded"), k.sem("behind_set"),
                                            k.sem("src_dst_in_records"), k.sem("steps_back_counted"),
                                            k.sem("steps_back_summed"))

            def sync(sp):
                sp.dma_start(tmp[:, :], by_edge(io["src"])).then_inc(s_ld, 16)
                sp.dma_start(node[:, :], by_edge(io["dst"])).then_inc(s_ld, 16)
                sp.wait_ge(s_z, 1)
                rest = (EP - 1) * EC
                sp.dma_start(behind[0:EP - 1, :], by_edge(io["dst"][1:rest + 1])).then_inc(s_ld, 16)
                sp.dma_start(behind[EP - 1:EP, 0:EC - 1],
                             io["dst"][rest + 1:E].rearrange("(p e) -> p e", p=1)).then_inc(s_ld, 16)

            def vector(v):
                v.memset(behind[:, :], NP).then_inc(s_z, 1)
                v.wait_ge(s_ld, 64)
                step = Chain(v, s_cv)
                step(v.tensor_copy(rec[:, :, 0], tmp[:, :]))
                step(v.tensor_copy(rec[:, :, 1], node[:, :]))
                step(v.tensor_copy(low[:, :], behind[:, :]))
                step(v.tensor_tensor(key[:, :], rec[:, :, 1], low[:, :], ALU.is_gt))
                v.tensor_reduce(steps_back[0:EP, 0:1], key[:, :], AXX, ALU.add).then_inc(s_back, 1)
                v.wait_ge(s_back, 1)
                v.wait_ge(s_n, 1)
                step(v.tensor_copy(unsorted[:, :], k.ps[6][0:1, 0:1]))
                low_part(v, step, low[:, :], tmp[:, :], node[:, :])
                high_part(v, step, key[:, :], tmp[:, :], node[:, :])

            def tensor(pe):
                pe.wait_ge(s_back, 1)
                pe.matmul(k.ps[6][:, 0:1], k.ones[0:EP, :], steps_back[0:EP, 0:1], start=True, stop=True)\
                    .then_inc(s_n, 1)
            in_one_block(k, {"sync": sync, "vector": vector, "tensor": tensor},
                         scatter(k, "move_src", ctx, rec_src, RS, pos_src, k.list_src),
                         conservation(k, io, ctx), degrees(k, ctx, low[:, :], key[:, :]), edge_terms(k, io, ctx, rec),
                         places(k, "sorted_dst", ctx, key[:, :], W, pos[:, :], True, k.win_dst, bank=4))
        with ExitStack() as ctx:
            s_pos, s_v, s_list, s_back = (k.sem("half_places_made"), k.sem("half_v"), k.sem("half_sorted"),
                                          k.sem("half_sorted_back"))
            half = places(k, "sort_low", ctx, key[:, :], P, pos[:, :], False)
            whole = places(k, "sort_dst", ctx, key[:, :], W, pos[:, :], True, k.win_dst, bank=2)
            move = scatter(k, "move_low", ctx, rec, RD, pos, k.list_a, ready=s_pos)

            def if_unsorted(body):
                def run(engine):
                    needed = engine.value_load(unsorted[0:1, 0:1], min_val=0, max_val=E)
                    with engine.If(needed):
                        body(engine)
                    with engine.Else():
                        engine.nop()
                    engine.nop(nofuse=True)
                return run

            def vector(v):
                step = Chain(v, s_v)
                low_part(v, step, key[:, :], tmp[:, :], node[:, :])
                half["vector"](v)
                v.nop(nofuse=True).then_inc(s_pos, 1)
                v.wait_ge(s_back, 16)
                step(v.tensor_copy(node[:, :], rec[:, :, 1]))
                high_part(v, step, key[:, :], tmp[:, :], node[:, :])
                whole["vector"](v)

            def tensor(pe):
                half["tensor"](pe)
                whole["tensor"](pe)

            def gpsimd(pool):
                move["gpsimd"](pool)
                pool.nop(nofuse=True).then_inc(s_list, 1)

            def sync(sp):
                sp.wait_ge(s_list, 1)
                sp.dma_start(rec[:, :, :], k.list_a.rearrange("(p e) r -> p e r", e=EC)).then_inc(s_back, 16)
                sp.wait_ge(s_back, 16)
            in_one_block(k, {"vector": if_unsorted(vector), "tensor": if_unsorted(tensor),
                             "scalar": if_unsorted(move["scalar"]), "gpsimd": if_unsorted(gpsimd),
                             "sync": if_unsorted(sync)})
        with ExitStack() as ctx:
            in_one_block(k, count_matrix(k, ctx),
                         scatter(k, "move_dst", ctx, rec, RD, pos, k.list_dst, by_scalar=False))


@own_semaphores
def read_list(k, tag, table, width, index, loc, extra, win, win_i):
    nc = k.nc
    with ExitStack() as ctx:
        buf = k.sb(ctx, f"{tag}_buf", [P, T, width])
        packed = k.sb(ctx, f"{tag}_packed", [1, T // G])
        s_ld, s_v = k.sem(f"{tag}_loaded"), k.sem(f"{tag}_v")
        with nc.Block() as block:
            @block.sync
            def _(sp):
                sp.dma_start(buf[:, :, :], table.rearrange("(p t) r -> p t r", p=P)).then_inc(s_ld, 16)

            @block.vector
            def _(v):
                step = Chain(v, s_v)
                v.wait_ge(s_ld, 16)
                step(v.memset(index[:, T:], 0))
                step(v.tensor_copy(index[:, 0:T], buf[:, :, 0]))
                step(v.scalar_tensor_tensor(loc[:, 0:T], win[:, :], -float(P), buf[:, :, 1],
                                            ALU.mult, ALU.add))
                step(v.memset(loc[:, T:], -1.0))
                if extra is not None:
                    step(v.tensor_copy(extra[:, 0:T], buf[:, :, 2]))
                    step(v.memset(extra[:, T:], 0.0))
                tile = win[0:1, :].rearrange("p (n g) -> p n g", g=G)
                step(v.tensor_copy(packed[:, :], tile[:, :, G - 1]))
                for g in range(G - 2, -1, -1):
                    step(v.scalar_tensor_tensor(packed[:, :], packed[:, :], float(W), tile[:, :, g], ALU.mult, ALU.add))
                step(v.tensor_copy(win_i[:, :], packed[:, :]))
@own_semaphores
def window_sums(k, tag, loc, win_i, table=None, index=None, weight=None, stream=None, values=None):
    steps = T // (R * G)
    with ExitStack() as ctx:
        hot = hot16 = None
        zero = k.sb(ctx, f"{tag}_zero", [1, PSUM_BANK])
        s_hot, s_used, s_idx, s_row, s_msg = ([k.sem(f"{tag}_{name}{r}") for r in range(R)] for name in
                                              ("hot", "summed", "index_staged", "streamed", "messages"))
        s_z = k.sem(f"{tag}_zero_set")
        rows = st = None
        featured = table is not None or stream is not None
        banks = [b for b in range(8) if (b == 7 and values is not None) or (b < 7 and featured)]
        if featured:
            hot = k.sb(ctx, f"{tag}_hot", [P, R, G, P])
            rows = k.sb(ctx, f"{tag}_rows", [P, R, G, D])
        if values is not None:
            n = values.shape[2]
            hot16 = k.sb(ctx, f"{tag}_hot_bf16", [P, R, G, P], BF16)
            parts = k.sb(ctx, f"{tag}_parts", [P, R, 3, G, n], BF16)
            rest = k.sb(ctx, f"{tag}_rest", [P, R, G, n])
            s_split = k.sem(f"{tag}_split_steps")
            s_part, s_hot16 = ([k.sem(f"{tag}_{name}{r}") for r in range(R)] for name in ("split", "hot_bf16"))
        if table is not None:
            s_row = k.pool_dma_sems(f"{tag}_gathered")
            st = k.sb(ctx, f"{tag}_st", [P, R, G], I32)

        def gpsimd(pool):
            with pool.Fori(0, steps) as i:
                for r in range(R):
                    pool.wait_ge(s_idx[r], i + 1)
                    pool.nop(nofuse=True)
                    for g in range(G):
                        pool.indirect_dma_start(rows[:, r, g, :], None, table,
                                                bass.IndirectOffsetOnAxis(ap=st[:, r, g:g + 1], axis=0))\
                            .then_inc(s_row[r], 16)

        def split_values(pool):
            with pool.Fori(0, steps) as i:
                for r in range(R):
                    n = i * R + r
                    mine = values[:, bass.ds(n * G, G), :]
                    high, middle, low = (parts[:, r, j, :, :] for j in range(3))
                    left = rest[:, r, :, :]
                    pool.wait_ge(s_used[r], i + 1)
                    pool.nop(nofuse=True)
                    pool.tensor_copy(high, mine).then_inc(s_split, 1)
                    pool.wait_ge(s_split, n * 4 + 1)
                    pool.nop(nofuse=True)
                    pool.tensor_tensor(left, mine, high, ALU.subtract).then_inc(s_split, 1)
                    pool.wait_ge(s_split, n * 4 + 2)
                    pool.nop(nofuse=True)
                    pool.tensor_copy(middle, left).then_inc(s_split, 1)
                    pool.wait_ge(s_split, n * 4 + 3)
                    pool.nop(nofuse=True)
                    pool.tensor_tensor(left, left, middle, ALU.subtract).then_inc(s_split, 1)
                    pool.wait_ge(s_split, n * 4 + 4)
                    pool.nop(nofuse=True)
                    pool.tensor_copy(low, left).then_inc(s_part[r], 1)

        def narrow_hot(act):
            with act.Fori(0, steps) as i:
                for r in range(R):
                    act.wait_ge(s_hot[r], i + 1)
                    act.nop(nofuse=True)
                    act.copy(hot16[:, r, :, :], hot[:, r, :, :]).then_inc(s_hot16[r], 1)

        def scalar(act):
            with act.Fori(0, steps) as i:
                for r in range(R):
                    act.wait_ge(s_used[r], i + 1)
                    act.nop(nofuse=True)
                    act.copy(st[:, r, :], index[:, bass.ds((i * R + r) * G, G)]).then_inc(s_idx[r], 1)

        def sync(sp):
            with sp.Fori(0, steps) as i:
                for r in range(R):
                    sp.wait_ge(s_used[r], i + 1)
                    sp.nop(nofuse=True)
                    sp.dma_start(rows[:, r, :, :],
                                 stream[bass.ds(i * R + r, 1), :, :, :].rearrange("a p g c -> (a p) g c"))\
                        .then_inc(s_row[r], 16)

        def vector(v):
            v.memset(zero[:, :], 0.0).then_inc(s_z, 1)
            with v.Fori(0, steps) as i:
                for r in range(R):
                    at = bass.ds((i * R + r) * G, G)
                    v.wait_ge(s_used[r], i + 1)
                    v.nop(nofuse=True)
                    if weight is not None:
                        for g in range(G):
                            n = bass.ds((i * R + r) * G + g, 1)
                            v.tensor_scalar(hot[:, r, g, :], k.iota[:, :], loc[:, n], weight[:, n],
                                            ALU.is_equal, ALU.mult).then_inc(s_hot[r], 1)
                    else:
                        to, done = (hot, s_hot) if featured else (hot16, s_hot16)
                        v.tensor_tensor(to[:, r, :, :], bc(loc[:, at].unsqueeze(2), [P, G, P]),
                                        bc(k.iota[:, :].unsqueeze(1), [P, G, P]), ALU.is_equal)\
                            .then_inc(done[r], 1)
                    if stream is not None:
                        v.wait_ge(s_row[r], i * 16 + 16)
                        v.nop(nofuse=True)
                        ft = rows[:, r, :, :].rearrange("p g (a c) -> p g a c", c=C)
                        v.tensor_tensor(ft, ft, bc(values[:, at, 0:HEADS].unsqueeze(3), [P, G, HEADS, C]),
                                        ALU.mult).then_inc(s_msg[r], 1)

        def tensor(pe):
            for s in s_used:
                pe.sem_inc(s, 1)
            pe.wait_ge(s_z, 1)
            for b in banks:
                pe.matmul(k.ps[b][:, :], zero[:, 0:P], zero[:, :], start=True, stop=False)
            with pe.Fori(0, steps) as i:
                for r in range(R):
                    to = windows_of(pe.value_load(win_i[0:1, bass.ds(i * R + r, 1)], min_val=0,
                                                  max_val=W ** G - 1))
                    if featured:
                        pe.wait_ge(s_hot[r], (i + 1) * (G if weight is not None else 1))
                    if values is not None:
                        pe.wait_ge(s_hot16[r], i + 1)
                        pe.wait_ge(s_part[r], i + 1)
                    if table is not None:
                        pe.wait_ge(s_row[r], (i + 1) * (16 * G))
                    if stream is not None:
                        pe.wait_ge(s_msg[r], i + 1)
                    pe.nop(nofuse=True)
                    for g in range(G):
                        if featured:
                            ins = pe.matmul(k.psum[:, bass.ds(to[g] * D, D)], hot[:, r, g, :], rows[:, r, g, :],
                                            start=False, stop=False)
                        if values is not None:
                            for j in range(3):
                                ins = pe.matmul(k.psum[:, bass.ds(to[g] * n + 7 * PSUM_BANK, n)],
                                                hot16[:, r, g, :], parts[:, r, j, g, :], start=False, stop=False)
                    ins.then_inc(s_used[r], 1)
            for b in banks:
                ins = pe.matmul(k.ps[b][:, :], zero[:, 0:P], zero[:, :], start=False, stop=True)
            ins.then_inc(s_z, 1)
            pe.wait_ge(s_z, 2)
        stage = {"vector": vector, "tensor": tensor}
        if table is not None:
            stage["gpsimd"], stage["scalar"] = gpsimd, scalar
        if stream is not None:
            stage["sync"], stage["scalar"] = sync, narrow_hot
        if values is not None:
            stage["gpsimd"] = split_values
        in_one_block(k, stage)


def feature_sums(k):
    return k.psum[:, 0:W * D].rearrange("p (w d) -> p w d", d=D)


def value_sums(k, n):
    return k.psum[:, 7 * PSUM_BANK:7 * PSUM_BANK + W * n].rearrange("p (w n) -> p w n", n=n)


@own_semaphores
def project(k, tag, src, weights, cols, keep, store=None):
    U = PSUM_BANK // P
    K = 6
    groups = [range(w, min(w + U, W)) for w in range(0, W, U)]
    with ExitStack() as ctx:
        src_t = k.sb(ctx, f"{tag}_src_t", [P, 2, U, P])
        s_tr, s_cp, s_mm, s_kept, s_out = (k.sem(f"{tag}_transposed"), k.sem(f"{tag}_copied"), k.sem(f"{tag}_product"),
                                           k.sem(f"{tag}_kept"), k.sem(f"{tag}_stored"))

        def scalar(act):
            for g, windows in enumerate(groups):
                act.wait_ge(s_tr, g + 1)
                if g >= 2:
                    act.wait_ge(s_mm, groups[g - 1][0])
                n = len(windows)
                act.copy(src_t[:, g % 2, 0:n, :], k.ps[g % 2][:, 0:n * P].rearrange("p (a b) -> p a b", b=P))\
                    .then_inc(s_cp, 1)

        def vector(v):
            for w in range(W):
                v.wait_ge(s_mm, w + 1)
                keep(v, w, k.ps[2 + w % K][:, 0:cols]).then_inc(s_kept, 1)
            v.wait_ge(s_kept, W)

        def tensor(pe):
            def transposes(g):
                if g >= 2:
                    pe.wait_ge(s_cp, g - 1)
                for u, w in enumerate(groups[g]):
                    ins = pe.transpose(k.ps[g % 2][:, u * P:(u + 1) * P], src[:, w, :], k.ident[:, :])
                ins.then_inc(s_tr, 1)

            transposes(0)
            for g, windows in enumerate(groups):
                if g + 1 < len(groups):
                    transposes(g + 1)
                pe.wait_ge(s_cp, g + 1)
                for u, w in enumerate(windows):
                    if w >= K:
                        pe.wait_ge(s_kept, w - K + 1)
                    pe.matmul(k.ps[2 + w % K][:, 0:cols], src_t[:, g % 2, u, :], weights, start=True, stop=True)\
                        .then_inc(s_mm, 1)

        def sync(sp):
            for windows in groups:
                sp.wait_ge(s_kept, windows[-1] + 1)
                to, what = store(windows[0], windows[-1] + 1)
                sp.dma_start(to, what).then_inc(s_out, 16)
            sp.wait_ge(s_out, 16 * len(groups))
        stage = {"scalar": scalar, "vector": vector, "tensor": tensor}
        if store is not None:
            stage["sync"] = sync
        in_one_block(k, stage)


@own_semaphores
def vector_steps(k, tag, steps, loads=(), stores=()):
    nc = k.nc
    s_ld, s_v, s_st = k.sem(f"{tag}_loads"), k.sem(f"{tag}_v"), k.sem(f"{tag}_stores")
    done = {}
    with nc.Block() as block:
        @block.vector
        def _(v):
            step = Chain(v, s_v)
            if loads:
                v.wait_ge(s_ld, 16 * len(loads))
            if steps is not None:
                steps(v, step)
            done["n"] = step.n

        @block.sync
        def _(sp):
            for dst, src in loads:
                sp.dma_start(dst, src).then_inc(s_ld, 16)
            if stores and steps is not None:
                sp.wait_ge(s_v, done["n"])
            for dst, src in stores:
                sp.dma_start(dst, src).then_inc(s_st, 16)
            if stores:
                sp.wait_ge(s_st, 16 * len(stores))


@own_semaphores
def split(k, tag, src, parts):
    with ExitStack() as ctx:
        rest = k.sb(ctx, f"{tag}_rest", [P, W, src.shape[2]])

        def steps(v, step):
            step(v.tensor_copy(parts[:, :, 0, :], src[:, :, :]))
            step(v.tensor_tensor(rest[:, :, :], src[:, :, :], parts[:, :, 0, :], ALU.subtract))
            step(v.tensor_copy(parts[:, :, 1, :], rest[:, :, :]))
            step(v.tensor_tensor(rest[:, :, :], rest[:, :, :], parts[:, :, 1, :], ALU.subtract))
            step(v.tensor_copy(parts[:, :, 2, :], rest[:, :, :]))
        vector_steps(k, f"{tag}_split", steps)


@own_semaphores
def edge_rows(k, tag, table_src, cols_src, by_dst, cols_dst, consume, keep_rows=None, beside=None):
    steps = T // (R * G)
    with ExitStack() as ctx:
        a = k.sb(ctx, f"{tag}_by_src", [P, R, G, cols_src])
        st = k.sb(ctx, f"{tag}_st", [P, R, G], I32)
        hot = k.sb(ctx, f"{tag}_hot", [P, 2, G, P], BF16)
        hot_t = k.sb(ctx, f"{tag}_hot_t", [P, 2, G, P], BF16)
        s_hot, s_tr, s_cp, s_mm, s_done = (k.sem(f"{tag}_{name}") for name in
                                           ("hot", "transposed", "hot_t_copied", "by_dst_made", "consumed"))
        s_st, s_kept = ([k.sem(f"{tag}_{name}{r}") for r in range(R)] for name in ("staged", "kept"))
        s_row = k.pool_dma_sems(f"{tag}_gathered")
        by_place = k.psum[:, 2 * PSUM_BANK:6 * PSUM_BANK].rearrange("p (q g c) -> p q g c", q=2, g=G)

        def gpsimd(pool):
            with pool.Fori(0, steps) as i:
                for r in range(R):
                    pool.wait_ge(s_st[r], i + 1)
                    if keep_rows is not None:
                        pool.wait_ge(s_kept[r], i * 16 + 1)
                    pool.nop(nofuse=True)
                    for g in range(G):
                        pool.indirect_dma_start(a[:, r, g, :], None, table_src,
                                                bass.IndirectOffsetOnAxis(ap=st[:, r, g:g + 1], axis=0))\
                            .then_inc(s_row[r], 16)

        def vector(v):
            v.sem_inc(s_done, R)

            def one_hots(n, q):
                v.wait_ge(s_tr, n + 1)
                v.nop(nofuse=True)
                v.tensor_tensor(hot[:, q, :, :], bc(k.loc[:, bass.ds(n * G, G)].unsqueeze(2), [P, G, P]),
                                bc(k.iota[:, :].unsqueeze(1), [P, G, P]), ALU.is_equal).then_inc(s_hot, 1)
            one_hots(0, 0)
            one_hots(1, 1)
            with v.Fori(0, steps) as i:
                for r in range(R):
                    n = i * R + r
                    one_hots(n + 2, r % 2)
                    v.wait_ge(s_mm, n + 3)
                    v.wait_ge(s_row[r], (i + 1) * (16 * G))
                    v.nop(nofuse=True)
                    consume(v, n, a[:, r, :, :], by_place[:, r % 2, :, 0:cols_dst]).then_inc(s_done, 1)

        def scalar(act):
            act.sem_inc(s_cp, 2)
            for r in range(R - 1):
                act.copy(st[:, r, :], k.src_i[:, r * G:(r + 1) * G]).then_inc(s_st[r], 1)
            with act.Fori(0, steps) as i:
                for r in range(R):
                    n, q, ahead = i * R + r, r % 2, (r + R - 1) % R
                    act.wait_ge(s_tr, n + 3)
                    act.wait_ge(s_mm, n + 1)
                    act.nop(nofuse=True)
                    act.copy(hot_t[:, q, :, :], k.ps[q][:, :].rearrange("p (g e) -> p g e", g=G)).then_inc(s_cp, 1)
                    act.wait_ge(s_done, n + R)
                    act.nop(nofuse=True)
                    act.copy(st[:, ahead, :], k.src_i[:, bass.ds((n + R - 1) * G, G)]).then_inc(s_st[ahead], 1)

        def tensor(pe):
            pe.sem_inc(s_tr, 2)
            pe.sem_inc(s_mm, 2)

            def transposes(n, q):
                pe.wait_ge(s_hot, n + 1)
                pe.wait_ge(s_cp, n + 1)
                pe.nop(nofuse=True)
                for g in range(G):
                    ins = pe.matmul(k.ps[q][:, g * P:(g + 1) * P], hot[:, q, g, :], k.ident16[:, :],
                                    start=True, stop=True)
                ins.then_inc(s_tr, 1)

            transposes(0, 0)
            with pe.Fori(0, steps) as i:
                for r in range(R):
                    n, q = i * R + r, r % 2
                    transposes(n + 1, (r + 1) % 2)
                    of = windows_of(pe.value_load(k.win_i[0:1, bass.ds(n, 1)], min_val=0, max_val=W ** G - 1))
                    pe.wait_ge(s_cp, n + 3)
                    pe.wait_ge(s_done, n + (R - 1))
                    pe.nop(nofuse=True)
                    for g in range(G):
                        for j in range(3):
                            ins = pe.matmul(by_place[:, q, g, 0:cols_dst], hot_t[:, q, g, :],
                                            by_dst[:, bass.ds(of[g], 1), j, :].rearrange("p a c -> p (a c)"),
                                            start=j == 0, stop=j == 2)
                    ins.then_inc(s_mm, 1)

        stage = {"gpsimd": gpsimd, "vector": vector, "scalar": scalar, "tensor": tensor}
        if keep_rows is not None:
            def sync(sp):
                for s in s_kept:
                    sp.sem_inc(s, 1)
                with sp.Fori(0, steps) as i:
                    for r in range(R):
                        sp.wait_ge(s_row[r], (i + 1) * (16 * G))
                        sp.nop(nofuse=True)
                        sp.dma_start(keep_rows[bass.ds(i * R + r, 1), :, :, :].rearrange("a p g c -> (a p) g c"),
                                     a[:, r, :, 0:D]).then_inc(s_kept[r], 16)
                for r in range(R):
                    sp.wait_ge(s_kept[r], 16 * steps + 1)
            stage["sync"] = sync
        in_one_block(k, stage, beside or {})


@own_semaphores
def across(k, tag, src, dst, forward, broadcast=False):
    U = 3
    with ExitStack() as ctx:
        st = k.sb(ctx, f"{tag}_st", [P, 2, U, P])
        s_st, s_tr, s_cp = k.sem(f"{tag}_staged"), k.sem(f"{tag}_transposed"), k.sem(f"{tag}_copied")

        def slots_side(buf, i):
            if broadcast:
                ap = buf.rearrange("p (c g) -> p c g", g=TG)[:, :, bass.ds(i * U, U)]
                return bc(ap.rearrange("p c g -> p g c").unsqueeze(3), [P, U, CH, HEADS])
            ap = buf.rearrange("p (c g) h -> p c g h", g=TG)[:, :, bass.ds(i * U, U), :]
            return ap.rearrange("p c g h -> p g c h")

        def over_steps(engine, body):
            with engine.Fori(0, TG // U // 2) as i:
                for q in range(2):
                    body(i * 2 + q, q)
            for n in range(TG // U // 2 * 2, TG // U):
                body(n, n % 2)

        def scalar(act):
            def stage(n, q):
                act.wait_ge(s_tr, n + 1)
                act.nop(nofuse=True)
                if forward:
                    act.copy(st[:, q, :, :].rearrange("p g (c h) -> p g c h", h=HEADS),
                             slots_side(src, n)).then_inc(s_st, 1)
                else:
                    act.copy(st[:, q, :, :].rearrange("p g e -> p (g e)"),
                             src[:, bass.ds(n * (U * P), U * P)]).then_inc(s_st, 1)
            over_steps(act, stage)

        def tensor(pe):
            for s in (s_tr, s_cp):
                pe.sem_inc(s, 2)

            def transposes(n, q):
                pe.wait_ge(s_st, n + 1)
                pe.wait_ge(s_cp, n + 1)
                pe.nop(nofuse=True)
                for u in range(U):
                    ins = pe.transpose(k.ps[q][:, u * P:(u + 1) * P], st[:, q, u, :], k.ident[:, :])
                ins.then_inc(s_tr, 1)
            over_steps(pe, transposes)

        def vector(v):
            def take(n, q):
                v.wait_ge(s_tr, n + 3)
                v.nop(nofuse=True)
                if forward:
                    v.tensor_copy(dst[:, bass.ds(n * (U * P), U * P)], k.ps[q][:, 0:U * P]).then_inc(s_cp, 1)
                else:
                    v.tensor_copy(slots_side(dst, n),
                                  k.ps[q][:, 0:U * P].rearrange("p (g c h) -> p g c h", g=U, h=HEADS))\
                        .then_inc(s_cp, 1)
            over_steps(v, take)
        in_one_block(k, {"scalar": scalar, "tensor": tensor, "vector": vector})


@own_semaphores
def segment_max(k, tag, val):
    nc = k.nc
    with ExitStack() as ctx:
        vt = k.sb(ctx, f"{tag}_vt", [P, L])
        out = k.sb(ctx, f"{tag}_out", [P, L])
        wall = k.sb(ctx, f"{tag}_wall", [P, L + 1])
        ends = k.sb(ctx, f"{tag}_ends", [P, 2])
        rows = k.sb(ctx, f"{tag}_rows", [1, 7, HEADS, CH])
        carry = k.sb(ctx, f"{tag}_carry", [P, 2])
        across(k, f"{tag}_dst", k.dst_f, out[:, :], True, broadcast=True)
        across(k, f"{tag}_val", val, vt[:, :], True)
        s_v, s_v2, s_pe = k.sem(f"{tag}_v"), k.sem(f"{tag}_v2"), k.sem(f"{tag}_pe")
        FIRST, LAST, VAL, WALL, IN, SCAN, BACK = range(7)

        with nc.Block() as block:
            @block.vector
            def _(v):
                step = Chain(v, s_v)
                step(v.tensor_copy(ends[:, 0:1], out[:, 0:1]))
                step(v.tensor_copy(ends[:, 1:2], out[:, L - 1:L]))
                step(v.tensor_tensor(wall[:, 1:L], out[:, 1:L], out[:, 0:L - 1], ALU.not_equal))
                step(v.memset(wall[:, 0:1], 0.0))
                step(v.memset(wall[:, L:L + 1], 0.0))
                step(v.tensor_scalar(wall[:, 1:L], wall[:, 1:L], -BIG, None, ALU.mult))
                step(v.tensor_tensor_scan(out[:, :], wall[:, 0:L], vt[:, :], -BIG, ALU.add, ALU.max))
                v.nop(nofuse=True).then_inc(s_v2, 1)

                def chunks(row):
                    return rows[0:1, row, :, :]

                def border(a, b, at):
                    here, there = (slice(1, CH), slice(0, CH - 1))
                    if a == FIRST:
                        here, there = there, here
                    step(v.memset(chunks(at), -BIG))
                    step(v.tensor_tensor(rows[0:1, at, :, here], rows[0:1, b, :, here],
                                         rows[0:1, a, :, there], ALU.not_equal))
                    step(v.tensor_scalar(rows[0:1, at, :, here], rows[0:1, at, :, here], -BIG, None, ALU.mult))
                    return here, there

                def carried(n, a, b, order):
                    v.wait_ge(s_pe, 1 + 2 * n)
                    if n == 0:
                        for q, row in enumerate((FIRST, LAST)):
                            step(v.tensor_copy(chunks(row), k.ps[1][0:1, q * P:(q + 1) * P]
                                               .rearrange("p (c h) -> p h c", h=HEADS)))
                    step(v.tensor_copy(chunks(VAL), k.ps[2][0:1, n * P:(n + 1) * P]
                                       .rearrange("p (c h) -> p h c", h=HEADS)))
                    border(a, a, WALL)
                    flat = lambda row: rows[0:1, row, :, :].rearrange("p h c -> p (h c)")[:, ::order]
                    step(v.tensor_tensor_scan(flat(SCAN), flat(WALL), flat(VAL), -BIG, ALU.add, ALU.max))
                    here, there = border(a, b, IN)
                    step(v.tensor_tensor(rows[0:1, IN, :, here], rows[0:1, IN, :, here],
                                         rows[0:1, SCAN, :, there], ALU.add))
                    step(v.tensor_copy(rows[0:1, BACK, :, :].rearrange("p h c -> p (h c)")
                                       .rearrange("p (c h) -> p c h", h=HEADS),
                                       rows[0:1, IN, :, :].rearrange("p h c -> p c h")))
                    v.nop(nofuse=True).then_inc(s_v2, 1)
                    v.wait_ge(s_pe, 2 + 2 * n)
                    step(v.tensor_scalar(carry[:, n:n + 1], k.ps[3][:, n:n + 1], -BIG, None, ALU.max))

                carried(0, LAST, FIRST, 1)
                step(v.tensor_tensor_scan(out[:, :], wall[:, 0:L], vt[:, :], carry[:, 0:1], ALU.add, ALU.max))
                step(v.tensor_tensor_scan(vt[:, ::-1], wall[:, L:0:-1], out[:, ::-1], -BIG, ALU.add, ALU.max))
                v.nop(nofuse=True).then_inc(s_v2, 1)
                carried(1, FIRST, LAST, -1)
                step(v.tensor_tensor_scan(vt[:, ::-1], wall[:, L:0:-1], out[:, ::-1], carry[:, 1:2],
                                          ALU.add, ALU.max))

            @block.tensor
            def _(pe):
                for n, last in ((0, out[:, L - 1:L]), (1, vt[:, 0:1])):
                    pe.wait_ge(s_v2, 1 + 2 * n)
                    if n == 0:
                        for q in range(2):
                            pe.matmul(k.ps[1][0:1, q * P:(q + 1) * P], ends[:, q:q + 1], k.ident[:, :],
                                      start=True, stop=True)
                    pe.matmul(k.ps[2][0:1, n * P:(n + 1) * P], last, k.ident[:, :], start=True, stop=True)\
                        .then_inc(s_pe, 1)
                    pe.wait_ge(s_v2, 2 + 2 * n)
                    pe.matmul(k.ps[3][:, n:n + 1], rows[0:1, BACK, :, :].rearrange("p h c -> p (h c)"),
                              k.ones[0:1, 0:1], start=True, stop=True).then_inc(s_pe, 1)
        across(k, f"{tag}_back", vt[:, :], val, False)


@own_semaphores
def count_product(k, tag, rows, acc):
    U = 5
    with ExitStack() as ctx:
        cnt = k.sb(ctx, f"{tag}_counts", [P, U, NP])
        st = k.sb(ctx, f"{tag}_rows", [P, U, D])
        zero = k.sb(ctx, f"{tag}_zero", [1, PSUM_BANK])
        sums = k.sb(ctx, f"{tag}_sums", [P, NP])
        s_z, s_all, s_cp, s_tr, s_kept = (k.sem(f"{tag}_zero_set"), k.sem(f"{tag}_summed"), k.sem(f"{tag}_copied"),
                                          k.sem(f"{tag}_transposed"), k.sem(f"{tag}_kept"))
        s_ld, s_st, s_used = ([k.sem(f"{tag}_{name}{u}") for u in range(U)] for name in ("loaded", "staged", "used"))
        banks = [(b, b * PSUM_BANK, min(PSUM_BANK, NP - b * PSUM_BANK)) for b in range(-(-NP // PSUM_BANK))]
        per = PSUM_BANK // P

        def sync(sp):
            with sp.Fori(0, W // U) as i:
                for u in range(U):
                    sp.wait_ge(s_used[u], i + 1)
                    sp.nop(nofuse=True)
                    sp.dma_start(cnt[:, u, :], k.counts[bass.ds(i * U + u, 1), :, :].rearrange("a p c -> (a p) c"))\
                        .then_inc(s_ld[u], 16)

        def scalar(act):
            with act.Fori(0, W // U) as i:
                for u in range(U):
                    act.wait_ge(s_used[u], i + 1)
                    act.nop(nofuse=True)
                    act.copy(st[:, u, :], rows[:, bass.ds(i * U + u, 1), :].rearrange("p a d -> p (a d)"))\
                        .then_inc(s_st[u], 1)
            act.wait_ge(s_all, 1)
            for b, col, n in banks:
                act.copy(sums[:, col:col + n], k.ps[b][:, 0:n]).then_inc(s_cp, 1)

        def vector(v):
            v.memset(zero[:, :], 0.0).then_inc(s_z, 1)
            for b, col, n in banks:
                v.wait_ge(s_tr, b + 1)
                v.tensor_copy(acc[:, b * per:b * per + n // P, :],
                              k.ps[b][:, 0:n].rearrange("p (w d) -> p w d", d=D)).then_inc(s_kept, 1)
            v.wait_ge(s_kept, len(banks))

        def tensor(pe):
            for s in s_used:
                pe.sem_inc(s, 1)
            pe.wait_ge(s_z, 1)
            for b, col, n in banks:
                pe.matmul(k.ps[b][:, 0:n], zero[:, 0:P], zero[:, 0:n], start=True, stop=False)
            with pe.Fori(0, W // U) as i:
                for u in range(U):
                    pe.wait_ge(s_ld[u], i * 16 + 16)
                    pe.wait_ge(s_st[u], i + 1)
                    pe.nop(nofuse=True)
                    for b, col, n in banks:
                        ins = pe.matmul(k.ps[b][:, 0:n], st[:, u, :], cnt[:, u, col:col + n], start=False, stop=False)
                    ins.then_inc(s_used[u], 1)
            for b, col, n in banks:
                ins = pe.matmul(k.ps[b][:, 0:n], zero[:, 0:P], zero[:, 0:n], start=False, stop=True)
            ins.then_inc(s_all, 1)
            for b, col, n in banks:
                pe.wait_ge(s_cp, b + 1)
                for w in range(n // P):
                    ins = pe.transpose(k.ps[b][:, w * P:(w + 1) * P], sums[:, col + w * P:col + (w + 1) * P],
                                       k.ident[:, :])
                ins.then_inc(s_tr, 1)
        in_one_block(k, {"sync": sync, "scalar": scalar, "vector": vector, "tensor": tensor})


@own_semaphores
def layer_filter(k, io):
    nc = k.nc
    with ExitStack() as ctx:
        h = k.sb(ctx, "l0_h", [P, W, D])
        layernorm(k, "ln0", k.x, h)
        scaled = k.sb(ctx, "l0_scaled", [P, W, D])
        acc = k.sb(ctx, "l0_acc", [P, W, D])
        tmp = k.sb(ctx, "l0_degree_tmp", [P, 4, W])
        wide = [P, W, D]
        s_c, s_s = k.sem("l0_clipped"), k.sem("l0_root")
        s_n = k.sem("l0_deg_steps")
        with nc.Block() as block:
            @block.vector
            def _(v):
                v.tensor_scalar(tmp[:, 0, :], k.deg[:, :], 1.0, None, ALU.max).then_inc(s_c, 1)
                v.wait_ge(s_s, 1)
                step = Chain(v, s_n)
                step(v.reciprocal(k.dinv[:, :], tmp[:, 1, :]))
                step(v.tensor_scalar(k.no_edge[:, :], k.deg[:, :], 0.0, None, ALU.is_equal))
                step(v.tensor_scalar(tmp[:, 2, :], k.deg[:, :], 0.0, None, ALU.is_gt))
                step(v.tensor_tensor(k.dinv0[:, :], k.dinv[:, :], tmp[:, 2, :], ALU.mult))
                step(v.reciprocal(k.inv_deg[:, :], tmp[:, 0, :]))

            @block.scalar
            def _(act):
                act.wait_ge(s_c, 1)
                act.activation(tmp[:, 1, :], tmp[:, 0, :], ACT.Sqrt).then_inc(s_s, 1)
        dinv = bc(k.dinv[:, :].unsqueeze(2), wide)

        def first(v, step):
            step(v.scalar_tensor_tensor(k.x[:, :, :], h[:, :, :], THETA[0], k.x[:, :, :], ALU.mult, ALU.add))
            step(v.tensor_tensor(scaled[:, :, :], h[:, :, :], dinv, ALU.mult))
        vector_steps(k, "l0_first", first)
        for r in range(1, len(THETA)):
            count_product(k, f"l0_sum{r}", scaled, acc)

            def update(v, step):
                step(v.tensor_tensor(acc[:, :, :], acc[:, :, :], dinv, ALU.mult))
                step(v.tensor_tensor(h[:, :, :], h[:, :, :], acc[:, :, :], ALU.subtract))
                step(v.scalar_tensor_tensor(k.x[:, :, :], h[:, :, :], THETA[r], k.x[:, :, :], ALU.mult, ALU.add))
                if r + 1 < len(THETA):
                    step(v.tensor_tensor(scaled[:, :, :], h[:, :, :], dinv, ALU.mult))
            vector_steps(k, f"l0_update{r}", update)


@own_semaphores
def layer_gat(k, io):
    nc = k.nc
    wide = [P, W, D]
    SLOPE = 0.2
    AD = 2 * HEADS + 1
    t_src = nc.dram_tensor("l1_by_src", [NP, D + HEADS], F32).ap()
    kept = nc.dram_tensor("l1_rows", [T // G, P, G, D], F32).ap()
    with ExitStack() as outer:
        dst_parts = k.sb(outer, "l1_dst_parts", [P, W, 3, AD], BF16)
        with ExitStack() as ctx:
            h = k.sb(ctx, "l1_ln", [P, W, D])
            layernorm(k, "ln1", k.x, h)
            by_src = k.sb(ctx, "l1_src_rows", [P, W, D + HEADS])
            by_dst = k.sb(ctx, "l1_dst_rows", [P, W, AD])
            w = k.sb(ctx, "l1_w", [P, D])
            att = k.sb(ctx, "l1_att", [P, 2, D])
            tmp = k.sb(ctx, "l1_tmp", [P, W, D])
            loads = [(w[:, :], io["L1_gnn_W"]),
                     (att[:, 0, :], io["L1_gnn_att_src"].rearrange("h c -> (h c)").partition_broadcast(P)),
                     (att[:, 1, :], io["L1_gnn_att_dst"].rearrange("h c -> (h c)").partition_broadcast(P))]
            vector_steps(k, "l1_load", None, loads=loads)
            project(k, "l1_h", h, w[:, :], D, lambda v, n, ps: v.tensor_copy(
                by_src[:, bass.ds(n, 1), 0:D].rearrange("p a d -> p (a d)"), ps))
            heads = lambda ap: ap.rearrange("p w (h c) -> p w h c", c=C)

            def scores(v, step):
                for q, dst in ((0, by_src[:, :, D:D + HEADS]), (1, by_dst[:, :, 0:HEADS])):
                    step(v.tensor_tensor(tmp[:, :, :], by_src[:, :, 0:D], bc(att[:, q, :].unsqueeze(1), wide),
                                         ALU.mult))
                    step(v.tensor_reduce(dst, heads(tmp[:, :, :]), AXX, ALU.add))
                own = by_dst[:, :, HEADS:2 * HEADS]
                step(v.tensor_tensor(own, by_src[:, :, D:D + HEADS], by_dst[:, :, 0:HEADS], ALU.add))
                step(v.scalar_tensor_tensor(own, own, SLOPE, own, ALU.mult, ALU.max))
                step(v.tensor_copy(by_dst[:, :, 2 * HEADS], k.inv_deg[:, :]))
            vector_steps(k, "l1_scores", scores, stores=[(rows_in(t_src), by_src[:, :, :])])
            split(k, "l1_dst", by_dst, dst_parts)
        with ExitStack() as ctx:
            shares = k.sb(ctx, "l1_shares", [P, T, 2 * HEADS])
            e = shares[:, :, 0:HEADS]
            own = k.sb(ctx, "l1_own", [P, T, HEADS + 1])
            top = shares[:, :, HEADS:]
            s_c = k.sem("l1_own_copied")

            def consume(v, n, a, b):
                at = bass.ds(n * G, G)
                v.tensor_copy(own[:, at, :], b[:, :, HEADS:AD]).then_inc(s_c, 1)
                return v.tensor_tensor(e[:, at, :], a[:, :, D:D + HEADS], b[:, :, 0:HEADS], ALU.add)
            edge_rows(k, "l1_edges", t_src, D + HEADS, dst_parts, AD, consume, keep_rows=kept)

            def leaky(v, step):
                step(v.scalar_tensor_tensor(e[:, :, :], e[:, :, :], SLOPE, e[:, :, :], ALU.mult, ALU.max))
                step(v.tensor_tensor(top[:, :, :], e[:, :, :], own[:, :, 0:HEADS], ALU.max))
            vector_steps(k, "l1_leaky", leaky)
            segment_max(k, "l1_max", top[:, :, :])
            s_a, s_b, s_c2 = k.sem("l1_less_top"), k.sem("l1_exp"), k.sem("l1_own_shared")
            with nc.Block() as block:
                @block.vector
                def _(v):
                    v.tensor_tensor(e[:, :, :], e[:, :, :], top[:, :, :], ALU.subtract).then_inc(s_a, 1)
                    v.tensor_tensor(own[:, :, 0:HEADS], own[:, :, 0:HEADS], top[:, :, :], ALU.subtract).then_inc(s_a, 1)
                    v.wait_ge(s_b, 2)
                    v.tensor_tensor(shares[:, :, HEADS:], own[:, :, 0:HEADS],
                                    bc(own[:, :, HEADS:HEADS + 1], [P, T, HEADS]), ALU.mult).then_inc(s_c2, 1)

                @block.scalar
                def _(act):
                    act.wait_ge(s_a, 1)
                    act.activation(e[:, :, :], e[:, :, :], ACT.Exp).then_inc(s_b, 1)
                    act.wait_ge(s_a, 2)
                    act.activation(own[:, :, 0:HEADS], own[:, :, 0:HEADS], ACT.Exp).then_inc(s_b, 1)
            window_sums(k, "l1_sum", k.loc, k.win_i, stream=kept, values=shares)
            sums = k.sb(ctx, "l1_sums", [P, W, 2 * HEADS])
            h2 = k.sb(ctx, "l1_h_back", [P, W, D])
            bias = k.sb(ctx, "l1_bias", [P, D])

            def finish(v, step):
                msg, den, loop = feature_sums(k), sums[:, :, 0:HEADS], sums[:, :, HEADS:]
                step(v.tensor_copy(sums[:, :, :], value_sums(k, 2 * HEADS)))
                per_head = lambda ap: bc(ap.unsqueeze(3), [P, W, HEADS, C])
                step(v.tensor_tensor(loop, loop, bc(k.no_edge[:, :].unsqueeze(2), [P, W, HEADS]), ALU.add))
                step(v.tensor_tensor(den, den, loop, ALU.add))
                step(v.reciprocal(den, den))
                step(v.tensor_tensor(heads(h2[:, :, :]), heads(h2[:, :, :]), per_head(loop), ALU.mult))
                step(v.tensor_tensor(h2[:, :, :], h2[:, :, :], msg, ALU.add))
                step(v.tensor_tensor(heads(h2[:, :, :]), heads(h2[:, :, :]), per_head(den), ALU.mult))
                step(v.tensor_tensor(h2[:, :, :], h2[:, :, :], bc(bias[:, :].unsqueeze(1), wide), ALU.add))
                step(v.tensor_tensor(k.x[:, :, :], k.x[:, :, :], h2[:, :, :], ALU.add))
            vector_steps(k, "l1_finish", finish, loads=[(h2[:, :, :], rows_in(t_src)[:, :, 0:D]),
                                                        (bias[:, :], io["L1_gnn_bias"].partition_broadcast(P))])


@own_semaphores
def layer_relational(k, io):
    nc = k.nc
    wide = [P, W, D]
    SLOPE = 0.01
    table = nc.dram_tensor("l2_table", [NP, TYPES * D], F32).ap()
    with ExitStack() as ctx:
        index = k.sb(ctx, "l2_index", [P, T + R * G], I32)
        loc = k.sb(ctx, "l2_loc", [P, T + 2 * G])
        wgt = k.sb(ctx, "l2_weight", [P, T + 2 * G])
        win_i = k.sb(ctx, "l2_win_i", [1, T // G], I32)
        read_list(k, "read_src", k.list_src, RS, index, loc, wgt, k.win_src, win_i)
        z = k.sb(ctx, "l2_z", [P, W, D])
        total = k.sb(ctx, "l2_total", [P, W, D])
        rows = k.sb(ctx, "l2_rows", [P, W, TYPES * D])
        w = k.sb(ctx, "l2_w", [P, TYPES, D])
        bias = k.sb(ctx, "l2_bias", [P, D])
        layernorm(k, "ln2", k.x, z)
        vector_steps(k, "l2_start", lambda v, step: step(v.tensor_copy(total[:, :, :], z[:, :, :])))
        dinv = bc(k.dinv0[:, :].unsqueeze(2), wide)
        for r in range(3):
            vector_steps(k, f"l2_load{r}", None,
                         loads=[(w[:, :, :], io[f"L2_gnn_W{r + 1}"].rearrange("t i o -> i t o")),
                                (bias[:, :], io[f"L2_gnn_b{r + 1}"].partition_broadcast(P))])
            project(k, f"l2_xw{r}", z, w[:, :, :].rearrange("p t o -> p (t o)"), TYPES * D,
                    lambda v, n, ps: v.tensor_scalar(rows[:, bass.ds(n, 1), :].rearrange("p a d -> p (a d)"), ps,
                                                     k.dinv0[:, n:n + 1], None, ALU.mult),
                    store=lambda a, b: (rows_in(table)[:, a:b, :], rows[:, a:b, :]))
            window_sums(k, f"l2_sum{r}", loc, win_i, table=table.rearrange("n (t o) -> (n t) o", t=TYPES),
                        index=index, weight=wgt)

            def update(v, step):
                step(v.tensor_tensor(z[:, :, :], feature_sums(k), dinv, ALU.mult))
                step(v.tensor_tensor(z[:, :, :], z[:, :, :], bc(bias[:, :].unsqueeze(1), wide), ALU.add))
                step(v.scalar_tensor_tensor(z[:, :, :], z[:, :, :], SLOPE, z[:, :, :], ALU.mult, ALU.max))
                step(v.tensor_tensor(total[:, :, :], total[:, :, :], z[:, :, :], ALU.add))
                if r == 2:
                    step(v.scalar_tensor_tensor(k.x[:, :, :], total[:, :, :], 0.25, k.x[:, :, :],
                                                ALU.mult, ALU.add))
            vector_steps(k, f"l2_update{r}", update)


@own_semaphores
def layer_attention(k, io, out):
    nc = k.nc
    t_q = nc.dram_tensor("l3_q", [NP, D], F32).ap()
    with ExitStack() as outer:
        h = k.sb(outer, "l3_h", [P, W, D])
        val = k.sb(outer, "l3_v", [P, W, D])
        wo = k.sb(outer, "l3_wo", [P, D])
        vecs = k.sb(outer, "l3_vecs", [P, 3, D])
        layernorm(k, "ln3", k.x, h)
        with ExitStack() as ctx:
            s = k.sb(ctx, "l3_scores", [P, T, HEADS])
            cns = k.sb(ctx, "l3_cons_slots", [P, T, HEADS])
            s_p, s_c = k.sem("l3_products"), k.sem("l3_cons_copied")

            def consume(v, n, a, b):
                at = bass.ds(n * G, G)
                v.tensor_copy(cns[:, at, :], b[:, :, D:D + HEADS]).then_inc(s_c, 1)
                v.tensor_tensor(a, a, b[:, :, 0:D], ALU.mult).then_inc(s_p, 1)
                v.wait_ge(s_p, n + 1)
                return v.tensor_reduce(s[:, at, :], a.rearrange("p g (h c) -> p g h c", c=C),
                                       AXX, ALU.add)
            with ExitStack() as inner:
                k_parts = k.sb(inner, "l3_k_parts", [P, W, 3, D + HEADS], BF16)
                with ExitStack() as first:
                    wqkv = k.sb(first, "l3_wqkv", [P, 3, D])
                    b = k.sb(first, "l3_bqkv", [P, 3 * D])
                    krow = k.sb(first, "l3_k_rows", [P, W, D + HEADS])
                    qkv = k.sb(first, "l3_qkv", [P, W, 3 * D])
                    vec = lambda name: io[name].partition_broadcast(P)
                    loads = [(wqkv[:, n, :], io[f"L3_gnn_W{c}"]) for n, c in enumerate("qkv")]
                    loads += [(b[:, n * D:(n + 1) * D], vec(f"L3_gnn_b{c}")) for n, c in enumerate("qkv")]
                    loads += [(wo[:, :], io["L3_gnn_Wo"]), (vecs[:, 0, :], vec("L3_gnn_bo")),
                              (vecs[:, 1, :], vec("L3_gnn_gamma")), (vecs[:, 2, :], vec("L3_gnn_beta"))]
                    vector_steps(k, "l3_load", None, loads=loads)
                    project(k, "l3_qkv", h, wqkv[:, :, :].rearrange("p t o -> p (t o)"), 3 * D,
                            lambda v, n, ps: v.tensor_tensor(qkv[:, bass.ds(n, 1), :].rearrange("p a d -> p (a d)"),
                                                             ps, b[:, :], ALU.add))

                    def rows(v, step):
                        step(v.tensor_copy(val[:, :, :], qkv[:, :, 2 * D:3 * D]))
                        step(v.tensor_copy(krow[:, :, 0:D], qkv[:, :, D:2 * D]))
                        step(v.tensor_copy(krow[:, :, D:D + HEADS], k.cons[:, :, :].rearrange("p h w -> p w h")))
                    vector_steps(k, "l3_rows", rows, stores=[(rows_in(t_q), qkv[:, :, 0:D])])
                    split(k, "l3_k", krow, k_parts)
                terms = k.sb(inner, "l3_terms", [P, T, RD])
                s_terms = k.sem("l3_terms_loaded")

                def load_terms(sp):
                    sp.dma_start(terms[:, :, :], k.list_dst.rearrange("(p t) r -> p t r", p=P)).then_inc(s_terms, 16)
                    sp.wait_ge(s_terms, 16)
                edge_rows(k, "l3_edges", t_q, D, k_parts, D + HEADS, consume, beside={"sync": load_terms})

                def score(v, step):
                    step(v.scalar_tensor_tensor(s[:, :, :], s[:, :, :], float(C) ** -0.5, terms[:, :, 2:2 + HEADS],
                                                ALU.mult, ALU.add))
                    step(v.tensor_tensor(s[:, :, :], s[:, :, :], cns[:, :, :], ALU.mult))
                    step(v.tensor_tensor(s[:, :, :], s[:, :, :], terms[:, :, 2 + HEADS:], ALU.add))
                    step(v.tensor_copy(cns[:, :, :], s[:, :, :]))
                vector_steps(k, "l3_score", score)
            segment_max(k, "l3_max", cns[:, :, :])
            s_a, s_b = k.sem("l3_less_top"), k.sem("l3_exp")
            with nc.Block() as block:
                @block.vector
                def _(v):
                    v.tensor_tensor(s[:, :, :], s[:, :, :], cns[:, :, :], ALU.subtract).then_inc(s_a, 1)

                @block.scalar
                def _(act):
                    act.wait_ge(s_a, 1)
                    act.activation(s[:, :, :], s[:, :, :], ACT.Exp).then_inc(s_b, 1)
                    act.wait_ge(s_b, 1)
            window_sums(k, "l3_sum", k.loc, k.win_i, values=s)
            acc_v = value_sums(k, HEADS)
            inv = k.sb(ctx, "l3_inv", [P, W, HEADS])

            def weigh(v, step):
                step(v.tensor_tensor(inv[:, :, :], acc_v, bc(k.no_edge[:, :].unsqueeze(2), [P, W, HEADS]), ALU.add))
                step(v.reciprocal(inv[:, :, :], inv[:, :, :]))
                step(v.tensor_tensor(inv[:, :, :], inv[:, :, :], acc_v, ALU.mult))
                heads = val[:, :, :].rearrange("p w (h c) -> p w h c", c=C)
                step(v.tensor_tensor(heads, heads, bc(inv[:, :, :].unsqueeze(3), [P, W, HEADS, C]), ALU.mult))
            vector_steps(k, "l3_weigh", weigh)
        y = k.sb(outer, "l3_y", [P, W, D])
        project(k, "l3_out", val, wo[:, :], D,
                lambda v, n, ps: v.tensor_tensor(y[:, bass.ds(n, 1), :].rearrange("p a d -> p (a d)"), ps,
                                                 vecs[:, 0, :], ALU.add))
        vector_steps(k, "l3_residual", lambda v, step: step(v.tensor_tensor(y[:, :, :], y[:, :, :], h[:, :, :],
                                                                             ALU.add)))
        layernorm(k, "ln4", y, h, relu=False, gamma=vecs[:, 1, :], beta=vecs[:, 2, :])
        full = N // P
        vector_steps(k, "l3_finish",
                     lambda v, step: step(v.tensor_tensor(k.x[:, :, :], k.x[:, :, :], h[:, :, :], ALU.add)),
                     stores=[(rows_in(out[0:full * P, :]), k.x[:, 0:full, :]),
                             (out[full * P:N, :], k.x[0:N - full * P, full, :])])


def program(nc, io, out):
    with ExitStack() as ctx:
        k = Core(nc)
        k.psum = ctx.enter_context(nc.psum_tensor("psum", [P, 8 * PSUM_BANK], F32))
        k.ps = [k.psum[:, b * PSUM_BANK:(b + 1) * PSUM_BANK] for b in range(8)]
        k.x = k.sb(ctx, "x_sb", [P, W, D])
        k.iota = k.sb(ctx, "iota", [P, P])
        k.pid = k.sb(ctx, "pid", [P, 1])
        k.ones = k.sb(ctx, "ones", [P, P])
        k.eps = k.sb(ctx, "eps", [P, 1])
        k.ident = k.sb(ctx, "ident", [P, P])
        k.ident16 = k.sb(ctx, "ident_bf16", [P, P], BF16)
        k.before = k.sb(ctx, "before", [P, P])
        k.win_dst = k.sb(ctx, "win_dst", [P, T])
        k.win_src = k.sb(ctx, "win_src", [P, T])
        k.src_i = k.sb(ctx, "src_i", [P, T + R * G], I32)
        k.dst_f = k.sb(ctx, "dst_f", [P, T])
        k.tile_no = k.dst_f
        k.loc = k.sb(ctx, "loc", [P, T + 2 * G])
        k.win_i = k.sb(ctx, "win_dst_i", [1, T // G], I32)
        k.deg, k.dinv, k.dinv0, k.inv_deg, k.no_edge = (
            k.sb(ctx, name, [P, W]) for name in ("deg", "dinv", "dinv0", "inv_deg", "no_edge"))
        k.list_a = nc.dram_tensor("half_sorted", [E, RD], F32).ap()
        k.list_dst = nc.dram_tensor("by_dst", [SLOTS, RD], F32).ap()
        k.list_src = nc.dram_tensor("by_src", [SLOTS, RS], F32).ap()
        k.counts = nc.dram_tensor("counts", [W, P, NP], F32).ap()
        k.cons = k.sb(ctx, "conservation", [P, HEADS, W])
        k.bounds_src = k.sb(ctx, "bounds_src", [1, W + 1], I32)
        setup(k, io)
        sort_both(k, io)
        read_list(k, "read_dst", k.list_dst, RD, k.src_i, k.loc, None, k.win_dst, k.win_i)
        vector_steps(k, "dst_of_slots", lambda v, step: step(v.scalar_tensor_tensor(
            k.dst_f[:, :], k.win_dst[:, :], float(P), k.loc[:, 0:T], ALU.mult, ALU.add)))
        layer_filter(k, io)
        layer_gat(k, io)
        layer_relational(k, io)
        layer_attention(k, io, out)


_INS = ['x', 'src', 'dst', 'edge_attr_64', 'edge_type_4', 'edge_weight', 'edge_weight1', 'node_vec1',
        'L1_gnn_W', 'L1_gnn_att_src', 'L1_gnn_att_dst', 'L1_gnn_bias',
        'L2_gnn_W1', 'L2_gnn_b1', 'L2_gnn_W2', 'L2_gnn_b2', 'L2_gnn_W3', 'L2_gnn_b3',
        'L3_gnn_Wq', 'L3_gnn_bq', 'L3_gnn_Wk', 'L3_gnn_bk', 'L3_gnn_Wv', 'L3_gnn_bv', 'L3_gnn_We', 'L3_gnn_be',
        'L3_gnn_Wc1', 'L3_gnn_bc1', 'L3_gnn_Wc2', 'L3_gnn_bc2', 'L3_gnn_Wd1', 'L3_gnn_bd1', 'L3_gnn_Wd2',
        'L3_gnn_bd2', 'L3_gnn_Wo', 'L3_gnn_bo', 'L3_gnn_gamma', 'L3_gnn_beta']


def kernel(**inputs):
    import numpy as _np
    import concourse.bacc as _bacc
    from concourse import mybir as _mybir
    from concourse.bass_utils import run_bass_kernel_spmd as _run

    nc = _bacc.Bacc("TRN2", target_bir_lowering=False, num_devices=1)
    arrays, io = {}, {}
    for name in _INS:
        a = _np.ascontiguousarray(inputs[name])
        arrays[f"in_{name}"] = a
        io[name] = nc.dram_tensor(f"in_{name}", a.shape, _mybir.dt.from_np(a.dtype), kind="ExternalInput").ap()
    out = nc.dram_tensor("out_x", (N, D), F32, kind="ExternalOutput").ap()
    program(nc, io, out)
    r = _run(nc, [arrays], core_ids=[0])
    return r.results[0]["out_x"]
```
